# Optimizing a Trainium2 kernel written in Bass

```python
import numpy as np
import jax
import jax.numpy as jnp

def _softmax(x, axis=-1):
    return jax.nn.softmax(x, axis=axis)

def _gelu(x):
    return jax.nn.gelu(x, approximate=True)

def _silu(x):
    return jax.nn.silu(x)

def _sigmoid(x):
    return jax.nn.sigmoid(x)

def _layernorm(x, axis=-1, eps=1e-05):
    m = jnp.mean(x, axis=axis, keepdims=True)
    v = jnp.var(x, axis=axis, keepdims=True)
    return (x - m) / jnp.sqrt(v + eps)

def _scatter_add(tgt, idx, src, axis=0):
    return tgt.at[idx].add(src)

def _segment_sum(src, seg, n):
    return jax.ops.segment_sum(src, seg, n)
kernel_name = 'mk_gnn_resnorm_d4_gnn_r64_733c21'

def setup_inputs(seed: int=0):
    np.random.seed(seed)
    _w = jnp.asarray

    def _rec_inputs():
        import jax
        import jax.numpy as jnp
        _gk = jax.random.key(seed)
        x = -0.000202 + 1 * jax.random.normal(jax.random.fold_in(_gk, 1), (100000, 128), jnp.float32)
        src = jax.random.randint(jax.random.fold_in(_gk, 2), (25000,), 0, 100000, jnp.int32)
        dst = jax.random.randint(jax.random.fold_in(_gk, 3), (25000,), 0, 100000, jnp.int32)
        _o = jnp.argsort(dst, stable=True)
        src = src[_o]
        dst = dst[_o]
        edge_attr_96 = 5.93493e-05 + 1.00006 * jax.random.normal(jax.random.fold_in(_gk, 13), (25000, 96), jnp.float32)
        edge_type_32 = jax.random.randint(jax.random.fold_in(_gk, 15), (25000,), 0, 32, jnp.int32)
        edge_weight = jax.random.uniform(jax.random.fold_in(_gk, 16), (25000,), jnp.float32, 0.0, 0.999998)
        edge_weight1 = jax.random.uniform(jax.random.fold_in(_gk, 17), (25000, 1), jnp.float32, 0.0, 0.999998)
        return (x, src, dst, edge_attr_96, edge_type_32, edge_weight, edge_weight1)
    x, src, dst, edge_attr_96, edge_type_32, edge_weight, edge_weight1 = _rec_inputs()

    def _L0_gnn_setup():
        import jax, jax.numpy as jnp
        import numpy as np
        N_NODES = 50000
        N_EDGES = 500000
        IN_FEAT = 128
        OUT_FEAT = 128
        NUM_RELS = 32
        NUM_BASES = 8
        key = jax.random.key(seed)
        ks = jax.random.split(key, 8)
        h = jax.random.normal(ks[0], (N_NODES, IN_FEAT), dtype=jnp.float32)
        src = jax.random.randint(ks[1], (N_EDGES,), 0, N_NODES, dtype=jnp.int32)
        dst = jax.random.randint(ks[2], (N_EDGES,), 0, N_NODES, dtype=jnp.int32)
        etype = jax.random.randint(ks[3], (N_EDGES,), 0, NUM_RELS, dtype=jnp.int32)
        norm = jax.random.uniform(ks[4], (N_EDGES, 1), dtype=jnp.float32)
        weight = jax.random.normal(ks[5], (NUM_BASES, IN_FEAT, OUT_FEAT), dtype=jnp.float32) * 0.05
        w_comp = jax.random.normal(ks[6], (NUM_RELS, NUM_BASES), dtype=jnp.float32) * 0.3
        bias_param = jax.random.normal(ks[7], (OUT_FEAT,), dtype=jnp.float32) * 0.05
        return {'h': h, 'src': src, 'dst': dst, 'etype': etype, 'norm': norm, 'weight': weight, 'w_comp': w_comp, 'bias_param': bias_param}
    _L0_gnn_all = _L0_gnn_setup()
    _L0_gnn_in = {k: v for k, v in _L0_gnn_all.items() if k in ('weight', 'w_comp', 'bias_param')}
    del _L0_gnn_all

    def _L1_gnn_setup():
        import jax, jax.numpy as jnp
        import numpy as np
        N_NODES = 100000
        N_EDGES = 10000
        DIM = 128
        key = jax.random.key(seed)
        k1, k2, k3, k4, k5 = jax.random.split(key, 5)
        x = jax.random.normal(k1, (N_NODES, DIM), dtype=jnp.float32)
        edge_index = jax.random.randint(k2, (2, N_EDGES), 0, N_NODES, dtype=jnp.int64)
        edge_weight = jax.random.uniform(k3, (N_EDGES,), dtype=jnp.float32)
        W = jax.random.normal(k4, (DIM, DIM), dtype=jnp.float32) * (1.0 / np.sqrt(DIM))
        b = jax.random.normal(k5, (DIM,), dtype=jnp.float32) * 0.01
        return {'x': x, 'edge_index': edge_index, 'edge_weight': edge_weight, 'W': W, 'b': b}
    _L1_gnn_all = _L1_gnn_setup()
    _L1_gnn_in = {k: v for k, v in _L1_gnn_all.items() if k in ('W', 'b')}
    del _L1_gnn_all

    def _L2_gnn_setup():
        import jax, jax.numpy as jnp
        import numpy as np
        N_NODES = 50000
        N_EDGES = 12500
        NODE_DIM = 128
        EDGE_DIM = 96
        HIDDEN = 256
        N_GRAPHS = 16
        U_DIM = 64

        def scatter_mean(vals, idx, num_segments):
            s = jax.ops.segment_sum(vals, idx, num_segments=num_segments)
            cnt = jax.ops.segment_sum(jnp.ones((vals.shape[0],), vals.dtype), idx, num_segments=num_segments)
            return s / jnp.maximum(cnt, 1.0)[:, None]
        key = jax.random.key(seed)
        ks = jax.random.split(key, 16)
        glorot = lambda k, shp: jax.random.normal(k, shp, dtype=jnp.float32) * (2.0 / (shp[0] + shp[1])) ** 0.5
        return {'x': jax.random.normal(ks[0], (N_NODES, NODE_DIM), dtype=jnp.float32), 'edge_index': jax.random.randint(ks[1], (2, N_EDGES), 0, N_NODES, dtype=jnp.int64), 'edge_attr': jax.random.normal(ks[2], (N_EDGES, EDGE_DIM), dtype=jnp.float32), 'u': jax.random.normal(ks[3], (N_GRAPHS, U_DIM), dtype=jnp.float32), 'batch': jax.random.randint(ks[4], (N_NODES,), 0, N_GRAPHS, dtype=jnp.int64), 'W1': glorot(ks[5], (NODE_DIM + EDGE_DIM, HIDDEN)), 'b1': jnp.zeros((HIDDEN,), jnp.float32), 'W2': glorot(ks[6], (HIDDEN, HIDDEN)), 'b2': jnp.zeros((HIDDEN,), jnp.float32), 'Wa': glorot(ks[7], (HIDDEN, 1)), 'ba': jnp.zeros((1,), jnp.float32), 'W3': glorot(ks[8], (NODE_DIM + HIDDEN, HIDDEN)), 'b3': jnp.zeros((HIDDEN,), jnp.float32), 'W4': glorot(ks[9], (HIDDEN, NODE_DIM)), 'b4': jnp.zeros((NODE_DIM,), jnp.float32)}
    _L2_gnn_all = _L2_gnn_setup()
    _L2_gnn_in = {k: v for k, v in _L2_gnn_all.items() if k in ('u', 'W1', 'b1', 'W2', 'b2', 'Wa', 'ba', 'W3', 'b3', 'W4', 'b4')}
    del _L2_gnn_all

    def _L3_gnn_setup():
        import jax, jax.numpy as jnp
        import numpy as np
        N_NODES = 50000
        N_EDGES = 9375
        IN_DIM = 128
        HID_DIM = 128
        key = jax.random.key(seed)
        k_h, k_src, k_dst, k_w1, k_b1, k_w2, k_b2 = jax.random.split(key, 7)
        h = jax.random.normal(k_h, (N_NODES, IN_DIM), dtype=jnp.float32)
        src = jax.random.randint(k_src, (N_EDGES,), 0, N_NODES, dtype=jnp.int32)
        dst = jax.random.randint(k_dst, (N_EDGES,), 0, N_NODES, dtype=jnp.int32)
        s1 = 1.0 / np.sqrt(IN_DIM)
        s2 = 1.0 / np.sqrt(HID_DIM)
        W1 = jax.random.uniform(k_w1, (IN_DIM, HID_DIM), jnp.float32, -s1, s1)
        b1 = jax.random.uniform(k_b1, (HID_DIM,), jnp.float32, -s1, s1)
        W2 = jax.random.uniform(k_w2, (HID_DIM, 1), jnp.float32, -s2, s2)
        b2 = jax.random.uniform(k_b2, (1,), jnp.float32, -s2, s2)
        return {'h': h, 'src': src, 'dst': dst, 'W1': W1, 'b1': b1, 'W2': W2, 'b2': b2}
    _L3_gnn_all = _L3_gnn_setup()
    _L3_gnn_in = {k: v for k, v in _L3_gnn_all.items() if k in ('W1', 'b1', 'W2', 'b2')}
    del _L3_gnn_all
    return {'x': x, 'src': src, 'dst': dst, 'edge_attr_96': edge_attr_96, 'edge_type_32': edge_type_32, 'edge_weight': edge_weight, 'edge_weight1': edge_weight1, 'L0_gnn_weight': _L0_gnn_in['weight'], 'L0_gnn_w_comp': _L0_gnn_in['w_comp'], 'L0_gnn_bias_param': _L0_gnn_in['bias_param'], 'L1_gnn_W': _L1_gnn_in['W'], 'L1_gnn_b': _L1_gnn_in['b'], 'L2_gnn_u': _L2_gnn_in['u'], 'L2_gnn_W1': _L2_gnn_in['W1'], 'L2_gnn_b1': _L2_gnn_in['b1'], 'L2_gnn_W2': _L2_gnn_in['W2'], 'L2_gnn_b2': _L2_gnn_in['b2'], 'L2_gnn_Wa': _L2_gnn_in['Wa'], 'L2_gnn_ba': _L2_gnn_in['ba'], 'L2_gnn_W3': _L2_gnn_in['W3'], 'L2_gnn_b3': _L2_gnn_in['b3'], 'L2_gnn_W4': _L2_gnn_in['W4'], 'L2_gnn_b4': _L2_gnn_in['b4'], 'L3_gnn_W1': _L3_gnn_in['W1'], 'L3_gnn_b1': _L3_gnn_in['b1'], 'L3_gnn_W2': _L3_gnn_in['W2'], 'L3_gnn_b2': _L3_gnn_in['b2']}

def reference(x, src, dst, edge_attr_96, edge_type_32, edge_weight, edge_weight1, L0_gnn_weight, L0_gnn_w_comp, L0_gnn_bias_param, L1_gnn_W, L1_gnn_b, L2_gnn_u, L2_gnn_W1, L2_gnn_b1, L2_gnn_W2, L2_gnn_b2, L2_gnn_Wa, L2_gnn_ba, L2_gnn_W3, L2_gnn_b3, L2_gnn_W4, L2_gnn_b4, L3_gnn_W1, L3_gnn_b1, L3_gnn_W2, L3_gnn_b2):
    import jax
    import jax.numpy as jnp

    def _L0_gnn_ref(h, src, dst, etype, norm, weight, w_comp, bias_param):
        import jax, jax.numpy as jnp
        import numpy as np
        N_NODES = 50000
        N_EDGES = 500000
        IN_FEAT = 128
        OUT_FEAT = 128
        NUM_RELS = 32
        NUM_BASES = 8
        hsrc = h[src]
        coef = w_comp[etype]
        msg = jnp.zeros((hsrc.shape[0], weight.shape[2]), dtype=h.dtype)
        for b in range(weight.shape[0]):
            msg = msg + hsrc @ weight[b] * coef[:, b][:, None]
        msg = msg * norm
        node_repr = jax.ops.segment_sum(msg, dst, num_segments=h.shape[0])
        node_repr = node_repr + bias_param
        return jax.nn.relu(node_repr)

    def _L1_gnn_ref(x, edge_index, edge_weight, W, b):
        import jax, jax.numpy as jnp
        import numpy as np
        N_NODES = 100000
        N_EDGES = 10000
        DIM = 128
        row, col = (edge_index[0], edge_index[1])
        msgs = edge_weight[:, None] * x[row]
        agg = jax.ops.segment_sum(msgs, col, num_segments=x.shape[0])
        return agg @ W.T + b

    def _L2_gnn_ref(x, edge_index, edge_attr, u, batch, W1, b1, W2, b2, Wa, ba, W3, b3, W4, b4):
        import jax, jax.numpy as jnp
        import numpy as np
        N_NODES = 50000
        N_EDGES = 12500
        NODE_DIM = 128
        EDGE_DIM = 96
        HIDDEN = 256
        N_GRAPHS = 16
        U_DIM = 64

        def scatter_mean(vals, idx, num_segments):
            s = jax.ops.segment_sum(vals, idx, num_segments=num_segments)
            cnt = jax.ops.segment_sum(jnp.ones((vals.shape[0],), vals.dtype), idx, num_segments=num_segments)
            return s / jnp.maximum(cnt, 1.0)[:, None]
        row = edge_index[0]
        agg = scatter_mean(edge_attr, row, x.shape[0])
        h = jnp.concatenate([x, agg], axis=1)
        h = jax.nn.relu(h @ W1 + b1) @ W2 + b2
        attn = jax.nn.sigmoid(h @ Wa + ba)
        h = h * attn
        h = jnp.concatenate([x, h], axis=1)
        return jax.nn.relu(h @ W3 + b3) @ W4 + b4

    def _L3_gnn_ref(h, src, dst, W1, b1, W2, b2):
        import jax, jax.numpy as jnp
        import numpy as np
        N_NODES = 50000
        N_EDGES = 9375
        IN_DIM = 128
        HID_DIM = 128
        n_nodes = h.shape[0]
        dif = h[src] - h[dst]
        hidden = jax.nn.relu(dif @ W1 + b1)
        att = jax.nn.relu(hidden @ W2 + b2)[:, 0]
        att = jax.nn.sigmoid(att)
        denom = jax.ops.segment_sum(att, src, num_segments=n_nodes)
        w = att / denom[src]
        msg = w[:, None] * h[src]
        out = jax.ops.segment_sum(msg, dst, num_segments=n_nodes)
        return out
    edge_index = jnp.stack([src, dst])
    batch0 = jnp.zeros((100000,), jnp.int32)
    x = _layernorm(x + _L0_gnn_ref(x, src, dst, edge_type_32, edge_weight1, L0_gnn_weight, L0_gnn_w_comp, L0_gnn_bias_param), axis=-1)
    x = _layernorm(x + _L1_gnn_ref(x, edge_index, edge_weight, L1_gnn_W, L1_gnn_b), axis=-1)
    x = _layernorm(x + _L2_gnn_ref(x, edge_index, edge_attr_96, L2_gnn_u, batch0, L2_gnn_W1, L2_gnn_b1, L2_gnn_W2, L2_gnn_b2, L2_gnn_Wa, L2_gnn_ba, L2_gnn_W3, L2_gnn_b3, L2_gnn_W4, L2_gnn_b4), axis=-1)
    x = _layernorm(x + _L3_gnn_ref(x, src, dst, L3_gnn_W1, L3_gnn_b1, L3_gnn_W2, L3_gnn_b2), axis=-1)
    return x

_drawn_inputs = setup_inputs


def setup_inputs(seed=0):
    import zlib

    import numpy as np

    out = dict(_drawn_inputs(seed))
    spreads = {'L2_gnn_b1': (0.0, 0.425),
     'L2_gnn_b2': (0.0, 0.326),
     'L2_gnn_b3': (0.0, 0.1),
     'L2_gnn_b4': (0.0, 0.1)}
    factors = {'L1_gnn_b': 5.181, 'L3_gnn_W1': 8.0, 'L3_gnn_b1': 8.0, 'L3_gnn_W2': 8.0}
    for name, (base, spread) in spreads.items():
        noise = np.random.default_rng([zlib.crc32(name.encode()), seed]).standard_normal(out[name].shape)
        drawn = base * np.exp(spread * noise) if base else spread * noise
        out[name] = jnp.asarray(drawn.astype(out[name].dtype))
    for name, factor in factors.items():
        out[name] = (out[name] * factor).astype(out[name].dtype)
    return out
```

```python
from contextlib import ExitStack

import concourse.bass as bass
from concourse import mybir

F32 = mybir.dt.float32
I32 = mybir.dt.int32
ALU = mybir.AluOpType
ACT = mybir.ActivationFunctionType
AX = mybir.AxisListType

P = 128
D = 128
N = 100000
E = 25000
A = 96
AW = A + 1
H = 256
R = 32
NB = 8
EP = 125
C = E // EP
J = 4
G = C // J
DUMMY = J * P
NR = N + DUMMY
T = 512
NT = -(-N // T)
EPS = 1e-5
SRC, DST, ETYPE, NORM, EW, FIELDS = 0, 1, 2, 3, 4, 5
MAGIC = 1597463007.0


class Signal:

    def __init__(self, sems, base, turns):
        self.sems, self.base, self.turns = sems, base, turns

    def __getitem__(self, s):
        return self.sems[s]

    def all(self, eng, each=1):
        for sem in self.sems:
            eng.wait_ge(sem, (self.base + self.turns) * each)


class Turn:

    def __init__(self, i, s, start=None):
        self.i, self.s = i, s
        self.t = i * 2 + s
        self.start = start

    def now(self, eng, sig, each=1):
        eng.wait_ge(sig[self.s], self.i * each + (sig.base + 1) * each)

    def again(self, eng, sig, each=1):
        eng.wait_ge(sig[self.s], self.i * each + sig.base * each)

    def before(self, eng, sig, each=1):
        eng.wait_ge(sig[1 - self.s], self.i * each + (sig.base + self.s) * each)


class Steps:

    def __init__(self, eng, sem, turn, each):
        self.eng, self.sem, self.each, self.n = eng, sem, each, 0
        self.base = turn.t * each if turn is not None else 0

    def done(self, ins):
        self.n += 1
        assert self.each is None or self.n <= self.each
        ins.then_inc(self.sem, 1)
        return self.n

    def wait(self):
        self.eng.wait_ge(self.sem, self.base + self.n)

    def step(self, ins):
        self.done(ins)
        self.wait()

    def close(self):
        assert self.n == self.each, self.n


def gnn_kernel(nc, x, src, dst, edge_attr, edge_type, edge_weight, edge_weight1, l0_w, l0_comp, l0_b,
               l1_w, l1_b, w1, b1, w2, b2, wa, ba, w3, b3, w4, b4, v1, c1, v2, c2, out):
    ctx = ExitStack()
    with ctx:
        def sb(name, shape, dt=F32):
            return ctx.enter_context(nc.sbuf_tensor(name, shape, dt))

        def ps(name, shape):
            return ctx.enter_context(nc.psum_tensor(name, shape, F32))

        def sem(name):
            return ctx.enter_context(nc.semaphore(name))

        def sem2(name):
            return [sem(name + "_0"), sem(name + "_1")]

        def table(name, shape):
            return nc.dram_tensor(name, shape, F32, kind="Internal").ap()

        agg0 = table("agg0", [NR, D])
        agg1 = table("agg1", [NR, D])
        attr = table("attr", [NR, AW])
        den = table("den", [NR, 1])
        x3 = table("x3", [NR, D])
        xsrc = table("xsrc", [G, P, J * D])
        hsrc = table("hsrc", [G, P, J * D])

        ident = sb("ident", [P, P])
        lower = sb("lower", [P, P])
        ones = sb("ones", [P, 1])
        part = sb("part", [P, 1])
        part_i = sb("part_i", [P, 1], I32)
        dummy = sb("dummy_row", [P, J, 2])
        dummy_i = sb("dummy_row_i", [P, J, 2], I32)
        zeros = sb("zeros", [P, 16 * D])
        row0 = sb("row0", [P, 16, D])
        row1 = sb("row1", [P, 16, D])
        wcat = sb("wcat", [P, NB, D])
        comp = sb("comp", [R, NB])
        l1w = sb("l1w", [P, D])
        l1wT = sb("l1wT", [P, D])
        w1x = sb("w1x", [P, H])
        w1a = sb("w1a", [A, H])
        w2n = sb("w2n", [P, 2, H])
        w2T = sb("w2T", [P, 2, H])
        w3x = sb("w3x", [P, H])
        w3h = sb("w3h", [P, 2, H])
        w23 = sb("w23", [P, 2, H])
        w4s = sb("w4s", [P, 2, D])
        wac = sb("wac", [P, 2])
        wab = sb("wab", [P, 2, P])
        w2a = sb("w2a", [P, 2, P])
        b1c = sb("b1c", [P, 2])
        b2c = sb("b2c", [P, 2])
        b2b = sb("b2b", [P, 2, P])
        b3c = sb("b3c", [P, 2])
        c23 = sb("c23", [P, 2])
        bab = sb("bab", [P, 1])
        zb = sb("zb", [P, 1])
        b4b = sb("b4b", [P, J, D])
        v1s = sb("v1s", [P, D])
        c1c = sb("c1c", [P, 1])
        v2s = sb("v2s", [P, 1])
        c2c = sb("c2c", [P, 1])

        src_x = sb("src_x", [P, C], I32)
        dst_x = sb("dst_x", [P, C], I32)
        src_s = sb("src_s", [P, C], I32)
        dst_s = sb("dst_s", [P, C], I32)
        et_i = sb("et_i", [P, C], I32)
        nrm = sb("nrm", [P, C])
        ew_s = sb("ew_s", [P, C])
        meta = sb("meta", [P, C, FIELDS])
        uniq = sb("uniq", [P, C, 2], I32)
        att_all = sb("att_all", [P, C])

        fa = sb("fa", [P, 2, J, D])
        fb = sb("fb", [P, 2, J, D])
        fc = sb("fc", [P, 2, J, D])
        fd = sb("fd", [P, 2, J, D])
        fe = sb("fe", [P, 2, J, D])
        ff = sb("ff", [P, 2, J, D])
        x2s = sb("x2s", [P, 2, J, D])
        big0 = sb("big0", [P, 2, J, T])
        big1 = sb("big1", [P, J, T])
        sl = sb("sl", [P, 2, J, P])
        at = sb("at", [P, 2, J, AW])
        ag = sb("ag", [P, 2, J, AW])
        m = sb("m", [P, 2, J, FIELDS])
        gi = sb("gi", [P, 2, J], I32)
        gi2 = sb("gi2", [P, 2, J], I32)
        ui = sb("ui", [P, 2, J, 2], I32)
        ot = sb("ot", [R, T])
        cf = sb("cf", [P, J, NB])
        prod = sb("prod", [P, 2, NB, D])
        dd = sb("dd", [P, J, 2])
        nf = sb("nf", [P, J, 2])
        st = sb("st", [P, J, 6])
        mv = sb("mv", [P, J, 2])
        h_sum = sb("h_sum", [P, J])
        h_dif = sb("h_dif", [P, J])
        h_sq = sb("h_sq", [P, J])
        nv = sb("nv", [P, 2 * J])
        ny = sb("ny", [P, 2 * J])
        na = sb("na", [P, 2 * J])
        nb_ = sb("nb_", [P, 2 * J])
        rc = sb("rc", [P, J])
        sm = sb("sm", [P, 2, J])
        sm2 = sb("sm2", [P, 2, J])
        rc2 = sb("rc2", [P, 2, J])
        x2T = sb("x2T", [P, 2, T])
        agT = sb("agT", [A, 2, T])
        rr = big0
        att_b = sb("att_b", [P, 2, T])
        h3 = big1

        yA = ps("yA", [P, 2 * T])
        yB = ps("yB", [P, 2 * T])
        bk = [ps(f"bk{n}", [P, T]) for n in range(4)]
        yAB = [yA, yB]

        def cols(bank, j):
            return bank[:, j * P:(j + 1) * P]

        s_zero = sem("zeros_set")
        s_const = sem("constants_set")
        s_pad = sem("padding_set")
        s_w = sem("weights_loaded")
        s_e = sem("edges_loaded")
        s_dup = sem("weight_copies_made")
        s_meta = sem("meta_made")
        s_at = sem("attr_slots_set")
        s_wt = sem("weights_transposed")
        s_wte = sem("weights_transposed_kept")
        s_wp = sem("weight_products")
        s_wpk = sem("weight_products_kept")
        s_row = sem("bias_rows_loaded")
        s_fill0 = sem("agg0_filled")
        s_fill1 = sem("agg1_filled")
        s_filla = sem("attr_filled")
        s_filld = sem("den_filled")
        s_gate = sem("pool_gate_passed")
        s_pset = sem("pool_set_up")

        block = ctx.enter_context(nc.Block())

        def edge_rows(a, g):
            return a.rearrange("(p c) f -> p c f", p=EP)[:, bass.ds(g * J, J), :]

        def node_rows(a, start, rows=T):
            return a[bass.ds(start, rows), :].rearrange("(p j) f -> p (j f)", p=P)

        def gate(pool):
            pool.sem_inc(s_gate, 1)

        pairs, counted = {}, {}

        def phase(name, turns, own, shared):
            found = {}
            for key, role in [(k, name + "_" + k) for k in own.split()] + list(shared.items()):
                if role not in pairs:
                    pairs[role], counted[role] = sem2(role), 0
                found[key] = Signal(pairs[role], counted[role], turns)
                counted[role] += turns
            return found

        def same(keys):
            return {k: k for k in keys.split()}

        q1 = phase("e1", G // 2, "types_bc type_hot coef_ps low y y_read msg attr_sum attr_kept earlier rows"
                   " attr_in attr_added",
                   {**same("meta dst_bc dst_eq src_bc src_eq sum sum_kept gidx uidx added"),
                    "x_in": "gathered", "x_out": "rows_saved", "xT_ps": "turned_ps", "xT": "turned"})
        q2 = phase("e2", G // 2, "y z_ps z v",
                   {**same("meta dst_bc dst_eq sum sum_kept gidx uidx added"),
                    "agg_in": "gathered", "x_in": "rows_loaded", "yT_ps": "turned_ps", "yT": "turned"})
        qn = phase("n", NT // 2, "in x2 attr_mean agT_ps agT h1_ps h1 z_ps attn scaled h3_ps h3_pre h3 y_ps x2b"
                   " t0 t3 x3 x4 x3_out x4_out", {"x2T_ps": "turned_ps", "x2T": "turned"})
        q3 = phase("e3", G // 2, "dif hid_ps hid att_ps att_relu att att_saved hd_in",
                   {**same("meta src_bc src_eq sum sum_kept gidx gidx2 uidx added"),
                    "hs_in": "gathered", "h_out": "rows_saved", "dT_ps": "turned_ps", "dT": "turned"})
        q4 = phase("e4", G // 2, "msg",
                   {**same("meta dst_bc dst_eq sum sum_kept gidx uidx added"),
                    "den_in": "gathered", "h_in": "rows_loaded"})
        q5 = phase("e5", G // 2, "y out", {**same("gidx gidx2"), "x_in": "gathered"})
        c1s, c2s, c3s, c4s, c5s = (sem(f"vector_steps_e{n}") for n in (1, 2, 3, 4, 5))
        cna, cnb = sem("vector_steps_n_front"), sem("vector_steps_n_back")
        x3_pad = sem("x3_dummies_set")

        WEIGHTS = 20

        @block.sync
        def _(sp):
            def bcast_rows(vec, n):
                return vec.rearrange("(o f) -> o f", o=1).to_broadcast([n, vec.shape[0]])

            sp.wait_ge(s_pad, 5)
            for tile, a in ((src_x, src), (src_s, src), (dst_x, dst), (dst_s, dst), (et_i, edge_type),
                            (ew_s, edge_weight)):
                sp.dma_start(tile[0:EP, :], a.rearrange("(p c) -> p c", p=EP)).then_inc(s_e, 16)
            sp.dma_start(nrm[0:EP, :], edge_weight1.rearrange("(p c) o -> p (c o)", p=EP)).then_inc(s_e, 16)
            for k in range(16):
                sp.dma_start(row0[:, k, :], bcast_rows(l0_b, P)).then_inc(s_row, 16)
            n = 0
            for o, i in ((wcat[:, :, :], l0_w.rearrange("b i o -> i b o")), (comp[:, :], l0_comp),
                         (l1w[:, :], l1_w), (w1x[:, :], w1[0:D, :]), (w1a[:, :], w1[D:D + A, :]),
                         (w2n[:, :, :], w2.rearrange("(k p) n -> p k n", p=P)),
                         (w3x[:, :], w3[0:D, :]),
                         (w3h[:, :, :], w3[D:D + H, :].rearrange("(k p) n -> p k n", p=P)),
                         (w4s[:, :, :], w4.rearrange("(k p) n -> p k n", p=P)),
                         (wac[:, :], wa.rearrange("(k p) o -> p (k o)", p=P)),
                         (b1c[:, :], b1.rearrange("(k p) -> p k", p=P)),
                         (b2c[:, :], b2.rearrange("(k p) -> p k", p=P)),
                         (b3c[:, :], b3.rearrange("(k p) -> p k", p=P)),
                         (bab[:, :], bcast_rows(ba, P)), (v1s[:, :], v1),
                         (c1c[:, :], c1.rearrange("(p o) -> p o", o=1)), (v2s[:, :], v2),
                         (c2c[:, :], bcast_rows(c2, P)), (b4b[:, 0, :], bcast_rows(b4, P)),
                         (row1[:, 0, :], bcast_rows(l1_b, P))):
                sp.dma_start(o, i, allow_slow_non_contiguous=True).then_inc(s_w, 16)
                n += 1
            assert n == WEIGHTS

            def fill(tab, tile, w, done):
                turns = NR // (16 * P)
                rest = (NR - turns * 16 * P) // 32
                view = tab[0:turns * 16 * P, :].rearrange("(t p j) f -> t p (j f)", p=P, j=16)
                with sp.Fori(0, turns) as t:
                    sp.dma_start(view[bass.ds(t, 1), :, :].rearrange("o p f -> (o p) f"), tile[:, 0:16 * w]).then_inc(done, 16)
                sp.dma_start(tab[turns * 16 * P:NR, :].rearrange("(p j) f -> p (j f)", p=32),
                             tile[0:32, 0:rest * w]).then_inc(done, 16)

            sp.wait_ge(s_row, 16 * 16)
            fill(agg0, row0[:, :, :].rearrange("p j f -> p (j f)"), D, s_fill0)
            sp.wait_ge(s_zero, 1)
            fill(attr, zeros, AW, s_filla)
            sp.dma_start(x3[N:NR, :].rearrange("(p j) f -> p (j f)", p=P), zeros[:, 0:J * D]).then_inc(x3_pad, 16)
            sp.dma_start(den.rearrange("(p j) o -> p (j o)", p=96), zeros[0:96, 0:NR // 96]).then_inc(s_filld, 16)
            sp.wait_ge(s_at, 2)
            with sp.Fori(0, G // 2) as i:
                for s in range(2):
                    tr = Turn(i, s)
                    tr.again(sp, q1["attr_sum"])
                    sp.dma_start(at[0:EP, s, :, 0:A], edge_rows(edge_attr, tr.t)).then_inc(q1["attr_in"][s], 16)
                for s in range(2):
                    tr = Turn(i, s)
                    tr.now(sp, q1["x_in"], 64)
                    sp.dma_start(xsrc[bass.ds(tr.t, 1), :, :].rearrange("o p f -> (o p) f"), fa[:, s, :, :].rearrange("p j f -> p (j f)")).then_inc(q1["x_out"][s], 16)
            sp.wait_ge(s_dup, 1)
            fill(agg1, row1[:, :, :].rearrange("p j f -> p (j f)"), D, s_fill1)
            q1["x_out"].all(sp, 16)
            with sp.Fori(0, G // 2) as i:
                for s in range(2):
                    tr = Turn(i, s)
                    tr.again(sp, q2["v"])
                    sp.dma_start(fa[:, s, :, :].rearrange("p j f -> p (j f)"), xsrc[bass.ds(tr.t, 1), :, :].rearrange("o p f -> (o p) f")).then_inc(q2["x_in"][s], 16)

            q1["added"].all(sp, 64)
            q1["attr_added"].all(sp, 64)
            q2["added"].all(sp, 64)
            q2["sum_kept"].all(sp)
            q1["attr_sum"].all(sp)

            def load(tr):
                tr.again(sp, qn["x2"])
                tr.again(sp, qn["attr_mean"])
                for tile, tab in ((fa, x), (fb, agg0), (fc, agg1), (at, attr)):
                    sp.dma_start(tile[:, tr.s, :, :].rearrange("p j f -> p (j f)"),
                                 node_rows(tab, tr.start)).then_inc(qn["in"][tr.s], 16)

            def store(tr, last=False):
                if last:
                    tr.before(sp, qn["x3_out"], 16)
                    tr.before(sp, qn["x4_out"], 16)
                tr.now(sp, qn["x3"])
                sp.dma_start(node_rows(x3, tr.start), fe[:, tr.s, :, :].rearrange("p j f -> p (j f)")).then_inc(qn["x3_out"][tr.s], 16)
                tr.now(sp, qn["x4"])
                sp.dma_start(node_rows(out, tr.start), ff[:, tr.s, :, :].rearrange("p j f -> p (j f)")).then_inc(qn["x4_out"][tr.s], 16)

            load(Turn(0, 0, 0))
            load(Turn(0, 1, T))
            with sp.Fori(0, NT // 2 - 2) as i:
                for s in range(2):
                    load(Turn(i + 1, s, i * (2 * T) + (2 + s) * T))
                    store(Turn(i, s, i * (2 * T) + s * T))
            k = NT // 2 - 2
            load(Turn(k + 1, 0, (NT - 2) * T))
            store(Turn(k, 0, (NT - 4) * T))
            load(Turn(k + 1, 1, N - T))
            store(Turn(k, 1, (NT - 3) * T))
            store(Turn(k + 1, 0, (NT - 2) * T))
            store(Turn(k + 1, 1, N - T), last=True)

            with sp.Fori(0, G // 2) as i:
                for s in range(2):
                    tr = Turn(i, s)
                    tr.now(sp, q3["hs_in"], 64)
                    sp.dma_start(hsrc[bass.ds(tr.t, 1), :, :].rearrange("o p f -> (o p) f"), fa[:, s, :, :].rearrange("p j f -> p (j f)")).then_inc(q3["h_out"][s], 16)
            q3["h_out"].all(sp, 16)
            q3["dif"].all(sp)
            with sp.Fori(0, G // 2) as i:
                for s in range(2):
                    tr = Turn(i, s)
                    tr.again(sp, q4["msg"])
                    sp.dma_start(fa[:, s, :, :].rearrange("p j f -> p (j f)"), hsrc[bass.ds(tr.t, 1), :, :].rearrange("o p f -> (o p) f")).then_inc(q4["h_in"][s], 16)
            qn["x4_out"].all(sp, 16)
            q5["out"].all(sp, 64)

        @block.gpsimd
        def _(pool):
            nc.gpsimd.memset(ident[:], 0.0).then_inc(s_pset, 1)
            nc.gpsimd.memset(lower[:], 1.0).then_inc(s_pset, 1)
            nc.gpsimd.iota(src_s[:], pattern=[[0, C]], base=N, channel_multiplier=J).then_inc(s_pad, 1)
            nc.gpsimd.iota(dst_s[:], pattern=[[0, C]], base=N, channel_multiplier=J).then_inc(s_pad, 1)
            nc.gpsimd.iota(part_i[:], pattern=[[0, 1]], base=0, channel_multiplier=1).then_inc(s_const, 1)
            nc.gpsimd.iota(dummy_i[:], pattern=[[1, J], [0, 2]], base=N, channel_multiplier=J).then_inc(s_const, 1)
            pool.wait_ge(s_pset, 2)
            nc.gpsimd.affine_select(out=ident[:], in_=ident[:], compare_op=ALU.not_equal, fill=1.0, base=0,
                                    pattern=[[-1, P]], channel_multiplier=1).then_inc(s_const, 1)
            nc.gpsimd.affine_select(out=lower[:], in_=lower[:], compare_op=ALU.is_gt, fill=0.0, base=0,
                                    pattern=[[1, P]], channel_multiplier=-1).then_inc(s_const, 1)
            pool.wait_ge(s_e, 16 * 7)

            def index(tr, q, key, slot, source):
                nc.gpsimd.tensor_copy(slot, source).then_inc(q[key][tr.s], 1)
                tr.now(pool, q[key])
                gate(pool)

            def gather(tab, idx, tiles, done):
                for j in range(J):
                    nc.gpsimd.indirect_dma_start(tiles[j], None, tab, bass.IndirectOffsetOnAxis(idx[:, j:j + 1], 0)).then_inc(done, 16)

            def add(tab, idx, tiles, done):
                for j in range(J):
                    nc.gpsimd.indirect_dma_start(tab, bass.IndirectOffsetOnAxis(idx[j], 0), tiles[j], None, compute_op=ALU.add).then_inc(done, 16)

            def rows4(tile, s):
                return [tile[:, s, j, :] for j in range(J)]

            def skewed(first, second):
                first(Turn(0, 0))
                with pool.Fori(0, G // 2 - 1) as i:
                    first(Turn(i, 1))
                    second(Turn(i, 0))
                    first(Turn(i + 1, 0))
                    second(Turn(i, 1))
                first(Turn(G // 2 - 1, 1))
                second(Turn(G // 2 - 1, 0))
                second(Turn(G // 2 - 1, 1))

            def x_rows(tr):
                tr.again(pool, q1["xT_ps"])
                tr.again(pool, q1["x_out"], 16)
                tr.again(pool, q1["x_in"], 64)
                gate(pool)
                index(tr, q1, "gidx", gi[:, tr.s, :], src_x[:, bass.ds(tr.t * J, J)])
                gather(x, gi[:, tr.s, :], rows4(fa, tr.s), q1["x_in"][tr.s])

            def add_sums(tr):
                tr.now(pool, q1["rows"])
                tr.before(pool, q1["added"], 64)
                tr.before(pool, q1["attr_added"], 64)
                gate(pool)
                index(tr, q1, "uidx", ui[:, tr.s, :, :], uniq[:, bass.ds(tr.t * J, J), :])
                tr.now(pool, q1["attr_kept"])
                gate(pool)
                add(attr, [ui[:, tr.s, j, 0:1] for j in range(J)], rows4(ag, tr.s), q1["attr_added"][tr.s])
                tr.now(pool, q1["sum_kept"])
                gate(pool)
                add(agg0, [ui[:, tr.s, j, 1:2] for j in range(J)], rows4(fd, tr.s), q1["added"][tr.s])

            turns = NR // (16 * P) + 1
            x_rows(Turn(0, 0))
            pool.wait_ge(s_fill0, 16 * turns)
            pool.wait_ge(s_filla, 16 * turns)
            with pool.Fori(0, G // 2 - 1) as i:
                x_rows(Turn(i, 1))
                add_sums(Turn(i, 0))
                x_rows(Turn(i + 1, 0))
                add_sums(Turn(i, 1))
            x_rows(Turn(G // 2 - 1, 1))
            add_sums(Turn(G // 2 - 1, 0))
            add_sums(Turn(G // 2 - 1, 1))

            q1["added"].all(pool, 64)
            q1["attr_added"].all(pool, 64)
            pool.wait_ge(s_fill1, 16 * turns)
            gate(pool)

            def agg_rows(tr):
                tr.again(pool, q2["v"])
                tr.again(pool, q2["agg_in"], 64)
                gate(pool)
                index(tr, q2, "gidx", gi[:, tr.s, :], src_x[:, bass.ds(tr.t * J, J)])
                gather(agg0, gi[:, tr.s, :], rows4(fb, tr.s), q2["agg_in"][tr.s])

            def add_layer1(tr):
                tr.before(pool, q2["added"], 64)
                gate(pool)
                index(tr, q2, "uidx", ui[:, tr.s, :, 1:2], uniq[:, bass.ds(tr.t * J, J), 1:2])
                tr.now(pool, q2["sum_kept"])
                gate(pool)
                add(agg1, [ui[:, tr.s, j, 1:2] for j in range(J)], rows4(fd, tr.s), q2["added"][tr.s])

            skewed(agg_rows, add_layer1)

            def residual(tr):
                tr.now(pool, qn["x2"])
                tr.again(pool, qn["t3"])
                nc.gpsimd.tensor_tensor(fd[:, tr.s, :, :], x2s[:, tr.s, :, :], b4b[:, :, :], ALU.add).then_inc(qn["x2b"][tr.s], 1)

            pool.wait_ge(s_dup, 1)
            q2["added"].all(pool, 64)
            with pool.Fori(0, NT // 2) as i:
                for s in range(2):
                    residual(Turn(i, s))

            qn["x3_out"].all(pool, 16)
            qn["t3"].all(pool)
            pool.wait_ge(x3_pad, 16)
            pool.wait_ge(s_filld, 16)

            def h_rows(tr):
                tr.again(pool, q3["dif"])
                tr.again(pool, q3["h_out"], 16)
                tr.again(pool, q3["hs_in"], 64)
                tr.again(pool, q3["hd_in"], 64)
                gate(pool)
                nc.gpsimd.tensor_copy(gi[:, tr.s, :], src_x[:, bass.ds(tr.t * J, J)]).then_inc(q3["gidx"][tr.s], 1)
                nc.gpsimd.tensor_copy(gi2[:, tr.s, :], dst_x[:, bass.ds(tr.t * J, J)]).then_inc(q3["gidx2"][tr.s], 1)
                tr.now(pool, q3["gidx"])
                tr.now(pool, q3["gidx2"])
                gate(pool)
                gather(x3, gi[:, tr.s, :], rows4(fa, tr.s), q3["hs_in"][tr.s])
                gather(x3, gi2[:, tr.s, :], rows4(fb, tr.s), q3["hd_in"][tr.s])

            def add_den(tr):
                tr.before(pool, q3["added"], 64)
                gate(pool)
                index(tr, q3, "uidx", ui[:, tr.s, :, 0:1], uniq[:, bass.ds(tr.t * J, J), 0:1])
                tr.now(pool, q3["sum_kept"])
                gate(pool)
                add(den, [ui[:, tr.s, j, 0:1] for j in range(J)], [sm2[:, tr.s, j:j + 1] for j in range(J)], q3["added"][tr.s])

            skewed(h_rows, add_den)

            q3["added"].all(pool, 64)
            q3["hs_in"].all(pool, 64)
            q3["hd_in"].all(pool, 64)
            q3["sum"].all(pool)
            q3["att_saved"].all(pool)
            gate(pool)

            def den_rows(tr):
                tr.again(pool, q4["msg"])
                tr.again(pool, q4["den_in"], 64)
                gate(pool)
                index(tr, q4, "gidx", gi[:, tr.s, :], src_s[:, bass.ds(tr.t * J, J)])
                gather(den, gi[:, tr.s, :], [sm[:, tr.s, j:j + 1] for j in range(J)], q4["den_in"][tr.s])

            def add_layer3(tr):
                tr.before(pool, q4["added"], 64)
                gate(pool)
                index(tr, q4, "uidx", ui[:, tr.s, :, 1:2], uniq[:, bass.ds(tr.t * J, J), 1:2])
                tr.now(pool, q4["sum_kept"])
                gate(pool)
                add(x3, [ui[:, tr.s, j, 1:2] for j in range(J)], rows4(fd, tr.s), q4["added"][tr.s])

            skewed(den_rows, add_layer3)

            q4["added"].all(pool, 64)
            q4["sum"].all(pool)
            qn["x4_out"].all(pool, 16)
            gate(pool)

            def sum_rows(tr):
                tr.again(pool, q5["y"])
                tr.again(pool, q5["out"], 64)
                gate(pool)
                nc.gpsimd.tensor_copy(gi[:, tr.s, :], dst_x[:, bass.ds(tr.t * J, J)]).then_inc(q5["gidx"][tr.s], 1)
                nc.gpsimd.tensor_copy(gi2[:, tr.s, :], uniq[:, bass.ds(tr.t * J, J), 1:2].rearrange("p j o -> p (j o)")).then_inc(q5["gidx2"][tr.s], 1)
                tr.now(pool, q5["gidx"])
                tr.now(pool, q5["gidx2"])
                gate(pool)
                gather(x3, gi[:, tr.s, :], rows4(fa, tr.s), q5["x_in"][tr.s])

            def put_rows(tr):
                tr.now(pool, q5["y"])
                tr.before(pool, q5["out"], 64)
                gate(pool)
                for j in range(J):
                    nc.gpsimd.indirect_dma_start(out, bass.IndirectOffsetOnAxis(gi2[:, tr.s, j:j + 1], 0), fd[:, tr.s, j, :],
                                                 None, bounds_check=N - 1, oob_is_err=False).then_inc(q5["out"][tr.s], 16)

            skewed(sum_rows, put_rows)

        @block.vector
        def _(dve):
            nc.vector.memset(zeros[:], 0.0).then_inc(s_zero, 1)
            nc.vector.memset(src_x[:], 0)
            nc.vector.memset(dst_x[:], 0)
            nc.vector.memset(et_i[:], 0).then_inc(s_pad, 1)
            nc.vector.memset(ew_s[:], 0.0).then_inc(s_pad, 1)
            nc.vector.memset(nrm[:], 0.0).then_inc(s_pad, 1)
            nc.vector.memset(ones[:], 1.0)
            nc.vector.memset(at[:], 0.0).then_inc(s_at, 1)
            dve.wait_ge(s_at, 1)
            nc.vector.memset(at[0:EP, :, :, A:AW], 1.0).then_inc(s_at, 1)
            dve.wait_ge(s_const, 4)
            nc.vector.tensor_copy(part[:], part_i[:])
            nc.vector.tensor_copy(dummy[:], dummy_i[:])
            dve.wait_ge(s_e, 16 * 7)
            for k, tile in ((SRC, src_s), (DST, dst_s), (ETYPE, et_i), (NORM, nrm), (EW, ew_s)):
                nc.vector.tensor_copy(meta[:, :, k:k + 1], tile[:].rearrange("p (c o) -> p c o", o=1)).then_inc(s_meta, 1)
            dve.wait_ge(s_meta, 5)

            def norm_scale(stp, width):
                a, b, v, y = (t[:, 0:width] for t in (na, nb_, nv, ny))
                stp.step(nc.vector.tensor_scalar(y.bitcast(I32), v.bitcast(I32), -0.5, MAGIC, ALU.mult, ALU.add))
                for _ in range(3):
                    stp.step(nc.vector.scalar_tensor_tensor(a, y, -0.5, y, ALU.mult, ALU.mult))
                    stp.step(nc.vector.tensor_tensor(b, a, v, ALU.mult))
                    stp.step(nc.vector.scalar_tensor_tensor(y, b, 1.5, y, ALU.add, ALU.mult))

            NORM_STEPS = 10

            def stats(stp, v):
                for j in range(J):
                    stp.done(nc.vector.bn_stats(st[:, j, :], v[:, j, :]))
                stp.wait()
                stp.done(nc.vector.tensor_tensor(h_sum[:], st[:, :, 1], st[:, :, 4], ALU.add))
                stp.done(nc.vector.tensor_tensor(h_dif[:], st[:, :, 1], st[:, :, 4], ALU.subtract))
                stp.done(nc.vector.tensor_tensor(h_sq[:], st[:, :, 2], st[:, :, 5], ALU.add))
                stp.wait()
                stp.done(nc.vector.tensor_scalar(mv[:, :, 0], h_sum[:], 0.5, None, ALU.mult))
                stp.step(nc.vector.scalar_tensor_tensor(h_dif[:], h_dif[:], 0.25, h_dif[:], ALU.mult, ALU.mult))
                stp.step(nc.vector.scalar_tensor_tensor(mv[:, :, 1], h_sq[:], 1.0 / D, h_dif[:], ALU.mult, ALU.add))

            STATS_STEPS = J + 6

            def equal(tr, bank, field, out4, done):
                for k in range(J):
                    last = nc.vector.tensor_scalar(out4[:, k, :], bank, m[:, tr.s, k, field:field + 1], None, ALU.is_equal)
                last.then_inc(done, 1)

            def meta_slot(tr, q):
                nc.vector.tensor_scalar(m[:, tr.s, :, :], meta[:, bass.ds(tr.t * J, J), :], 0.0, None,
                                        ALU.add).then_inc(q["meta"][tr.s], 1)
                tr.now(dve, q["meta"])

            def low(eq, out4):
                for j in range(J):
                    last = nc.vector.tensor_tensor(out4[:, j, :], eq[:, j, j * P:(j + 1) * P], lower[:], ALU.mult)
                return last

            def message(tr, stp, j):
                y = yAB[j % 2]
                dve.wait_ge(q1["y"][tr.s], tr.i * J + (j + 1))
                if j < 2:
                    tr.before(dve, q1["msg"], J)
                else:
                    dve.wait_ge(q1["msg"][tr.s], tr.i * J + (j - 1))
                ins = nc.vector.tensor_tensor(prod[:, j % 2, :, :], y[:].rearrange("p (b f) -> p b f", b=NB),
                                              cf[:, j, :].rearrange("p (b o) -> p b o", o=1).to_broadcast([P, NB, D]), ALU.mult)
                ins.then_inc(q1["y_read"][tr.s], 1)
                dve.wait_ge(q1["y_read"][tr.s], tr.i * J + (j + 1))
                nc.vector.tensor_reduce(fc[:, tr.s, j, :], prod[:, j % 2, :, :].rearrange("p b f -> p f b"), AX.X, ALU.add).then_inc(q1["msg"][tr.s], 1)

            with dve.Fori(0, G // 2) as i:
                for s in range(2):
                    tr = Turn(i, s)
                    stp = Steps(dve, c1s, tr, 2)
                    tr.again(dve, q1["sum"])
                    tr.again(dve, q1["rows"])
                    meta_slot(tr, q1)
                    nc.vector.tensor_tensor(dd[:], dummy[:], m[:, s, :, 0:2], ALU.subtract)
                    tr.now(dve, q1["types_bc"])
                    nc.vector.tensor_scalar(ot[:], bk[0][0:R, :], part[0:R, :], None, ALU.is_equal).then_inc(q1["type_hot"][s], 1)
                    tr.now(dve, q1["dst_bc"])
                    equal(tr, bk[1][:], DST, big0[:, 0, :, :], q1["dst_eq"][s])
                    tr.now(dve, q1["coef_ps"])
                    stp.done(nc.vector.tensor_tensor(cf[:], bk[0][:, 0:J * NB].rearrange("p (j b) -> p j b", b=NB),
                                                     m[:, s, :, NORM:NORM + 1].to_broadcast([P, J, NB]), ALU.mult))
                    tr.now(dve, q1["dst_eq"])
                    low(big0[:, 0, :, :], sl[:, 1, :, :])
                    stp.wait()
                    message(tr, stp, 0)
                    tr.now(dve, q1["src_bc"])
                    equal(tr, bk[1][:], SRC, big1[:, :, :], q1["src_eq"][s])
                    tr.now(dve, q1["src_eq"])
                    low(big1[:, :, :], sl[:, 0, :, :]).then_inc(q1["low"][s], 1)
                    for j in range(1, J):
                        message(tr, stp, j)
                    tr.now(dve, q1["earlier"])
                    stp.step(nc.vector.scalar_tensor_tensor(nf[:], bk[0][:, 64:64 + 2 * J].rearrange("p (j v) -> p j v", v=2),
                                                            1.0, dd[:], ALU.min, ALU.mult))
                    nc.vector.tensor_tensor(uniq[:, bass.ds(tr.t * J, J), :], nf[:], m[:, s, :, 0:2], ALU.add).then_inc(q1["rows"][s], 1)
                    stp.close()
            dve.wait_ge(s_w, 16 * WEIGHTS)
            for k in range(1, J):
                nc.vector.tensor_copy(b4b[:, k, :], b4b[:, 0, :])
            for k in range(1, 16):
                last = nc.vector.tensor_copy(row1[:, k, :], row1[:, 0, :])
            last.then_inc(s_dup, 1)

            S2 = STATS_STEPS + 1 + NORM_STEPS + 2
            with dve.Fori(0, G // 2) as i:
                for s in range(2):
                    tr = Turn(i, s)
                    stp = Steps(dve, c2s, tr, S2)
                    tr.again(dve, q2["sum"])
                    meta_slot(tr, q2)
                    tr.now(dve, q2["x_in"], 16)
                    tr.now(dve, q2["agg_in"], 64)
                    tr.again(dve, q2["y"])
                    nc.vector.scalar_tensor_tensor(fe[:, s, :, :], fb[:, s, :, :], 0.0, fa[:, s, :, :], ALU.max, ALU.add).then_inc(q2["v"][s], 1)
                    tr.now(dve, q2["v"])
                    stats(stp, fe[:, s, :, :])
                    stp.step(nc.vector.tensor_scalar(nv[:, 0:J], mv[:, :, 1], EPS, None, ALU.add))
                    norm_scale(stp, J)
                    stp.step(nc.vector.tensor_tensor(rc[:], ny[:, 0:J], m[:, s, :, EW], ALU.mult))
                    stp.step(nc.vector.tensor_tensor(na[:, 0:J], mv[:, :, 0], rc[:], ALU.mult))
                    stp.close()
                    tr.again(dve, q2["yT_ps"])
                    for j in range(J):
                        last = nc.vector.tensor_scalar(fc[:, s, j, :], fe[:, s, j, :], rc[:, j:j + 1], na[:, j:j + 1], ALU.mult, ALU.subtract)
                    last.then_inc(q2["y"][s], 1)
                    tr.now(dve, q2["dst_bc"])
                    equal(tr, bk[1][:], DST, big0[:, 0, :, :], q2["dst_eq"][s])

            FRONT = 1 + (STATS_STEPS + 1 + NORM_STEPS) + 1 + (STATS_STEPS + 1 + NORM_STEPS) + 2
            BACK = STATS_STEPS + 2 + NORM_STEPS

            def front(tr):
                s = tr.s
                stp = Steps(dve, cna, tr, FRONT)
                tr.now(dve, qn["in"], 64)
                v = fa[:, s, :, :]
                stp.step(nc.vector.scalar_tensor_tensor(v, fb[:, s, :, :], 0.0, v, ALU.max, ALU.add))
                stats(stp, v)
                stp.step(nc.vector.tensor_scalar(nv[:, 0:J], mv[:, :, 1], EPS, None, ALU.add))
                norm_scale(stp, J)
                for j in range(J):
                    last = nc.vector.scalar_tensor_tensor(v[:, j, :], v[:, j, :], ny[:, j:j + 1], fc[:, s, j, :], ALU.mult, ALU.add)
                stp.step(last)
                stats(stp, v)
                stp.step(nc.vector.tensor_scalar(nv[:, 0:J], mv[:, :, 1], EPS, None, ALU.add))
                norm_scale(stp, J)
                tr.again(dve, qn["x2T_ps"])
                tr.again(dve, qn["x2b"])
                for j in range(J):
                    last = nc.vector.tensor_scalar(x2s[:, s, j, :], v[:, j, :], mv[:, j, 0:1], ny[:, j:j + 1], ALU.subtract, ALU.mult)
                last.then_inc(qn["x2"][s], 1)
                stp.step(nc.vector.tensor_scalar(rc[:], at[:, s, :, A], 1.0, None, ALU.max))
                stp.step(nc.vector.reciprocal(rc[:], rc[:]))
                stp.close()
                tr.again(dve, qn["agT_ps"])
                nc.vector.tensor_tensor(ag[:, s, :, 0:A], at[:, s, :, 0:A], rc[:].rearrange("p (j o) -> p j o", o=1).to_broadcast([P, J, A]), ALU.mult).then_inc(qn["attr_mean"][s], 1)

            def scale(tr):
                tr.now(dve, qn["attn"])
                for k in range(2):
                    last = nc.vector.tensor_tensor(rr[:, tr.s, 2 + k, :], rr[:, tr.s, k, :], att_b[:, tr.s, :], ALU.mult)
                last.then_inc(qn["scaled"][tr.s], 1)

            def back(tr):
                s = tr.s
                tr.now(dve, qn["h3_ps"])
                tr.before(dve, qn["h3"])
                for k in range(2):
                    last = nc.vector.scalar_tensor_tensor(h3[:, 2 + k, :], att_b[:, s, :], c23[:, k:k + 1], yB[:, k * T:(k + 1) * T], ALU.mult, ALU.add)
                last.then_inc(qn["h3_pre"][s], 1)

            def tail(tr):
                s = tr.s
                stp = Steps(dve, cnb, tr, BACK)
                tr.now(dve, qn["y_ps"])
                tr.now(dve, qn["x2b"])
                t3 = fd[:, s, :, :]
                nc.vector.tensor_tensor(t3, bk[3][:].rearrange("p (j f) -> p j f", j=J), t3, ALU.add).then_inc(qn["t0"][s], 1)
                tr.now(dve, qn["t0"])
                stats(stp, t3)
                stp.step(nc.vector.tensor_scalar(nv[:, 0:J], mv[:, :, 1], EPS, None, ALU.add))
                stp.step(nc.vector.scalar_tensor_tensor(nv[:, J:2 * J], nv[:, 0:J], EPS, mv[:, :, 1], ALU.mult, ALU.add))
                norm_scale(stp, 2 * J)
                stp.close()
                tr.again(dve, qn["x3_out"], 16)
                for j in range(J):
                    last = nc.vector.tensor_scalar(fe[:, s, j, :], t3[:, j, :], mv[:, j, 0:1], ny[:, j:j + 1], ALU.subtract, ALU.mult)
                last.then_inc(qn["x3"][s], 1)
                tr.again(dve, qn["x4_out"], 16)
                for j in range(J):
                    last = nc.vector.tensor_scalar(ff[:, s, j, :], t3[:, j, :], mv[:, j, 0:1], ny[:, J + j:J + j + 1], ALU.subtract, ALU.mult)
                last.then_inc(qn["x4"][s], 1)
                tr.now(dve, qn["x3"])
                tr.now(dve, qn["x4"])
                nc.vector.tensor_copy(st[:, 0, 0:1], ones[:]).then_inc(qn["t3"][s], 1)

            dve.wait_ge(s_wpk, 1)
            front(Turn(0, 0))
            scale(Turn(0, 0))
            with dve.Fori(0, NT // 2 - 1) as i:
                for a, b in ((Turn(i, 0), Turn(i, 1)), (Turn(i, 1), Turn(i + 1, 0))):
                    front(b)
                    back(a)
                    scale(b)
                    tail(a)
            k = NT // 2 - 1
            front(Turn(k, 1))
            back(Turn(k, 0))
            scale(Turn(k, 1))
            tail(Turn(k, 0))
            back(Turn(k, 1))
            tail(Turn(k, 1))

            with dve.Fori(0, G // 2) as i:
                for s in range(2):
                    tr = Turn(i, s)
                    tr.again(dve, q3["sum"])
                    meta_slot(tr, q3)
                    tr.now(dve, q3["hs_in"], 64)
                    tr.now(dve, q3["hd_in"], 64)
                    tr.again(dve, q3["dT_ps"])
                    nc.vector.tensor_tensor(fc[:, s, :, :], fa[:, s, :, :], fb[:, s, :, :], ALU.subtract).then_inc(q3["dif"][s], 1)
                    tr.now(dve, q3["src_bc"])
                    equal(tr, bk[1][:], SRC, big0[:, 0, :, :], q3["src_eq"][s])
                    tr.now(dve, q3["att"])
                    nc.vector.tensor_scalar(att_all[:, bass.ds(tr.t * J, J)], sm[:, s, :], 0.0, None, ALU.add).then_inc(q3["att_saved"][s], 1)

            q3["att_saved"].all(dve)
            with dve.Fori(0, G // 2) as i:
                for s in range(2):
                    tr = Turn(i, s)
                    stp = Steps(dve, c4s, tr, 2)
                    tr.again(dve, q4["sum"])
                    meta_slot(tr, q4)
                    tr.now(dve, q4["h_in"], 16)
                    tr.now(dve, q4["den_in"], 64)
                    stp.step(nc.vector.reciprocal(rc[:], sm[:, s, :]))
                    stp.step(nc.vector.tensor_tensor(rc[:], rc[:], att_all[:, bass.ds(tr.t * J, J)], ALU.mult))
                    stp.close()
                    nc.vector.tensor_tensor(fc[:, s, :, :], fa[:, s, :, :], rc[:].rearrange("p (j o) -> p j o", o=1).to_broadcast([P, J, D]), ALU.mult).then_inc(q4["msg"][s], 1)
                    tr.now(dve, q4["dst_bc"])
                    equal(tr, bk[1][:], DST, big0[:, 0, :, :], q4["dst_eq"][s])

            S5 = STATS_STEPS + 1 + NORM_STEPS
            with dve.Fori(0, G // 2) as i:
                for s in range(2):
                    tr = Turn(i, s)
                    stp = Steps(dve, c5s, tr, S5)
                    tr.now(dve, q5["x_in"], 64)
                    v = fa[:, s, :, :]
                    stats(stp, v)
                    stp.step(nc.vector.tensor_scalar(nv[:, 0:J], mv[:, :, 1], EPS, None, ALU.add))
                    norm_scale(stp, J)
                    stp.close()
                    tr.again(dve, q5["out"], 64)
                    for j in range(J):
                        last = nc.vector.tensor_scalar(fd[:, s, j, :], v[:, j, :], mv[:, j, 0:1], ny[:, j:j + 1], ALU.subtract, ALU.mult)
                    last.then_inc(q5["y"][s], 1)

        @block.scalar
        def _(act):
            act.wait_ge(s_w, 16 * WEIGHTS)
            nc.scalar.activation(wab[:, 0, :], zeros[:, 0:P], ACT.Identity, bias=wac[:, 0:1])
            nc.scalar.activation(wab[:, 1, :], zeros[:, 0:P], ACT.Identity, bias=wac[:, 1:2])
            nc.scalar.activation(b2b[:, 0, :], zeros[:, 0:P], ACT.Identity, bias=b2c[:, 0:1])
            nc.scalar.activation(b2b[:, 1, :], zeros[:, 0:P], ACT.Identity, bias=b2c[:, 1:2])
            act.wait_ge(s_wt, 1)
            nc.scalar.copy(w2T[:, 0, :], bk[0][:, 0:H])
            nc.scalar.copy(w2T[:, 1, :], bk[0][:, H:2 * H])
            nc.scalar.copy(l1wT[:], bk[1][:, 0:D]).then_inc(s_wte, 1)
            act.wait_ge(s_wp, 1)
            nc.scalar.copy(w23[:, 0, :], bk[2][:, 0:H])
            nc.scalar.copy(w23[:, 1, :], bk[2][:, H:2 * H])
            nc.scalar.copy(w2a[:, 0, :], bk[3][:, 0:P])
            nc.scalar.copy(w2a[:, 1, :], bk[3][:, P:2 * P])
            nc.scalar.copy(c23[:], bk[3][:, 2 * P:2 * P + 2])
            nc.scalar.activation(zb[:], bk[3][:, 2 * P + 2:2 * P + 3], ACT.Identity, bias=bab[:]).then_inc(s_wpk, 1)

            with act.Fori(0, G // 2) as i:
                for s in range(2):
                    tr = Turn(i, s)
                    tr.now(act, q1["xT_ps"])
                    tr.again(act, q1["y"], J)
                    nc.scalar.copy(x2T[:, s, :], bk[1][:]).then_inc(q1["xT"][s], 1)
                    tr.now(act, q1["attr_sum"])
                    tr.again(act, q1["attr_added"], 64)
                    nc.scalar.copy(ag[:, s, :, :].rearrange("p j f -> p (j f)"), bk[3][:, 0:J * AW]).then_inc(q1["attr_kept"][s], 1)
                    tr.now(act, q1["sum"])
                    tr.again(act, q1["added"], 64)
                    nc.scalar.copy(fd[:, s, :, :].rearrange("p j f -> p (j f)"), bk[2][:]).then_inc(q1["sum_kept"][s], 1)
            q1["added"].all(act, 64)
            with act.Fori(0, G // 2) as i:
                for s in range(2):
                    tr = Turn(i, s)
                    tr.now(act, q2["yT_ps"])
                    tr.again(act, q2["z_ps"])
                    nc.scalar.copy(x2T[:, s, :], bk[0][:]).then_inc(q2["yT"][s], 1)
                    tr.now(act, q2["z_ps"])
                    tr.again(act, q2["sum"])
                    nc.scalar.copy(ff[:, s, :, :].rearrange("p j f -> p (j f)"), bk[3][:]).then_inc(q2["z"][s], 1)
                    tr.now(act, q2["sum"])
                    tr.again(act, q2["added"], 64)
                    nc.scalar.copy(fd[:, s, :, :].rearrange("p j f -> p (j f)"), bk[2][:]).then_inc(q2["sum_kept"][s], 1)
            q2["sum"].all(act)

            def front(tr):
                s = tr.s
                tr.now(act, qn["x2T_ps"])
                tr.again(act, qn["h3_ps"])
                nc.scalar.copy(x2T[:, s, :], bk[0][:]).then_inc(qn["x2T"][s], 1)
                tr.now(act, qn["agT_ps"])
                tr.again(act, qn["h1_ps"])
                nc.scalar.copy(agT[:, s, :], bk[1][0:A, :]).then_inc(qn["agT"][s], 1)
                tr.now(act, qn["h1_ps"])
                tr.again(act, qn["scaled"])
                for k in range(2):
                    last = nc.scalar.activation(rr[:, s, k, :], yA[:, k * T:(k + 1) * T], ACT.Relu, bias=b1c[:, k:k + 1])
                last.then_inc(qn["h1"][s], 1)

            def attn(tr):
                tr.now(act, qn["z_ps"])
                tr.again(act, qn["h3_pre"])
                nc.scalar.activation(att_b[:, tr.s, :], bk[2][:], ACT.Sigmoid, bias=zb[:]).then_inc(qn["attn"][tr.s], 1)

            def back(tr):
                tr.now(act, qn["h3_pre"])
                tr.before(act, qn["y_ps"])
                for k in range(2):
                    last = nc.scalar.activation(h3[:, k, :], h3[:, 2 + k, :], ACT.Relu, bias=b3c[:, k:k + 1])
                last.then_inc(qn["h3"][tr.s], 1)

            front(Turn(0, 0))
            attn(Turn(0, 0))
            with act.Fori(0, NT // 2 - 1) as i:
                for a, b in ((Turn(i, 0), Turn(i, 1)), (Turn(i, 1), Turn(i + 1, 0))):
                    front(b)
                    attn(b)
                    back(a)
            k = NT // 2 - 1
            front(Turn(k, 1))
            attn(Turn(k, 1))
            back(Turn(k, 0))
            back(Turn(k, 1))

            with act.Fori(0, G // 2) as i:
                for s in range(2):
                    tr = Turn(i, s)
                    tr.now(act, q3["dT_ps"])
                    tr.again(act, q3["hid_ps"])
                    nc.scalar.copy(x2T[:, s, :], bk[0][:]).then_inc(q3["dT"][s], 1)
                    tr.now(act, q3["hid_ps"])
                    tr.again(act, q3["att_ps"])
                    nc.scalar.activation(att_b[:, s, :], bk[2][:], ACT.Relu, bias=c1c[:]).then_inc(q3["hid"][s], 1)
                    tr.now(act, q3["att_ps"])
                    tr.again(act, q3["att"])
                    nc.scalar.activation(rc2[:, s, :], bk[3][:, 0:J], ACT.Relu, bias=c2c[:]).then_inc(q3["att_relu"][s], 1)
                    tr.now(act, q3["att_relu"])
                    tr.again(act, q3["att_saved"])
                    tr.again(act, q3["sum"])
                    nc.scalar.activation(sm[:, s, :], rc2[:, s, :], ACT.Sigmoid).then_inc(q3["att"][s], 1)
                    tr.now(act, q3["sum"])
                    tr.again(act, q3["added"], 64)
                    nc.scalar.copy(sm2[:, s, :], bk[3][:, 8:8 + J]).then_inc(q3["sum_kept"][s], 1)
            with act.Fori(0, G // 2) as i:
                for s in range(2):
                    tr = Turn(i, s)
                    tr.now(act, q4["sum"])
                    tr.again(act, q4["added"], 64)
                    nc.scalar.copy(fd[:, s, :, :].rearrange("p j f -> p (j f)"), bk[2][:]).then_inc(q4["sum_kept"][s], 1)



        @block.tensor
        def _(pe):
            def mm(o, l, r, k, n):
                return nc.tensor.matmul(o, l, r, start=(k == 0), stop=(k == n - 1))

            pe.wait_ge(s_const, 4)
            pe.wait_ge(s_w, 16 * WEIGHTS)
            for k in range(2):
                for h in range(2):
                    nc.tensor.transpose(bk[0][:, h * H + k * P:h * H + (k + 1) * P], w2n[:, k, h * P:(h + 1) * P], ident[:])
            nc.tensor.transpose(bk[1][:, 0:D], l1w[:], ident[:]).then_inc(s_wt, 1)
            pe.wait_ge(s_wte, 1)
            for i_ in range(2):
                for k in range(2):
                    mm(bk[2][:, i_ * H:(i_ + 1) * H], w2T[:, k, i_ * P:(i_ + 1) * P], w3h[:, k, :], k, 2)
            for i_ in range(2):
                for k in range(2):
                    mm(bk[3][:, i_ * P:(i_ + 1) * P], w2T[:, k, i_ * P:(i_ + 1) * P], wab[:, k, :], k, 2)
            for h in range(2):
                for k in range(2):
                    mm(bk[3][:, 2 * P + h:2 * P + h + 1], w3h[:, k, h * P:(h + 1) * P], b2c[:, k:k + 1], k, 2)
            for k in range(2):
                last = mm(bk[3][:, 2 * P + 2:2 * P + 3], b2b[:, k, :], wac[:, k:k + 1], k, 2)
            last.then_inc(s_wp, 1)
            pe.wait_ge(s_wpk, 1)

            def spread(tr, bank, field, done):
                for j in range(J):
                    last = nc.tensor.transpose(cols(bank, j), m[:, tr.s, j, field:field + 1].to_broadcast([P, P]), ident[:])
                last.then_inc(done, 1)

            def turned(bank, tile, s, done, w=D):
                for j in range(J):
                    last = nc.tensor.transpose(bank[0:w, j * P:(j + 1) * P], tile[:, s, j, 0:w], ident[:])
                last.then_inc(done, 1)

            def totals(eq, rows, place, done):
                for j in range(J):
                    for k in range(J):
                        last = mm(place(j), eq[:, k, j * P:(j + 1) * P], rows(k), k, J)
                last.then_inc(done, 1)

            with pe.Fori(0, G // 2) as i:
                for s in range(2):
                    tr = Turn(i, s)
                    eq_d, eq_s = big0[:, 0, :, :], big1[:, :, :]

                    def product(j):
                        if j < 2:
                            tr.before(pe, q1["y_read"], J)
                        else:
                            pe.wait_ge(q1["y_read"][s], i * J + (j - 1))
                        for h in range(2):
                            last = nc.tensor.matmul(yAB[j % 2][:, h * T:(h + 1) * T], x2T[:, s, j * P:(j + 1) * P],
                                                    wcat[:, h * 4:(h + 1) * 4, :].rearrange("p b f -> p (b f)"), start=True, stop=True)
                        last.then_inc(q1["y"][s], 1)

                    tr.now(pe, q1["x_in"], 64)
                    tr.before(pe, q1["src_eq"])
                    turned(bk[1], fa, s, q1["xT_ps"][s])
                    tr.now(pe, q1["meta"])
                    tr.before(pe, q1["rows"])
                    spread(tr, bk[0], ETYPE, q1["types_bc"][s])
                    tr.now(pe, q1["xT"])
                    spread(tr, bk[1], DST, q1["dst_bc"][s])
                    tr.now(pe, q1["type_hot"])
                    for j in range(J):
                        last = nc.tensor.matmul(bk[0][:, j * NB:(j + 1) * NB], ot[:, j * P:(j + 1) * P], comp[:], start=True, stop=True)
                    last.then_inc(q1["coef_ps"][s], 1)
                    product(0)
                    tr.now(pe, q1["dst_eq"])
                    product(1)
                    spread(tr, bk[1], SRC, q1["src_bc"][s])
                    product(2)
                    tr.now(pe, q1["src_eq"])
                    tr.now(pe, q1["attr_in"], 16)
                    tr.before(pe, q1["attr_kept"])
                    totals(eq_s, lambda k: at[:, s, k, :], lambda j: bk[3][:, j * AW:(j + 1) * AW], q1["attr_sum"][s])
                    product(3)
                    tr.now(pe, q1["low"])
                    for j in range(J):
                        for v, eq in ((0, eq_s), (1, eq_d)):
                            o = bk[0][:, 64 + 2 * j + v:65 + 2 * j + v]
                            for k in range(j):
                                mm(o, eq[:, k, j * P:(j + 1) * P], ones[:], k, j + 1)
                            last = mm(o, sl[:, v, j, :], ones[:], j, j + 1)
                    last.then_inc(q1["earlier"][s], 1)
                    tr.now(pe, q1["msg"], J)
                    tr.before(pe, q1["sum_kept"])
                    totals(eq_d, lambda k: fc[:, s, k, :], lambda j: cols(bk[2], j), q1["sum"][s])

            q1["rows"].all(pe)
            q1["src_eq"].all(pe)
            q1["sum_kept"].all(pe)
            q1["attr_kept"].all(pe)
            with pe.Fori(0, G // 2) as i:
                for s in range(2):
                    tr = Turn(i, s)
                    tr.now(pe, q2["meta"])
                    tr.before(pe, q2["dst_eq"])
                    spread(tr, bk[1], DST, q2["dst_bc"][s])
                    tr.now(pe, q2["y"])
                    tr.before(pe, q2["yT"])
                    turned(bk[0], fc, s, q2["yT_ps"][s])
                    tr.now(pe, q2["yT"])
                    tr.before(pe, q2["z"])
                    for j in range(J):
                        last = nc.tensor.matmul(cols(bk[3], j), x2T[:, s, j * P:(j + 1) * P], l1wT[:], start=True, stop=True)
                    last.then_inc(q2["z_ps"][s], 1)
                    tr.now(pe, q2["dst_eq"])
                    tr.now(pe, q2["z"])
                    tr.before(pe, q2["sum_kept"])
                    totals(big0[:, 0, :, :], lambda k: ff[:, s, k, :], lambda j: cols(bk[2], j), q2["sum"][s])

            q2["dst_eq"].all(pe)
            q2["sum_kept"].all(pe)
            q1["y_read"].all(pe, J)

            def front(tr):
                s = tr.s
                tr.now(pe, qn["x2"])
                tr.before(pe, qn["x2T"])
                turned(bk[0], x2s, s, qn["x2T_ps"][s])
                tr.now(pe, qn["attr_mean"])
                tr.before(pe, qn["agT"])
                turned(bk[1], ag, s, qn["agT_ps"][s], A)
                tr.now(pe, qn["x2T"])
                tr.now(pe, qn["agT"])
                tr.before(pe, qn["h1"])
                for k in range(2):
                    mm(yA[:, k * T:(k + 1) * T], w1x[:, k * P:(k + 1) * P], x2T[:, s, :], 0, 2)
                    last = mm(yA[:, k * T:(k + 1) * T], w1a[:, k * P:(k + 1) * P], agT[:, s, :], 1, 2)
                last.then_inc(qn["h1_ps"][s], 1)

            def attn(tr):
                tr.now(pe, qn["h1"])
                tr.before(pe, qn["attn"])
                for k in range(2):
                    last = mm(bk[2][:], w2a[:, k, :], rr[:, tr.s, k, :], k, 2)
                last.then_inc(qn["z_ps"][tr.s], 1)

            def back(tr):
                s = tr.s
                tr.before(pe, qn["h3_pre"])
                tr.now(pe, qn["scaled"])
                for k in range(2):
                    o = yB[:, k * T:(k + 1) * T]
                    mm(o, w3x[:, k * P:(k + 1) * P], x2T[:, s, :], 0, 3)
                    for h in range(2):
                        last = mm(o, w23[:, h, k * P:(k + 1) * P], rr[:, s, 2 + h, :], 1 + h, 3)
                last.then_inc(qn["h3_ps"][s], 1)

            def tail(tr):
                tr.now(pe, qn["h3"])
                tr.before(pe, qn["t0"])
                for j in range(J):
                    for k in range(2):
                        last = mm(cols(bk[3], j), h3[:, k, j * P:(j + 1) * P], w4s[:, k, :], k, 2)
                last.then_inc(qn["y_ps"][tr.s], 1)

            front(Turn(0, 0))
            attn(Turn(0, 0))
            with pe.Fori(0, NT // 2 - 1) as i:
                for a, b in ((Turn(i, 0), Turn(i, 1)), (Turn(i, 1), Turn(i + 1, 0))):
                    back(a)
                    front(b)
                    attn(b)
                    tail(a)
            k = NT // 2 - 1
            back(Turn(k, 0))
            front(Turn(k, 1))
            attn(Turn(k, 1))
            tail(Turn(k, 0))
            back(Turn(k, 1))
            tail(Turn(k, 1))

            qn["t0"].all(pe)
            with pe.Fori(0, G // 2) as i:
                for s in range(2):
                    tr = Turn(i, s)
                    tr.now(pe, q3["dif"])
                    tr.before(pe, q3["dT"])
                    turned(bk[0], fc, s, q3["dT_ps"][s])
                    tr.now(pe, q3["meta"])
                    tr.before(pe, q3["src_eq"])
                    spread(tr, bk[1], SRC, q3["src_bc"][s])
                    tr.now(pe, q3["dT"])
                    tr.before(pe, q3["hid"])
                    nc.tensor.matmul(bk[2][:], v1s[:], x2T[:, s, :], start=True, stop=True).then_inc(q3["hid_ps"][s], 1)
                    tr.now(pe, q3["hid"])
                    tr.before(pe, q3["att_relu"])
                    for j in range(J):
                        last = nc.tensor.matmul(bk[3][:, j:j + 1], att_b[:, s, j * P:(j + 1) * P], v2s[:], start=True, stop=True)
                    last.then_inc(q3["att_ps"][s], 1)
                    tr.now(pe, q3["src_eq"])
                    tr.now(pe, q3["att"])
                    tr.before(pe, q3["sum_kept"])
                    totals(big0[:, 0, :, :], lambda k: sm[:, s, k:k + 1], lambda j: bk[3][:, 8 + j:9 + j], q3["sum"][s])
            q3["src_eq"].all(pe)
            q3["hid"].all(pe)
            with pe.Fori(0, G // 2) as i:
                for s in range(2):
                    tr = Turn(i, s)
                    tr.now(pe, q4["meta"])
                    tr.before(pe, q4["dst_eq"])
                    spread(tr, bk[1], DST, q4["dst_bc"][s])
                    tr.now(pe, q4["dst_eq"])
                    tr.now(pe, q4["msg"])
                    tr.before(pe, q4["sum_kept"])
                    totals(big0[:, 0, :, :], lambda k: fc[:, s, k, :], lambda j: cols(bk[2], j), q4["sum"][s])


_INS = ['x', 'src', 'dst', 'edge_attr_96', 'edge_type_32', 'edge_weight', 'edge_weight1', 'L0_gnn_weight',
        'L0_gnn_w_comp', 'L0_gnn_bias_param', 'L1_gnn_W', 'L1_gnn_b', 'L2_gnn_W1', 'L2_gnn_b1', 'L2_gnn_W2',
        'L2_gnn_b2', 'L2_gnn_Wa', 'L2_gnn_ba', 'L2_gnn_W3', 'L2_gnn_b3', 'L2_gnn_W4', 'L2_gnn_b4', 'L3_gnn_W1',
        'L3_gnn_b1', 'L3_gnn_W2', 'L3_gnn_b2']
_OUTS = [((N, D), 'float32')]


def kernel(**inputs):
    import numpy as _np
    import concourse.bacc as _bacc
    from concourse import mybir as _mybir
    from concourse.bass_utils import run_bass_kernel_spmd as _run

    nc = _bacc.Bacc("TRN2", target_bir_lowering=False, num_devices=1)
    arrays, args = {}, []
    for name in _INS:
        a = _np.ascontiguousarray(inputs[name])
        arrays[f"in_{name}_dram"] = a
        args.append(nc.dram_tensor(f"in_{name}_dram", a.shape, _mybir.dt.from_np(a.dtype), kind="ExternalInput").ap())
    for i, (shape, dtype) in enumerate(_OUTS):
        dt = _mybir.dt.from_np(_np.dtype(dtype))
        args.append(nc.dram_tensor(f"out_{i}_dram", shape, dt, kind="ExternalOutput").ap())
    gnn_kernel(nc, *args)
    r = _run(nc, [arrays], core_ids=[0])
    return r.results[0]["out_0_dram"]
```

```python
from contextlib import ExitStack

import concourse.bass as bass
from concourse import mybir

F32 = mybir.dt.float32
I32 = mybir.dt.int32
ALU = mybir.AluOpType
ACT = mybir.ActivationFunctionType
AX = mybir.AxisListType

P = 128
D = 128
N = 100000
E = 25000
A = 96
AW = A + 1
H = 256
R = 32
NB = 8
EP = 125
C = E // EP
J = 4
G = C // J
DUMMY = J * P
NR = N + DUMMY
T = 512
NT = -(-N // T)
EPS = 1e-5
SRC, DST, ETYPE, NORM, EW, FIELDS = 0, 1, 2, 3, 4, 5
HALF, MINUS_HALF, PER_ROW, NORM_EPS, THREE_HALVES = range(5)
CONSTANTS = (0.5, -0.5, 1.0 / D, EPS, 1.5)
MAGIC = 1597463007.0


class Signal:

    def __init__(self, sems, base, turns):
        self.sems, self.base, self.turns = sems, base, turns

    def __getitem__(self, s):
        return self.sems[s]

    def all(self, eng, each=1):
        for sem in self.sems:
            eng.wait_ge(sem, (self.base + self.turns) * each)


class Turn:

    def __init__(self, i, s, start=None):
        self.i, self.s = i, s
        self.t = i * 2 + s
        self.start = start

    def now(self, eng, sig, each=1):
        eng.wait_ge(sig[self.s], self.i * each + (sig.base + 1) * each)

    def part(self, eng, sig, each, k):
        eng.wait_ge(sig[self.s], self.i * each + (sig.base * each + k))

    def again(self, eng, sig, each=1):
        eng.wait_ge(sig[self.s], self.i * each + sig.base * each)

    def before(self, eng, sig, each=1):
        eng.wait_ge(sig[1 - self.s], self.i * each + (sig.base + self.s) * each)


class Step:

    def __init__(self, n, i=None):
        self.n, self.i = n, i

    def turn(self, d):
        t = self.n + d
        if self.i is None:
            return Turn(t // 2, t % 2, min(t * T, N - T))
        return Turn(self.i + t // 2, t % 2, self.i * (2 * T) + t * T)

    def tile(self, d):
        return self.turn(d) if self.i is not None or 0 <= self.n + d < NT else None


def node_steps(eng, step):
    for n in range(-4, 4):
        step(Step(n))
    with eng.Fori(2, NT // 2 - 3) as i:
        for n in range(2):
            step(Step(n, i))
    for n in range(NT - 6, NT + 3):
        step(Step(n))


class Steps:

    def __init__(self, eng, sem, turn, each):
        self.eng, self.sem, self.each, self.n = eng, sem, each, 0
        self.base = turn.t * each if turn is not None else 0

    def done(self, ins):
        self.n += 1
        assert self.each is None or self.n <= self.each
        ins.then_inc(self.sem, 1)
        return self.n

    def wait(self):
        self.eng.wait_ge(self.sem, self.base + self.n)

    def step(self, ins):
        self.done(ins)
        self.wait()

    def close(self):
        assert self.n == self.each, self.n


def gnn_kernel(nc, x, src, dst, edge_attr, edge_type, edge_weight, edge_weight1, l0_w, l0_comp, l0_b,
               l1_w, l1_b, w1, b1, w2, b2, wa, ba, w3, b3, w4, b4, v1, c1, v2, c2, out):
    ctx = ExitStack()
    with ctx:
        def sb(name, shape, dt=F32):
            return ctx.enter_context(nc.sbuf_tensor(name, shape, dt))

        def ps(name, shape):
            return ctx.enter_context(nc.psum_tensor(name, shape, F32))

        def sem(name):
            return ctx.enter_context(nc.semaphore(name))

        def sem2(name):
            return [sem(name + "_0"), sem(name + "_1")]

        def table(name, shape):
            return nc.dram_tensor(name, shape, F32, kind="Internal").ap()

        agg0 = table("agg0", [NR, D])
        agg1 = table("agg1", [NR, D])
        attr = table("attr", [NR, AW])
        den = table("den", [NR, 1])
        x3 = table("x3", [NR, D])
        xsrc = table("xsrc", [G, P, J * D])
        hsrc = table("hsrc", [G, P, J * D])

        ident = sb("ident", [P, P])
        lower = sb("lower", [P, P])
        ones = sb("ones", [P, 1])
        part = sb("part", [P, 1])
        part_i = sb("part_i", [P, 1], I32)
        dummy = sb("dummy_row", [P, J, 2])
        dummy_i = sb("dummy_row_i", [P, J, 2], I32)
        zeros = sb("zeros", [P, 16 * D])
        row0 = sb("row0", [P, 16, D])
        row1 = sb("row1", [P, 16, D])
        wcat = sb("wcat", [P, NB, D])
        comp = sb("comp", [R, NB])
        l1w = sb("l1w", [P, D])
        l1wT = sb("l1wT", [P, D])
        w1x = sb("w1x", [P, H])
        w1a = sb("w1a", [A, H])
        w2n = sb("w2n", [P, 2, H])
        w2T = sb("w2T", [P, 2, H])
        w3x = sb("w3x", [P, H])
        w3h = sb("w3h", [P, 2, H])
        w23 = sb("w23", [P, 2, H])
        w4s = sb("w4s", [P, 2, D])
        wac = sb("wac", [P, 2])
        wab = sb("wab", [P, 2, P])
        w2a = sb("w2a", [P, 2, P])
        b1c = sb("b1c", [P, 2])
        b2c = sb("b2c", [P, 2])
        b2b = sb("b2b", [P, 2, P])
        b3c = sb("b3c", [P, 2])
        c23 = sb("c23", [P, 2])
        bab = sb("bab", [P, 1])
        zb = sb("zb", [P, 1])
        b4b = sb("b4b", [P, J, D])
        v1s = sb("v1s", [P, D])
        c1c = sb("c1c", [P, 1])
        v2s = sb("v2s", [P, 1])
        c2c = sb("c2c", [P, 1])

        src_x = sb("src_x", [P, C], I32)
        dst_x = sb("dst_x", [P, C], I32)
        src_s = sb("src_s", [P, C], I32)
        dst_s = sb("dst_s", [P, C], I32)
        et_i = sb("et_i", [P, C], I32)
        nrm = sb("nrm", [P, C])
        ew_s = sb("ew_s", [P, C])
        meta = sb("meta", [P, C, FIELDS])
        uniq = sb("uniq", [P, C, 2], I32)
        att_all = sb("att_all", [P, C])

        fa = sb("fa", [P, 2, J, D])
        fb = sb("fb", [P, 2, J, D])
        fc = sb("fc", [P, 2, J, D])
        fd = sb("fd", [P, 2, J, D])
        fe = sb("fe", [P, 2, J, D])
        ff = sb("ff", [P, 2, J, D])
        x2s = sb("x2s", [P, 2, J, D])
        big0 = sb("big0", [P, 2, J, T])
        big1 = sb("big1", [P, J, T])
        sl = sb("sl", [P, 2, J, P])
        at = sb("at", [P, 2, J, AW])
        ag = sb("ag", [P, 2, J, AW])
        m = sb("m", [P, 2, J, FIELDS])
        gi = sb("gi", [P, 2, J], I32)
        gi2 = sb("gi2", [P, 2, J], I32)
        ui = sb("ui", [P, 2, J, 2], I32)
        ot = sb("ot", [R, T])
        cf = sb("cf", [P, J, NB])
        prod = sb("prod", [P, 2, NB, D])
        dd = sb("dd", [P, J, 2])
        nf = sb("nf", [P, J, 2])
        st = sb("st", [P, J, 6])
        mv = sb("mv", [P, J, 2])
        h_sum = sb("h_sum", [P, J])
        h_dif = sb("h_dif", [P, J])
        h_sq = sb("h_sq", [P, J])
        nv = sb("nv", [P, 2 * J])
        ny = sb("ny", [P, 2 * J])
        na = sb("na", [P, 2 * J])
        nb_ = sb("nb_", [P, 2 * J])
        rc = sb("rc", [P, J])
        sm = sb("sm", [P, 2, J])
        sm2 = sb("sm2", [P, 2, J])
        rc2 = sb("rc2", [P, 2, J])
        va = sb("va", [P, 2, J, D])
        vb = sb("vb", [P, 2, J, D])
        t3 = sb("t3", [P, 2, J, D])
        stq = sb("stq", [P, 2, 3, J, 6])
        nmean = sb("nmean", [P, 2, 3, J])
        nry = sb("nry", [P, 2, 4, J])
        nbias = sb("nbias", [P, 2, 2, J])
        pa, pb, pc, pd = (sb(n, [P, 3, J]) for n in ("pa", "pb", "pc", "pd"))
        pv, pe_ = (sb(n, [P, 4, J]) for n in ("pv", "pe"))
        pnm = sb("pnm", [P, J])
        kc = sb("kc", [P, 5])
        x2T = sb("x2T", [P, 2, T])
        agT = sb("agT", [A, 2, T])
        rr = big0
        att_b = sb("att_b", [P, 2, T])
        h3 = big1

        yA = ps("yA", [P, 2 * T])
        yB = ps("yB", [P, 2 * T])
        bk = [ps(f"bk{n}", [P, T]) for n in range(4)]
        yAB = [yA, yB]

        def cols(bank, j):
            return bank[:, j * P:(j + 1) * P]

        s_zero = sem("zeros_set")
        s_const = sem("constants_set")
        s_pad = sem("padding_set")
        s_w = sem("weights_loaded")
        s_e = sem("edges_loaded")
        s_dup = sem("weight_copies_made")
        s_meta = sem("meta_made")
        s_at = sem("attr_slots_set")
        s_wt = sem("weights_transposed")
        s_wte = sem("weights_transposed_kept")
        s_wp = sem("weight_products")
        s_wpk = sem("weight_products_kept")
        s_row = sem("bias_rows_loaded")
        s_fill0 = sem("agg0_filled")
        s_fill1 = sem("agg1_filled")
        s_filla = sem("attr_filled")
        s_filld = sem("den_filled")
        s_gate = sem("pool_gate_passed")
        s_pset = sem("pool_set_up")

        block = ctx.enter_context(nc.Block())

        def edge_rows(a, g):
            return a.rearrange("(p c) f -> p c f", p=EP)[:, bass.ds(g * J, J), :]

        def node_rows(a, start, rows=T):
            return a[bass.ds(start, rows), :].rearrange("(p j) f -> p (j f)", p=P)

        def gate(pool):
            pool.sem_inc(s_gate, 1)

        pairs, counted = {}, {}

        def phase(name, turns, own, shared):
            found = {}
            for key, role in [(k, name + "_" + k) for k in own.split()] + list(shared.items()):
                if role not in pairs:
                    pairs[role], counted[role] = sem2(role), 0
                found[key] = Signal(pairs[role], counted[role], turns)
                counted[role] += turns
            return found

        def same(keys):
            return {k: k for k in keys.split()}

        q1 = phase("e1", G // 2, "types_bc type_hot coef_ps low y y_read msg attr_sum attr_kept earlier rows"
                   " attr_added",
                   {"attr_in": "attr_loaded", **same("meta dst_bc dst_eq src_bc src_eq sum sum_kept gidx uidx added"),
                    "x_in": "gathered", "x_out": "rows_saved", "xT_ps": "turned_ps", "xT": "turned"})
        q2 = phase("e2", G // 2, "y z_ps z",
                   {"v": "residual_0", **same("meta dst_bc dst_eq sum sum_kept gidx uidx added"),
                    "agg_in": "gathered", "x_in": "rows_loaded", "yT_ps": "turned_ps", "yT": "turned"})
        qn = phase("n", NT // 2, "in agg1_in v1 attr_mean agT_ps agT scaled h3_ps h3_pre h3 y_ps x2b t3 x3 x4"
                   " x3_out x4_out stats scales",
                   {"x2T_ps": "turned_ps", "x2T": "turned", "h1_ps": "hidden_ps", "h1": "hidden", "z_ps": "logit_ps",
                    "attn": "attention", "v0": "residual_0", "x2": "normed", "attr_in": "attr_loaded"})
        q3 = phase("e3", G // 2, "dif att_relu att_saved hd_in",
                   {"hid_ps": "hidden_ps", "hid": "hidden", "att_ps": "logit_ps", "att": "attention", **same("meta src_bc src_eq sum sum_kept gidx gidx2 uidx added"),
                    "hs_in": "gathered", "h_out": "rows_saved", "dT_ps": "turned_ps", "dT": "turned"})
        q4 = phase("e4", G // 2, "msg",
                   {**same("meta dst_bc dst_eq sum sum_kept gidx uidx added"),
                    "den_in": "gathered", "h_in": "rows_loaded"})
        q5 = phase("e5", G // 2, "out", {"y": "normed", **same("gidx gidx2"), "x_in": "gathered"})
        c1s, c2s, c3s, c4s, c5s = (sem(f"vector_steps_e{n}") for n in (1, 2, 3, 4, 5))
        cna, pool_n = sem("vector_steps_n"), sem("pool_steps_n")
        s_kc = sem("constant_columns_set")
        s_stq = sem("stats_slots_set")
        x3_pad = sem("x3_dummies_set")

        WEIGHTS = 20

        @block.sync
        def _(sp):
            def bcast_rows(vec, n):
                return vec.rearrange("(o f) -> o f", o=1).to_broadcast([n, vec.shape[0]])

            sp.wait_ge(s_pad, 5)
            for tile, a in ((src_x, src), (src_s, src), (dst_x, dst), (dst_s, dst), (et_i, edge_type),
                            (ew_s, edge_weight)):
                sp.dma_start(tile[0:EP, :], a.rearrange("(p c) -> p c", p=EP)).then_inc(s_e, 16)
            sp.dma_start(nrm[0:EP, :], edge_weight1.rearrange("(p c) o -> p (c o)", p=EP)).then_inc(s_e, 16)
            for k in range(16):
                sp.dma_start(row0[:, k, :], bcast_rows(l0_b, P)).then_inc(s_row, 16)
            n = 0
            for o, i in ((wcat[:, :, :], l0_w.rearrange("b i o -> i b o")), (comp[:, :], l0_comp),
                         (l1w[:, :], l1_w), (w1x[:, :], w1[0:D, :]), (w1a[:, :], w1[D:D + A, :]),
                         (w2n[:, :, :], w2.rearrange("(k p) n -> p k n", p=P)),
                         (w3x[:, :], w3[0:D, :]),
                         (w3h[:, :, :], w3[D:D + H, :].rearrange("(k p) n -> p k n", p=P)),
                         (w4s[:, :, :], w4.rearrange("(k p) n -> p k n", p=P)),
                         (wac[:, :], wa.rearrange("(k p) o -> p (k o)", p=P)),
                         (b1c[:, :], b1.rearrange("(k p) -> p k", p=P)),
                         (b2c[:, :], b2.rearrange("(k p) -> p k", p=P)),
                         (b3c[:, :], b3.rearrange("(k p) -> p k", p=P)),
                         (bab[:, :], bcast_rows(ba, P)), (v1s[:, :], v1),
                         (c1c[:, :], c1.rearrange("(p o) -> p o", o=1)), (v2s[:, :], v2),
                         (c2c[:, :], bcast_rows(c2, P)), (b4b[:, 0, :], bcast_rows(b4, P)),
                         (row1[:, 0, :], bcast_rows(l1_b, P))):
                sp.dma_start(o, i, allow_slow_non_contiguous=True).then_inc(s_w, 16)
                n += 1
            assert n == WEIGHTS

            def fill(tab, tile, w, done):
                turns = NR // (16 * P)
                rest = (NR - turns * 16 * P) // 32
                view = tab[0:turns * 16 * P, :].rearrange("(t p j) f -> t p (j f)", p=P, j=16)
                with sp.Fori(0, turns) as t:
                    sp.dma_start(view[bass.ds(t, 1), :, :].rearrange("o p f -> (o p) f"), tile[:, 0:16 * w]).then_inc(done, 16)
                sp.dma_start(tab[turns * 16 * P:NR, :].rearrange("(p j) f -> p (j f)", p=32),
                             tile[0:32, 0:rest * w]).then_inc(done, 16)

            sp.wait_ge(s_row, 16 * 16)
            fill(agg0, row0[:, :, :].rearrange("p j f -> p (j f)"), D, s_fill0)
            sp.wait_ge(s_zero, 1)
            fill(attr, zeros, AW, s_filla)
            sp.dma_start(x3[N:NR, :].rearrange("(p j) f -> p (j f)", p=P), zeros[:, 0:J * D]).then_inc(x3_pad, 16)
            sp.dma_start(den.rearrange("(p j) o -> p (j o)", p=96), zeros[0:96, 0:NR // 96]).then_inc(s_filld, 16)
            sp.wait_ge(s_at, 2)
            with sp.Fori(0, G // 2) as i:
                for s in range(2):
                    tr = Turn(i, s)
                    tr.again(sp, q1["attr_sum"])
                    sp.dma_start(at[0:EP, s, :, 0:A], edge_rows(edge_attr, tr.t)).then_inc(q1["attr_in"][s], 16)
                for s in range(2):
                    tr = Turn(i, s)
                    tr.now(sp, q1["x_in"], 64)
                    sp.dma_start(xsrc[bass.ds(tr.t, 1), :, :].rearrange("o p f -> (o p) f"), fa[:, s, :, :].rearrange("p j f -> p (j f)")).then_inc(q1["x_out"][s], 16)
            sp.wait_ge(s_dup, 1)
            fill(agg1, row1[:, :, :].rearrange("p j f -> p (j f)"), D, s_fill1)
            q1["x_out"].all(sp, 16)
            with sp.Fori(0, G // 2) as i:
                for s in range(2):
                    tr = Turn(i, s)
                    tr.again(sp, q2["v"])
                    sp.dma_start(fa[:, s, :, :].rearrange("p j f -> p (j f)"), xsrc[bass.ds(tr.t, 1), :, :].rearrange("o p f -> (o p) f")).then_inc(q2["x_in"][s], 16)

            q1["added"].all(sp, 64)
            q1["attr_added"].all(sp, 64)
            q2["added"].all(sp, 64)
            q2["sum_kept"].all(sp)
            q1["attr_sum"].all(sp)

            def flat(tile, s):
                return tile[:, s, :, :].rearrange("p j f -> p (j f)")

            def node_io(st):
                tr = st.tile(4)
                if tr:
                    tr.again(sp, qn["v0"])
                    sp.dma_start(flat(fa, tr.s), node_rows(x, tr.start)).then_inc(qn["in"][tr.s], 16)
                    sp.dma_start(flat(fb, tr.s), node_rows(agg0, tr.start)).then_inc(qn["in"][tr.s], 16)
                tr = st.tile(3)
                if tr:
                    tr.again(sp, qn["v1"])
                    sp.dma_start(flat(fc, tr.s), node_rows(agg1, tr.start)).then_inc(qn["agg1_in"][tr.s], 16)
                tr = st.tile(2)
                if tr:
                    tr.again(sp, qn["attr_mean"])
                    sp.dma_start(flat(at, tr.s), node_rows(attr, tr.start)).then_inc(qn["attr_in"][tr.s], 16)
                tr = st.tile(-3)
                if tr:
                    if st.n - 3 == NT - 1 and st.i is None:
                        tr.before(sp, qn["x3_out"], 16)
                        tr.before(sp, qn["x4_out"], 16)
                    tr.now(sp, qn["x3"])
                    sp.dma_start(node_rows(x3, tr.start), flat(fe, tr.s)).then_inc(qn["x3_out"][tr.s], 16)
                    tr.now(sp, qn["x4"])
                    sp.dma_start(node_rows(out, tr.start), flat(ff, tr.s)).then_inc(qn["x4_out"][tr.s], 16)

            node_steps(sp, node_io)

            with sp.Fori(0, G // 2) as i:
                for s in range(2):
                    tr = Turn(i, s)
                    tr.now(sp, q3["hs_in"], 64)
                    sp.dma_start(hsrc[bass.ds(tr.t, 1), :, :].rearrange("o p f -> (o p) f"), fa[:, s, :, :].rearrange("p j f -> p (j f)")).then_inc(q3["h_out"][s], 16)
            q3["h_out"].all(sp, 16)
            q3["dif"].all(sp)
            with sp.Fori(0, G // 2) as i:
                for s in range(2):
                    tr = Turn(i, s)
                    tr.again(sp, q4["msg"])
                    sp.dma_start(fa[:, s, :, :].rearrange("p j f -> p (j f)"), hsrc[bass.ds(tr.t, 1), :, :].rearrange("o p f -> (o p) f")).then_inc(q4["h_in"][s], 16)
            qn["x4_out"].all(sp, 16)
            q5["out"].all(sp, 64)

        @block.gpsimd
        def _(pool):
            nc.gpsimd.memset(ident[:], 0.0).then_inc(s_pset, 1)
            nc.gpsimd.memset(lower[:], 1.0).then_inc(s_pset, 1)
            nc.gpsimd.iota(src_s[:], pattern=[[0, C]], base=N, channel_multiplier=J).then_inc(s_pad, 1)
            nc.gpsimd.iota(dst_s[:], pattern=[[0, C]], base=N, channel_multiplier=J).then_inc(s_pad, 1)
            nc.gpsimd.iota(part_i[:], pattern=[[0, 1]], base=0, channel_multiplier=1).then_inc(s_const, 1)
            nc.gpsimd.iota(dummy_i[:], pattern=[[1, J], [0, 2]], base=N, channel_multiplier=J).then_inc(s_const, 1)
            pool.wait_ge(s_pset, 2)
            nc.gpsimd.affine_select(out=ident[:], in_=ident[:], compare_op=ALU.not_equal, fill=1.0, base=0,
                                    pattern=[[-1, P]], channel_multiplier=1).then_inc(s_const, 1)
            nc.gpsimd.affine_select(out=lower[:], in_=lower[:], compare_op=ALU.is_gt, fill=0.0, base=0,
                                    pattern=[[1, P]], channel_multiplier=-1).then_inc(s_const, 1)
            pool.wait_ge(s_e, 16 * 7)

            def index(tr, q, key, slot, source):
                nc.gpsimd.tensor_copy(slot, source).then_inc(q[key][tr.s], 1)
                tr.now(pool, q[key])
                gate(pool)

            def gather(tab, idx, tiles, done):
                for j in range(J):
                    nc.gpsimd.indirect_dma_start(tiles[j], None, tab, bass.IndirectOffsetOnAxis(idx[:, j:j + 1], 0)).then_inc(done, 16)

            def add(tab, idx, tiles, done):
                for j in range(J):
                    nc.gpsimd.indirect_dma_start(tab, bass.IndirectOffsetOnAxis(idx[j], 0), tiles[j], None, compute_op=ALU.add).then_inc(done, 16)

            def rows4(tile, s):
                return [tile[:, s, j, :] for j in range(J)]

            def skewed(first, second):
                first(Turn(0, 0))
                with pool.Fori(0, G // 2 - 1) as i:
                    first(Turn(i, 1))
                    second(Turn(i, 0))
                    first(Turn(i + 1, 0))
                    second(Turn(i, 1))
                first(Turn(G // 2 - 1, 1))
                second(Turn(G // 2 - 1, 0))
                second(Turn(G // 2 - 1, 1))

            def x_rows(tr):
                tr.again(pool, q1["xT_ps"])
                tr.again(pool, q1["x_out"], 16)
                tr.again(pool, q1["x_in"], 64)
                gate(pool)
                index(tr, q1, "gidx", gi[:, tr.s, :], src_x[:, bass.ds(tr.t * J, J)])
                gather(x, gi[:, tr.s, :], rows4(fa, tr.s), q1["x_in"][tr.s])

            def add_sums(tr):
                tr.now(pool, q1["rows"])
                tr.before(pool, q1["added"], 64)
                tr.before(pool, q1["attr_added"], 64)
                gate(pool)
                index(tr, q1, "uidx", ui[:, tr.s, :, :], uniq[:, bass.ds(tr.t * J, J), :])
                tr.now(pool, q1["attr_kept"])
                gate(pool)
                add(attr, [ui[:, tr.s, j, 0:1] for j in range(J)], rows4(ag, tr.s), q1["attr_added"][tr.s])
                tr.now(pool, q1["sum_kept"])
                gate(pool)
                add(agg0, [ui[:, tr.s, j, 1:2] for j in range(J)], rows4(fd, tr.s), q1["added"][tr.s])

            turns = NR // (16 * P) + 1
            x_rows(Turn(0, 0))
            pool.wait_ge(s_fill0, 16 * turns)
            pool.wait_ge(s_filla, 16 * turns)
            with pool.Fori(0, G // 2 - 1) as i:
                x_rows(Turn(i, 1))
                add_sums(Turn(i, 0))
                x_rows(Turn(i + 1, 0))
                add_sums(Turn(i, 1))
            x_rows(Turn(G // 2 - 1, 1))
            add_sums(Turn(G // 2 - 1, 0))
            add_sums(Turn(G // 2 - 1, 1))

            q1["added"].all(pool, 64)
            q1["attr_added"].all(pool, 64)
            pool.wait_ge(s_fill1, 16 * turns)
            gate(pool)

            def agg_rows(tr):
                tr.again(pool, q2["v"])
                tr.again(pool, q2["agg_in"], 64)
                gate(pool)
                index(tr, q2, "gidx", gi[:, tr.s, :], src_x[:, bass.ds(tr.t * J, J)])
                gather(agg0, gi[:, tr.s, :], rows4(fb, tr.s), q2["agg_in"][tr.s])

            def add_layer1(tr):
                tr.before(pool, q2["added"], 64)
                gate(pool)
                index(tr, q2, "uidx", ui[:, tr.s, :, 1:2], uniq[:, bass.ds(tr.t * J, J), 1:2])
                tr.now(pool, q2["sum_kept"])
                gate(pool)
                add(agg1, [ui[:, tr.s, j, 1:2] for j in range(J)], rows4(fd, tr.s), q2["added"][tr.s])

            skewed(agg_rows, add_layer1)

            pool.wait_ge(s_dup, 1)
            for k, value in enumerate(CONSTANTS):
                nc.gpsimd.memset(kc[:, k:k + 1], value).then_inc(s_kc, 1)
            pool.wait_ge(s_kc, len(CONSTANTS))
            q2["added"].all(pool, 64)

            def batch(st, idx):
                idx.now(pool, qn["stats"])
                if st.tile(-4):
                    st.tile(-4).now(pool, qn["x4"])
                g = nc.gpsimd
                sp_ = Steps(pool, pool_n, idx, POOL_STEPS)
                raw, mean, y, bias = stq[:, idx.s], nmean[:, idx.s], nry[:, idx.s], nbias[:, idx.s]
                sp_.done(g.tensor_tensor(pa[:], raw[:, :, :, 1], raw[:, :, :, 4], ALU.add))
                sp_.done(g.tensor_tensor(pb[:], raw[:, :, :, 1], raw[:, :, :, 4], ALU.subtract))
                sp_.step(g.tensor_tensor(pc[:], raw[:, :, :, 2], raw[:, :, :, 5], ALU.add))
                sp_.done(g.tensor_tensor(mean, pa[:], const(HALF, 3), ALU.mult))
                sp_.done(g.tensor_tensor(pnm[:], pa[:, 2, :], const(MINUS_HALF), ALU.mult))
                sp_.done(g.tensor_tensor(pb[:], pb[:], const(HALF, 3), ALU.mult))
                sp_.step(g.tensor_tensor(pc[:], pc[:], const(PER_ROW, 3), ALU.mult))
                sp_.step(g.tensor_tensor(pd[:], pb[:], pb[:], ALU.mult))
                sp_.step(g.tensor_tensor(pc[:], pc[:], pd[:], ALU.add))
                sp_.step(g.tensor_tensor(pv[:, 0:3, :], pc[:], const(NORM_EPS, 3), ALU.add))
                sp_.step(g.tensor_tensor(pv[:, 3, :], pv[:, 2, :], const(NORM_EPS), ALU.mult))
                sp_.step(g.tensor_tensor(pv[:, 3, :], pv[:, 3, :], pc[:, 2, :], ALU.add))
                gate(pool)
                sp_.step(g.tensor_scalar(y.bitcast(I32), pv[:].bitcast(I32), -0.5, MAGIC, ALU.mult, ALU.add))
                sp_.done(g.tensor_tensor(pv[:], pv[:], const(HALF, 4), ALU.mult))
                for k in range(3):
                    sp_.step(g.tensor_tensor(pe_[:], y, y, ALU.mult))
                    sp_.step(g.tensor_tensor(pe_[:], pe_[:], pv[:], ALU.mult))
                    sp_.step(g.tensor_tensor(pe_[:], const(THREE_HALVES, 4), pe_[:], ALU.subtract))
                    sp_.step(g.tensor_tensor(y, y, pe_[:], ALU.mult))
                sp_.done(g.tensor_tensor(bias[:, 0, :], pnm[:], y[:, 2, :], ALU.mult))
                sp_.close()
                g.tensor_tensor(bias[:, 1, :], pnm[:], y[:, 3, :], ALU.mult).then_inc(qn["scales"][idx.s], 1)

            POOL_STEPS = 27

            def const(k, rows=None):
                if rows is None:
                    return kc[:, k:k + 1].to_broadcast([P, J])
                return kc[:, k:k + 1].rearrange("p (o j) -> p o j", o=1).to_broadcast([P, rows, J])

            def node_pool(st):
                if st.tile(3) or st.tile(2) or st.tile(-2):
                    batch(st, st.turn(3))
                tr = st.tile(0)
                if tr:
                    tr.now(pool, qn["x2"])
                    tr.again(pool, qn["t3"])
                    nc.gpsimd.tensor_tensor(fd[:, tr.s, :, :], x2s[:, tr.s, :, :], b4b[:, :, :], ALU.add).then_inc(qn["x2b"][tr.s], 1)

            node_steps(pool, node_pool)

            qn["x3_out"].all(pool, 16)
            qn["t3"].all(pool)
            pool.wait_ge(x3_pad, 16)
            pool.wait_ge(s_filld, 16)

            def h_rows(tr):
                tr.again(pool, q3["dif"])
                tr.again(pool, q3["h_out"], 16)
                tr.again(pool, q3["hs_in"], 64)
                tr.again(pool, q3["hd_in"], 64)
                gate(pool)
                nc.gpsimd.tensor_copy(gi[:, tr.s, :], src_x[:, bass.ds(tr.t * J, J)]).then_inc(q3["gidx"][tr.s], 1)
                nc.gpsimd.tensor_copy(gi2[:, tr.s, :], dst_x[:, bass.ds(tr.t * J, J)]).then_inc(q3["gidx2"][tr.s], 1)
                tr.now(pool, q3["gidx"])
                tr.now(pool, q3["gidx2"])
                gate(pool)
                gather(x3, gi[:, tr.s, :], rows4(fa, tr.s), q3["hs_in"][tr.s])
                gather(x3, gi2[:, tr.s, :], rows4(fb, tr.s), q3["hd_in"][tr.s])

            def add_den(tr):
                tr.before(pool, q3["added"], 64)
                gate(pool)
                index(tr, q3, "uidx", ui[:, tr.s, :, 0:1], uniq[:, bass.ds(tr.t * J, J), 0:1])
                tr.now(pool, q3["sum_kept"])
                gate(pool)
                add(den, [ui[:, tr.s, j, 0:1] for j in range(J)], [sm2[:, tr.s, j:j + 1] for j in range(J)], q3["added"][tr.s])

            skewed(h_rows, add_den)

            q3["added"].all(pool, 64)
            q3["hs_in"].all(pool, 64)
            q3["hd_in"].all(pool, 64)
            q3["sum"].all(pool)
            q3["att_saved"].all(pool)
            gate(pool)

            def den_rows(tr):
                tr.again(pool, q4["msg"])
                tr.again(pool, q4["den_in"], 64)
                gate(pool)
                index(tr, q4, "gidx", gi[:, tr.s, :], src_s[:, bass.ds(tr.t * J, J)])
                gather(den, gi[:, tr.s, :], [sm[:, tr.s, j:j + 1] for j in range(J)], q4["den_in"][tr.s])

            def add_layer3(tr):
                tr.before(pool, q4["added"], 64)
                gate(pool)
                index(tr, q4, "uidx", ui[:, tr.s, :, 1:2], uniq[:, bass.ds(tr.t * J, J), 1:2])
                tr.now(pool, q4["sum_kept"])
                gate(pool)
                add(x3, [ui[:, tr.s, j, 1:2] for j in range(J)], rows4(fd, tr.s), q4["added"][tr.s])

            skewed(den_rows, add_layer3)

            q4["added"].all(pool, 64)
            q4["sum"].all(pool)
            qn["x4_out"].all(pool, 16)
            gate(pool)

            def sum_rows(tr):
                tr.again(pool, q5["y"])
                tr.again(pool, q5["out"], 64)
                gate(pool)
                nc.gpsimd.tensor_copy(gi[:, tr.s, :], dst_x[:, bass.ds(tr.t * J, J)]).then_inc(q5["gidx"][tr.s], 1)
                nc.gpsimd.tensor_copy(gi2[:, tr.s, :], uniq[:, bass.ds(tr.t * J, J), 1:2].rearrange("p j o -> p (j o)")).then_inc(q5["gidx2"][tr.s], 1)
                tr.now(pool, q5["gidx"])
                tr.now(pool, q5["gidx2"])
                gate(pool)
                gather(x3, gi[:, tr.s, :], rows4(fa, tr.s), q5["x_in"][tr.s])

            def put_rows(tr):
                tr.now(pool, q5["y"])
                tr.before(pool, q5["out"], 64)
                gate(pool)
                for j in range(J):
                    nc.gpsimd.indirect_dma_start(out, bass.IndirectOffsetOnAxis(gi2[:, tr.s, j:j + 1], 0), fd[:, tr.s, j, :],
                                                 None, bounds_check=N - 1, oob_is_err=False).then_inc(q5["out"][tr.s], 16)

            skewed(sum_rows, put_rows)

        @block.vector
        def _(dve):
            nc.vector.memset(zeros[:], 0.0).then_inc(s_zero, 1)
            nc.vector.memset(src_x[:], 0)
            nc.vector.memset(dst_x[:], 0)
            nc.vector.memset(et_i[:], 0).then_inc(s_pad, 1)
            nc.vector.memset(ew_s[:], 0.0).then_inc(s_pad, 1)
            nc.vector.memset(nrm[:], 0.0).then_inc(s_pad, 1)
            nc.vector.memset(ones[:], 1.0)
            nc.vector.memset(at[:], 0.0).then_inc(s_at, 1)
            dve.wait_ge(s_at, 1)
            nc.vector.memset(at[0:EP, :, :, A:AW], 1.0).then_inc(s_at, 1)
            dve.wait_ge(s_const, 4)
            nc.vector.tensor_copy(part[:], part_i[:])
            nc.vector.tensor_copy(dummy[:], dummy_i[:])
            dve.wait_ge(s_e, 16 * 7)
            for k, tile in ((SRC, src_s), (DST, dst_s), (ETYPE, et_i), (NORM, nrm), (EW, ew_s)):
                nc.vector.tensor_copy(meta[:, :, k:k + 1], tile[:].rearrange("p (c o) -> p c o", o=1)).then_inc(s_meta, 1)
            dve.wait_ge(s_meta, 5)

            def norm_scale(stp, width):
                a, b, v, y = (t[:, 0:width] for t in (na, nb_, nv, ny))
                stp.step(nc.vector.tensor_scalar(y.bitcast(I32), v.bitcast(I32), -0.5, MAGIC, ALU.mult, ALU.add))
                for _ in range(3):
                    stp.step(nc.vector.scalar_tensor_tensor(a, y, -0.5, y, ALU.mult, ALU.mult))
                    stp.step(nc.vector.tensor_tensor(b, a, v, ALU.mult))
                    stp.step(nc.vector.scalar_tensor_tensor(y, b, 1.5, y, ALU.add, ALU.mult))

            NORM_STEPS = 10

            def stats(stp, v):
                for j in range(J):
                    stp.done(nc.vector.bn_stats(st[:, j, :], v[:, j, :]))
                stp.wait()
                stp.done(nc.vector.tensor_tensor(h_sum[:], st[:, :, 1], st[:, :, 4], ALU.add))
                stp.done(nc.vector.tensor_tensor(h_dif[:], st[:, :, 1], st[:, :, 4], ALU.subtract))
                stp.done(nc.vector.tensor_tensor(h_sq[:], st[:, :, 2], st[:, :, 5], ALU.add))
                stp.wait()
                stp.done(nc.vector.tensor_scalar(mv[:, :, 0], h_sum[:], 0.5, None, ALU.mult))
                stp.step(nc.vector.scalar_tensor_tensor(h_dif[:], h_dif[:], 0.25, h_dif[:], ALU.mult, ALU.mult))
                stp.step(nc.vector.scalar_tensor_tensor(mv[:, :, 1], h_sq[:], 1.0 / D, h_dif[:], ALU.mult, ALU.add))

            STATS_STEPS = J + 6

            def equal(tr, bank, field, out4, done):
                for k in range(J):
                    last = nc.vector.tensor_scalar(out4[:, k, :], bank, m[:, tr.s, k, field:field + 1], None, ALU.is_equal)
                last.then_inc(done, 1)

            def meta_slot(tr, q):
                nc.vector.tensor_scalar(m[:, tr.s, :, :], meta[:, bass.ds(tr.t * J, J), :], 0.0, None,
                                        ALU.add).then_inc(q["meta"][tr.s], 1)
                tr.now(dve, q["meta"])

            def low(eq, out4):
                for j in range(J):
                    last = nc.vector.tensor_tensor(out4[:, j, :], eq[:, j, j * P:(j + 1) * P], lower[:], ALU.mult)
                return last

            def message(tr, stp, j):
                y = yAB[j % 2]
                dve.wait_ge(q1["y"][tr.s], tr.i * J + (j + 1))
                if j < 2:
                    tr.before(dve, q1["msg"], J)
                else:
                    dve.wait_ge(q1["msg"][tr.s], tr.i * J + (j - 1))
                ins = nc.vector.tensor_tensor(prod[:, j % 2, :, :], y[:].rearrange("p (b f) -> p b f", b=NB),
                                              cf[:, j, :].rearrange("p (b o) -> p b o", o=1).to_broadcast([P, NB, D]), ALU.mult)
                ins.then_inc(q1["y_read"][tr.s], 1)
                dve.wait_ge(q1["y_read"][tr.s], tr.i * J + (j + 1))
                nc.vector.tensor_reduce(fc[:, tr.s, j, :], prod[:, j % 2, :, :].rearrange("p b f -> p f b"), AX.X, ALU.add).then_inc(q1["msg"][tr.s], 1)

            with dve.Fori(0, G // 2) as i:
                for s in range(2):
                    tr = Turn(i, s)
                    stp = Steps(dve, c1s, tr, 2)
                    tr.again(dve, q1["sum"])
                    tr.again(dve, q1["rows"])
                    meta_slot(tr, q1)
                    nc.vector.tensor_tensor(dd[:], dummy[:], m[:, s, :, 0:2], ALU.subtract)
                    tr.now(dve, q1["types_bc"])
                    nc.vector.tensor_scalar(ot[:], bk[0][0:R, :], part[0:R, :], None, ALU.is_equal).then_inc(q1["type_hot"][s], 1)
                    tr.now(dve, q1["dst_bc"])
                    equal(tr, bk[1][:], DST, big0[:, 0, :, :], q1["dst_eq"][s])
                    tr.now(dve, q1["coef_ps"])
                    stp.done(nc.vector.tensor_tensor(cf[:], bk[0][:, 0:J * NB].rearrange("p (j b) -> p j b", b=NB),
                                                     m[:, s, :, NORM:NORM + 1].to_broadcast([P, J, NB]), ALU.mult))
                    tr.now(dve, q1["dst_eq"])
                    low(big0[:, 0, :, :], sl[:, 1, :, :])
                    stp.wait()
                    message(tr, stp, 0)
                    tr.now(dve, q1["src_bc"])
                    equal(tr, bk[1][:], SRC, big1[:, :, :], q1["src_eq"][s])
                    tr.now(dve, q1["src_eq"])
                    low(big1[:, :, :], sl[:, 0, :, :]).then_inc(q1["low"][s], 1)
                    for j in range(1, J):
                        message(tr, stp, j)
                    tr.now(dve, q1["earlier"])
                    stp.step(nc.vector.scalar_tensor_tensor(nf[:], bk[0][:, 64:64 + 2 * J].rearrange("p (j v) -> p j v", v=2),
                                                            1.0, dd[:], ALU.min, ALU.mult))
                    nc.vector.tensor_tensor(uniq[:, bass.ds(tr.t * J, J), :], nf[:], m[:, s, :, 0:2], ALU.add).then_inc(q1["rows"][s], 1)
                    stp.close()
            dve.wait_ge(s_w, 16 * WEIGHTS)
            for k in range(1, J):
                nc.vector.tensor_copy(b4b[:, k, :], b4b[:, 0, :])
            for k in range(1, 16):
                last = nc.vector.tensor_copy(row1[:, k, :], row1[:, 0, :])
            last.then_inc(s_dup, 1)

            S2 = STATS_STEPS + 1 + NORM_STEPS + 2
            with dve.Fori(0, G // 2) as i:
                for s in range(2):
                    tr = Turn(i, s)
                    stp = Steps(dve, c2s, tr, S2)
                    tr.again(dve, q2["sum"])
                    meta_slot(tr, q2)
                    tr.now(dve, q2["x_in"], 16)
                    tr.now(dve, q2["agg_in"], 64)
                    tr.again(dve, q2["y"])
                    nc.vector.scalar_tensor_tensor(fe[:, s, :, :], fb[:, s, :, :], 0.0, fa[:, s, :, :], ALU.max, ALU.add).then_inc(q2["v"][s], 1)
                    tr.now(dve, q2["v"])
                    stats(stp, fe[:, s, :, :])
                    stp.step(nc.vector.tensor_scalar(nv[:, 0:J], mv[:, :, 1], EPS, None, ALU.add))
                    norm_scale(stp, J)
                    stp.step(nc.vector.tensor_tensor(rc[:], ny[:, 0:J], m[:, s, :, EW], ALU.mult))
                    stp.step(nc.vector.tensor_tensor(na[:, 0:J], mv[:, :, 0], rc[:], ALU.mult))
                    stp.close()
                    tr.again(dve, q2["yT_ps"])
                    for j in range(J):
                        last = nc.vector.tensor_scalar(fc[:, s, j, :], fe[:, s, j, :], rc[:, j:j + 1], na[:, j:j + 1], ALU.mult, ALU.subtract)
                    last.then_inc(q2["y"][s], 1)
                    tr.now(dve, q2["dst_bc"])
                    equal(tr, bk[1][:], DST, big0[:, 0, :, :], q2["dst_eq"][s])

            def stat(v, place):
                for j in range(J):
                    last = nc.vector.bn_stats(place[:, j, :], v[:, j, :])
                return last

            def node_vector(st):
                idx = st.turn(3)
                made = None
                if st.tile(3) or st.tile(2) or st.tile(-2):
                    idx.again(dve, qn["scales"])
                tr = st.tile(-1)
                if tr:
                    tr.now(dve, qn["attn"])
                    tr.again(dve, qn["h3_ps"], 2)
                    for k in range(2):
                        last = nc.vector.tensor_tensor(rr[:, tr.s, 2 + k, :], rr[:, tr.s, k, :], att_b[:, tr.s, :], ALU.mult)
                    last.then_inc(qn["scaled"][tr.s], 1)
                tr = st.tile(-2)
                if tr:
                    tr.now(dve, qn["y_ps"])
                    tr.now(dve, qn["x2b"])
                    tr.again(dve, qn["x4"])
                    nc.vector.tensor_tensor(t3[:, tr.s, :, :], bk[3][:].rearrange("p (j f) -> p j f", j=J), fd[:, tr.s, :, :],
                                            ALU.add).then_inc(qn["t3"][tr.s], 1)
                    tr.now(dve, qn["t3"])
                    made = stat(t3[:, tr.s], stq[:, idx.s, 2])
                tr = st.tile(3)
                if tr:
                    tr.now(dve, qn["in"], 32)
                    tr.again(dve, qn["v1"])
                    nc.vector.scalar_tensor_tensor(va[:, tr.s, :, :], fb[:, tr.s, :, :], 0.0, fa[:, tr.s, :, :], ALU.max, ALU.add).then_inc(qn["v0"][tr.s], 1)
                    tr.now(dve, qn["v0"])
                    made = stat(va[:, tr.s], stq[:, idx.s, 0])
                before = st.turn(2)
                tr = st.tile(2)
                if tr:
                    tr.now(dve, qn["agg1_in"], 16)
                    before.now(dve, qn["scales"])
                    tr.again(dve, qn["x2"])
                    for j in range(J):
                        last = nc.vector.scalar_tensor_tensor(vb[:, tr.s, j, :], va[:, tr.s, j, :], nry[:, before.s, 0, j:j + 1],
                                                              fc[:, tr.s, j, :], ALU.mult, ALU.add)
                    last.then_inc(qn["v1"][tr.s], 1)
                    tr.now(dve, qn["v1"])
                    made = stat(vb[:, tr.s], stq[:, idx.s, 1])
                if made is not None:
                    made.then_inc(qn["stats"][idx.s], 1)
                tr = st.tile(1)
                if tr:
                    before.now(dve, qn["scales"])
                    tr.again(dve, qn["x2T_ps"])
                    tr.again(dve, qn["x2b"])
                    for j in range(J):
                        last = nc.vector.tensor_scalar(x2s[:, tr.s, j, :], vb[:, tr.s, j, :], nmean[:, before.s, 1, j:j + 1],
                                                       nry[:, before.s, 1, j:j + 1], ALU.subtract, ALU.mult)
                    last.then_inc(qn["x2"][tr.s], 1)
                    tr.now(dve, qn["attr_in"], 16)
                    stp = Steps(dve, cna, tr, 2)
                    stp.step(nc.vector.tensor_scalar(rc[:], at[:, tr.s, :, A], 1.0, None, ALU.max))
                    stp.step(nc.vector.reciprocal(rc[:], rc[:]))
                    tr.again(dve, qn["agT_ps"])
                    nc.vector.tensor_tensor(ag[:, tr.s, :, 0:A], at[:, tr.s, :, 0:A], rc[:].rearrange("p (j o) -> p j o", o=1).to_broadcast([P, J, A]),
                                            ALU.mult).then_inc(qn["attr_mean"][tr.s], 1)
                    tr.now(dve, qn["attr_mean"])
                tr = st.tile(-1)
                if tr:
                    tr.before(dve, qn["h3"])
                    for k in range(2):
                        tr.part(dve, qn["h3_ps"], 2, k + 1)
                        nc.vector.scalar_tensor_tensor(h3[:, 2 + k, :], att_b[:, tr.s, :], c23[:, k:k + 1], yB[:, k * T:(k + 1) * T],
                                                       ALU.mult, ALU.add).then_inc(qn["h3_pre"][tr.s], 1)

            dve.wait_ge(s_wpk, 1)
            nc.vector.memset(stq[:], 1.0).then_inc(s_stq, 1)
            dve.wait_ge(s_stq, 1)
            node_steps(dve, node_vector)

            with dve.Fori(0, G // 2) as i:
                for s in range(2):
                    tr = Turn(i, s)
                    tr.again(dve, q3["sum"])
                    meta_slot(tr, q3)
                    tr.now(dve, q3["hs_in"], 64)
                    tr.now(dve, q3["hd_in"], 64)
                    tr.again(dve, q3["dT_ps"])
                    nc.vector.tensor_tensor(fc[:, s, :, :], fa[:, s, :, :], fb[:, s, :, :], ALU.subtract).then_inc(q3["dif"][s], 1)
                    tr.now(dve, q3["src_bc"])
                    equal(tr, bk[1][:], SRC, big0[:, 0, :, :], q3["src_eq"][s])
                    tr.now(dve, q3["att"])
                    nc.vector.tensor_scalar(att_all[:, bass.ds(tr.t * J, J)], sm[:, s, :], 0.0, None, ALU.add).then_inc(q3["att_saved"][s], 1)

            q3["att_saved"].all(dve)
            with dve.Fori(0, G // 2) as i:
                for s in range(2):
                    tr = Turn(i, s)
                    stp = Steps(dve, c4s, tr, 2)
                    tr.again(dve, q4["sum"])
                    meta_slot(tr, q4)
                    tr.now(dve, q4["h_in"], 16)
                    tr.now(dve, q4["den_in"], 64)
                    stp.step(nc.vector.reciprocal(rc[:], sm[:, s, :]))
                    stp.step(nc.vector.tensor_tensor(rc[:], rc[:], att_all[:, bass.ds(tr.t * J, J)], ALU.mult))
                    stp.close()
                    nc.vector.tensor_tensor(fc[:, s, :, :], fa[:, s, :, :], rc[:].rearrange("p (j o) -> p j o", o=1).to_broadcast([P, J, D]), ALU.mult).then_inc(q4["msg"][s], 1)
                    tr.now(dve, q4["dst_bc"])
                    equal(tr, bk[1][:], DST, big0[:, 0, :, :], q4["dst_eq"][s])

            S5 = STATS_STEPS + 1 + NORM_STEPS
            with dve.Fori(0, G // 2) as i:
                for s in range(2):
                    tr = Turn(i, s)
                    stp = Steps(dve, c5s, tr, S5)
                    tr.now(dve, q5["x_in"], 64)
                    v = fa[:, s, :, :]
                    stats(stp, v)
                    stp.step(nc.vector.tensor_scalar(nv[:, 0:J], mv[:, :, 1], EPS, None, ALU.add))
                    norm_scale(stp, J)
                    stp.close()
                    tr.again(dve, q5["out"], 64)
                    for j in range(J):
                        last = nc.vector.tensor_scalar(fd[:, s, j, :], v[:, j, :], mv[:, j, 0:1], ny[:, j:j + 1], ALU.subtract, ALU.mult)
                    last.then_inc(q5["y"][s], 1)

        @block.scalar
        def _(act):
            act.wait_ge(s_w, 16 * WEIGHTS)
            nc.scalar.activation(wab[:, 0, :], zeros[:, 0:P], ACT.Identity, bias=wac[:, 0:1])
            nc.scalar.activation(wab[:, 1, :], zeros[:, 0:P], ACT.Identity, bias=wac[:, 1:2])
            nc.scalar.activation(b2b[:, 0, :], zeros[:, 0:P], ACT.Identity, bias=b2c[:, 0:1])
            nc.scalar.activation(b2b[:, 1, :], zeros[:, 0:P], ACT.Identity, bias=b2c[:, 1:2])
            act.wait_ge(s_wt, 1)
            nc.scalar.copy(w2T[:, 0, :], bk[0][:, 0:H])
            nc.scalar.copy(w2T[:, 1, :], bk[0][:, H:2 * H])
            nc.scalar.copy(l1wT[:], bk[1][:, 0:D]).then_inc(s_wte, 1)
            act.wait_ge(s_wp, 1)
            nc.scalar.copy(w23[:, 0, :], bk[2][:, 0:H])
            nc.scalar.copy(w23[:, 1, :], bk[2][:, H:2 * H])
            nc.scalar.copy(w2a[:, 0, :], bk[3][:, 0:P])
            nc.scalar.copy(w2a[:, 1, :], bk[3][:, P:2 * P])
            nc.scalar.copy(c23[:], bk[3][:, 2 * P:2 * P + 2])
            nc.scalar.activation(zb[:], bk[3][:, 2 * P + 2:2 * P + 3], ACT.Identity, bias=bab[:]).then_inc(s_wpk, 1)

            with act.Fori(0, G // 2) as i:
                for s in range(2):
                    tr = Turn(i, s)
                    tr.now(act, q1["xT_ps"])
                    tr.again(act, q1["y"], J)
                    nc.scalar.copy(x2T[:, s, :], bk[1][:]).then_inc(q1["xT"][s], 1)
                    tr.now(act, q1["attr_sum"])
                    tr.again(act, q1["attr_added"], 64)
                    nc.scalar.copy(ag[:, s, :, :].rearrange("p j f -> p (j f)"), bk[3][:, 0:J * AW]).then_inc(q1["attr_kept"][s], 1)
                    tr.now(act, q1["sum"])
                    tr.again(act, q1["added"], 64)
                    nc.scalar.copy(fd[:, s, :, :].rearrange("p j f -> p (j f)"), bk[2][:]).then_inc(q1["sum_kept"][s], 1)
            q1["added"].all(act, 64)
            with act.Fori(0, G // 2) as i:
                for s in range(2):
                    tr = Turn(i, s)
                    tr.now(act, q2["yT_ps"])
                    tr.again(act, q2["z_ps"])
                    nc.scalar.copy(x2T[:, s, :], bk[0][:]).then_inc(q2["yT"][s], 1)
                    tr.now(act, q2["z_ps"])
                    tr.again(act, q2["sum"])
                    nc.scalar.copy(ff[:, s, :, :].rearrange("p j f -> p (j f)"), bk[3][:]).then_inc(q2["z"][s], 1)
                    tr.now(act, q2["sum"])
                    tr.again(act, q2["added"], 64)
                    nc.scalar.copy(fd[:, s, :, :].rearrange("p j f -> p (j f)"), bk[2][:]).then_inc(q2["sum_kept"][s], 1)
            q2["sum"].all(act)

            def node_scalar(st):
                before = st.turn(2)
                tr = st.tile(-3)
                if tr:
                    before.now(act, qn["scales"])
                    for v, (tile, key) in enumerate(((fe, "x3"), (ff, "x4"))):
                        tr.again(act, qn[key + "_out"], 16)
                        for j in range(J):
                            last = nc.scalar.activation(tile[:, tr.s, j, :], t3[:, tr.s, j, :], ACT.Identity,
                                                        bias=nbias[:, before.s, v, j:j + 1], scale=nry[:, before.s, 2 + v, j:j + 1])
                        last.then_inc(qn[key][tr.s], 1)
                tr = st.tile(0)
                if tr:
                    tr.now(act, qn["h1_ps"])
                    tr.again(act, qn["scaled"])
                    for k in range(2):
                        last = nc.scalar.activation(rr[:, tr.s, k, :], yA[:, k * T:(k + 1) * T], ACT.Relu, bias=b1c[:, k:k + 1])
                    last.then_inc(qn["h1"][tr.s], 1)
                tr = st.tile(-1)
                if tr:
                    tr.before(act, qn["y_ps"])
                    for k in range(2):
                        tr.part(act, qn["h3_pre"], 2, k + 1)
                        last = nc.scalar.activation(h3[:, k, :], h3[:, 2 + k, :], ACT.Relu, bias=b3c[:, k:k + 1])
                    last.then_inc(qn["h3"][tr.s], 1)
                tr = st.tile(1)
                if tr:
                    tr.now(act, qn["x2T_ps"])
                    tr.again(act, qn["h3_ps"], 2)
                    nc.scalar.copy(x2T[:, tr.s, :], bk[0][:]).then_inc(qn["x2T"][tr.s], 1)
                    tr.now(act, qn["agT_ps"])
                    tr.again(act, qn["h1_ps"])
                    nc.scalar.copy(agT[:, tr.s, :], bk[1][0:A, :]).then_inc(qn["agT"][tr.s], 1)
                tr = st.tile(0)
                if tr:
                    tr.now(act, qn["z_ps"])
                    tr.again(act, qn["h3_pre"], 2)
                    nc.scalar.activation(att_b[:, tr.s, :], bk[2][:], ACT.Sigmoid, bias=zb[:]).then_inc(qn["attn"][tr.s], 1)

            node_steps(act, node_scalar)

            with act.Fori(0, G // 2) as i:
                for s in range(2):
                    tr = Turn(i, s)
                    tr.now(act, q3["dT_ps"])
                    tr.again(act, q3["hid_ps"])
                    nc.scalar.copy(x2T[:, s, :], bk[0][:]).then_inc(q3["dT"][s], 1)
                    tr.now(act, q3["hid_ps"])
                    tr.again(act, q3["att_ps"])
                    nc.scalar.activation(att_b[:, s, :], bk[2][:], ACT.Relu, bias=c1c[:]).then_inc(q3["hid"][s], 1)
                    tr.now(act, q3["att_ps"])
                    tr.again(act, q3["att"])
                    nc.scalar.activation(rc2[:, s, :], bk[3][:, 0:J], ACT.Relu, bias=c2c[:]).then_inc(q3["att_relu"][s], 1)
                    tr.now(act, q3["att_relu"])
                    tr.again(act, q3["att_saved"])
                    tr.again(act, q3["sum"])
                    nc.scalar.activation(sm[:, s, :], rc2[:, s, :], ACT.Sigmoid).then_inc(q3["att"][s], 1)
                    tr.now(act, q3["sum"])
                    tr.again(act, q3["added"], 64)
                    nc.scalar.copy(sm2[:, s, :], bk[3][:, 8:8 + J]).then_inc(q3["sum_kept"][s], 1)
            with act.Fori(0, G // 2) as i:
                for s in range(2):
                    tr = Turn(i, s)
                    tr.now(act, q4["sum"])
                    tr.again(act, q4["added"], 64)
                    nc.scalar.copy(fd[:, s, :, :].rearrange("p j f -> p (j f)"), bk[2][:]).then_inc(q4["sum_kept"][s], 1)



        @block.tensor
        def _(pe):
            def mm(o, l, r, k, n):
                return nc.tensor.matmul(o, l, r, start=(k == 0), stop=(k == n - 1))

            pe.wait_ge(s_const, 4)
            pe.wait_ge(s_w, 16 * WEIGHTS)
            for k in range(2):
                for h in range(2):
                    nc.tensor.transpose(bk[0][:, h * H + k * P:h * H + (k + 1) * P], w2n[:, k, h * P:(h + 1) * P], ident[:])
            nc.tensor.transpose(bk[1][:, 0:D], l1w[:], ident[:]).then_inc(s_wt, 1)
            pe.wait_ge(s_wte, 1)
            for i_ in range(2):
                for k in range(2):
                    mm(bk[2][:, i_ * H:(i_ + 1) * H], w2T[:, k, i_ * P:(i_ + 1) * P], w3h[:, k, :], k, 2)
            for i_ in range(2):
                for k in range(2):
                    mm(bk[3][:, i_ * P:(i_ + 1) * P], w2T[:, k, i_ * P:(i_ + 1) * P], wab[:, k, :], k, 2)
            for h in range(2):
                for k in range(2):
                    mm(bk[3][:, 2 * P + h:2 * P + h + 1], w3h[:, k, h * P:(h + 1) * P], b2c[:, k:k + 1], k, 2)
            for k in range(2):
                last = mm(bk[3][:, 2 * P + 2:2 * P + 3], b2b[:, k, :], wac[:, k:k + 1], k, 2)
            last.then_inc(s_wp, 1)
            pe.wait_ge(s_wpk, 1)

            def spread(tr, bank, field, done):
                for j in range(J):
                    last = nc.tensor.transpose(cols(bank, j), m[:, tr.s, j, field:field + 1].to_broadcast([P, P]), ident[:])
                last.then_inc(done, 1)

            def turned(bank, tile, s, done, w=D):
                for j in range(J):
                    last = nc.tensor.transpose(bank[0:w, j * P:(j + 1) * P], tile[:, s, j, 0:w], ident[:])
                last.then_inc(done, 1)

            def totals(eq, rows, place, done):
                for j in range(J):
                    for k in range(J):
                        last = mm(place(j), eq[:, k, j * P:(j + 1) * P], rows(k), k, J)
                last.then_inc(done, 1)

            with pe.Fori(0, G // 2) as i:
                for s in range(2):
                    tr = Turn(i, s)
                    eq_d, eq_s = big0[:, 0, :, :], big1[:, :, :]

                    def product(j):
                        if j < 2:
                            tr.before(pe, q1["y_read"], J)
                        else:
                            pe.wait_ge(q1["y_read"][s], i * J + (j - 1))
                        for h in range(2):
                            last = nc.tensor.matmul(yAB[j % 2][:, h * T:(h + 1) * T], x2T[:, s, j * P:(j + 1) * P],
                                                    wcat[:, h * 4:(h + 1) * 4, :].rearrange("p b f -> p (b f)"), start=True, stop=True)
                        last.then_inc(q1["y"][s], 1)

                    tr.now(pe, q1["x_in"], 64)
                    tr.before(pe, q1["src_eq"])
                    turned(bk[1], fa, s, q1["xT_ps"][s])
                    tr.now(pe, q1["meta"])
                    tr.before(pe, q1["rows"])
                    spread(tr, bk[0], ETYPE, q1["types_bc"][s])
                    tr.now(pe, q1["xT"])
                    spread(tr, bk[1], DST, q1["dst_bc"][s])
                    tr.now(pe, q1["type_hot"])
                    for j in range(J):
                        last = nc.tensor.matmul(bk[0][:, j * NB:(j + 1) * NB], ot[:, j * P:(j + 1) * P], comp[:], start=True, stop=True)
                    last.then_inc(q1["coef_ps"][s], 1)
                    product(0)
                    tr.now(pe, q1["dst_eq"])
                    product(1)
                    spread(tr, bk[1], SRC, q1["src_bc"][s])
                    product(2)
                    tr.now(pe, q1["src_eq"])
                    tr.now(pe, q1["attr_in"], 16)
                    tr.before(pe, q1["attr_kept"])
                    totals(eq_s, lambda k: at[:, s, k, :], lambda j: bk[3][:, j * AW:(j + 1) * AW], q1["attr_sum"][s])
                    product(3)
                    tr.now(pe, q1["low"])
                    for j in range(J):
                        for v, eq in ((0, eq_s), (1, eq_d)):
                            o = bk[0][:, 64 + 2 * j + v:65 + 2 * j + v]
                            for k in range(j):
                                mm(o, eq[:, k, j * P:(j + 1) * P], ones[:], k, j + 1)
                            last = mm(o, sl[:, v, j, :], ones[:], j, j + 1)
                    last.then_inc(q1["earlier"][s], 1)
                    tr.now(pe, q1["msg"], J)
                    tr.before(pe, q1["sum_kept"])
                    totals(eq_d, lambda k: fc[:, s, k, :], lambda j: cols(bk[2], j), q1["sum"][s])

            q1["rows"].all(pe)
            q1["src_eq"].all(pe)
            q1["sum_kept"].all(pe)
            q1["attr_kept"].all(pe)
            with pe.Fori(0, G // 2) as i:
                for s in range(2):
                    tr = Turn(i, s)
                    tr.now(pe, q2["meta"])
                    tr.before(pe, q2["dst_eq"])
                    spread(tr, bk[1], DST, q2["dst_bc"][s])
                    tr.now(pe, q2["y"])
                    tr.before(pe, q2["yT"])
                    turned(bk[0], fc, s, q2["yT_ps"][s])
                    tr.now(pe, q2["yT"])
                    tr.before(pe, q2["z"])
                    for j in range(J):
                        last = nc.tensor.matmul(cols(bk[3], j), x2T[:, s, j * P:(j + 1) * P], l1wT[:], start=True, stop=True)
                    last.then_inc(q2["z_ps"][s], 1)
                    tr.now(pe, q2["dst_eq"])
                    tr.now(pe, q2["z"])
                    tr.before(pe, q2["sum_kept"])
                    totals(big0[:, 0, :, :], lambda k: ff[:, s, k, :], lambda j: cols(bk[2], j), q2["sum"][s])

            q2["dst_eq"].all(pe)
            q2["sum_kept"].all(pe)
            q1["y_read"].all(pe, J)

            def node_tensor(st):
                tr = st.tile(0)
                if tr:
                    tr.now(pe, qn["x2T"])
                    tr.now(pe, qn["agT"])
                    tr.before(pe, qn["h1"])
                    for k in range(2):
                        o = yA[:, k * T:(k + 1) * T]
                        mm(o, w1x[:, k * P:(k + 1) * P], x2T[:, tr.s, :], 0, 2)
                        last = mm(o, w1a[:, k * P:(k + 1) * P], agT[:, tr.s, :], 1, 2)
                    last.then_inc(qn["h1_ps"][tr.s], 1)
                tr = st.tile(-1)
                if tr:
                    tr.before(pe, qn["h3_pre"], 2)
                    tr.now(pe, qn["scaled"])
                    for k in range(2):
                        o = yB[:, k * T:(k + 1) * T]
                        mm(o, w3x[:, k * P:(k + 1) * P], x2T[:, tr.s, :], 0, 3)
                        for h in range(2):
                            last = mm(o, w23[:, h, k * P:(k + 1) * P], rr[:, tr.s, 2 + h, :], 1 + h, 3)
                        last.then_inc(qn["h3_ps"][tr.s], 1)
                tr = st.tile(1)
                if tr:
                    tr.now(pe, qn["x2"])
                    tr.before(pe, qn["x2T"])
                    turned(bk[0], x2s, tr.s, qn["x2T_ps"][tr.s])
                    tr.now(pe, qn["attr_mean"])
                    tr.before(pe, qn["agT"])
                    turned(bk[1], ag, tr.s, qn["agT_ps"][tr.s], A)
                tr = st.tile(0)
                if tr:
                    tr.now(pe, qn["h1"])
                    tr.before(pe, qn["attn"])
                    for k in range(2):
                        last = mm(bk[2][:], w2a[:, k, :], rr[:, tr.s, k, :], k, 2)
                    last.then_inc(qn["z_ps"][tr.s], 1)
                tr = st.tile(-1)
                if tr:
                    tr.now(pe, qn["h3"])
                    tr.before(pe, qn["t3"])
                    for j in range(J):
                        for k in range(2):
                            last = mm(cols(bk[3], j), h3[:, k, j * P:(j + 1) * P], w4s[:, k, :], k, 2)
                    last.then_inc(qn["y_ps"][tr.s], 1)

            node_steps(pe, node_tensor)

            qn["t3"].all(pe)
            with pe.Fori(0, G // 2) as i:
                for s in range(2):
                    tr = Turn(i, s)
                    tr.now(pe, q3["dif"])
                    tr.before(pe, q3["dT"])
                    turned(bk[0], fc, s, q3["dT_ps"][s])
                    tr.now(pe, q3["meta"])
                    tr.before(pe, q3["src_eq"])
                    spread(tr, bk[1], SRC, q3["src_bc"][s])
                    tr.now(pe, q3["dT"])
                    tr.before(pe, q3["hid"])
                    nc.tensor.matmul(bk[2][:], v1s[:], x2T[:, s, :], start=True, stop=True).then_inc(q3["hid_ps"][s], 1)
                    tr.now(pe, q3["hid"])
                    tr.before(pe, q3["att_relu"])
                    for j in range(J):
                        last = nc.tensor.matmul(bk[3][:, j:j + 1], att_b[:, s, j * P:(j + 1) * P], v2s[:], start=True, stop=True)
                    last.then_inc(q3["att_ps"][s], 1)
                    tr.now(pe, q3["src_eq"])
                    tr.now(pe, q3["att"])
                    tr.before(pe, q3["sum_kept"])
                    totals(big0[:, 0, :, :], lambda k: sm[:, s, k:k + 1], lambda j: bk[3][:, 8 + j:9 + j], q3["sum"][s])
            q3["src_eq"].all(pe)
            q3["hid"].all(pe)
            with pe.Fori(0, G // 2) as i:
                for s in range(2):
                    tr = Turn(i, s)
                    tr.now(pe, q4["meta"])
                    tr.before(pe, q4["dst_eq"])
                    spread(tr, bk[1], DST, q4["dst_bc"][s])
                    tr.now(pe, q4["dst_eq"])
                    tr.now(pe, q4["msg"])
                    tr.before(pe, q4["sum_kept"])
                    totals(big0[:, 0, :, :], lambda k: fc[:, s, k, :], lambda j: cols(bk[2], j), q4["sum"][s])


_INS = ['x', 'src', 'dst', 'edge_attr_96', 'edge_type_32', 'edge_weight', 'edge_weight1', 'L0_gnn_weight',
        'L0_gnn_w_comp', 'L0_gnn_bias_param', 'L1_gnn_W', 'L1_gnn_b', 'L2_gnn_W1', 'L2_gnn_b1', 'L2_gnn_W2',
        'L2_gnn_b2', 'L2_gnn_Wa', 'L2_gnn_ba', 'L2_gnn_W3', 'L2_gnn_b3', 'L2_gnn_W4', 'L2_gnn_b4', 'L3_gnn_W1',
        'L3_gnn_b1', 'L3_gnn_W2', 'L3_gnn_b2']
_OUTS = [((N, D), 'float32')]


def kernel(**inputs):
    import numpy as _np
    import concourse.bacc as _bacc
    from concourse import mybir as _mybir
    from concourse.bass_utils import run_bass_kernel_spmd as _run

    nc = _bacc.Bacc("TRN2", target_bir_lowering=False, num_devices=1)
    arrays, args = {}, []
    for name in _INS:
        a = _np.ascontiguousarray(inputs[name])
        arrays[f"in_{name}_dram"] = a
        args.append(nc.dram_tensor(f"in_{name}_dram", a.shape, _mybir.dt.from_np(a.dtype), kind="ExternalInput").ap())
    for i, (shape, dtype) in enumerate(_OUTS):
        dt = _mybir.dt.from_np(_np.dtype(dtype))
        args.append(nc.dram_tensor(f"out_{i}_dram", shape, dt, kind="ExternalOutput").ap())
    gnn_kernel(nc, *args)
    r = _run(nc, [arrays], core_ids=[0])
    return r.results[0]["out_0_dram"]
```

```python
from contextlib import ExitStack

import concourse.bass as bass
from concourse import mybir

F32 = mybir.dt.float32
I32 = mybir.dt.int32
BF16 = mybir.dt.bfloat16
F32R = mybir.dt.float32r
ALU = mybir.AluOpType
ACT = mybir.ActivationFunctionType
AX = mybir.AxisListType

P = 128
D = 128
N = 100000
E = 25000
A = 96
AW = A + 1
H = 256
R = 32
NB = 8
EP = 125
C = E // EP
J = 4
G = C // J
PAIRS = G // 2
DUMMY = J * P
NR = N + DUMMY
T = 512
NT = -(-N // T)
DQ = -(-NR // P)
EPS = 1e-5
SRC, DST, ETYPE, NORM, EW, SRC_P, SRC_Q, FIELDS = range(8)
HALF, MINUS_HALF, PER_ROW, NORM_EPS, THREE_HALVES = range(5)
CONSTANTS = (0.5, -0.5, 1.0 / D, EPS, 1.5)
MAGIC = 1597463007.0


class Signal:

    def __init__(self, sems, base, turns):
        self.sems, self.base, self.turns = sems, base, turns

    def __getitem__(self, s):
        return self.sems[s]

    def all(self, eng, each=1):
        for sem, base, turns in zip(self.sems, self.base, self.turns):
            eng.wait_ge(sem, (base + turns) * each)


class Turn:

    def __init__(self, i, s, start=None):
        self.i, self.s = i, s
        self.t = i * 2 + s
        self.start = start

    def now(self, eng, sig, each=1):
        eng.wait_ge(sig[self.s], self.i * each + (sig.base[self.s] + 1) * each)

    def part(self, eng, sig, each, k):
        eng.wait_ge(sig[self.s], self.i * each + (sig.base[self.s] * each + k))

    def again(self, eng, sig, each=1):
        eng.wait_ge(sig[self.s], self.i * each + sig.base[self.s] * each)

    def before(self, eng, sig, each=1):
        eng.wait_ge(sig[1 - self.s], self.i * each + (sig.base[1 - self.s] + self.s) * each)

    def before_part(self, eng, sig, each, k):
        if isinstance(self.t, int) and self.t == 0 and sig.base[1] == 0:
            return
        eng.wait_ge(sig[1 - self.s], self.i * each + ((sig.base[1 - self.s] + self.s - 1) * each + k))

    def long_ago(self, eng, sig, each=1):
        eng.wait_ge(sig[self.s], self.i * each + (sig.base[self.s] - 1) * each)

    def group(self, a):
        return Turn(self.t, a)


class Step:

    def __init__(self, count, n, i=None):
        self.count, self.n, self.i = count, n, i

    def turn(self, d):
        t = self.n + d
        if self.i is None:
            return Turn(t // 2, t % 2, min(t * T, N - T))
        return Turn(self.i + t // 2, t % 2, self.i * (2 * T) + t * T)

    def tile(self, d):
        return self.turn(d) if self.i is not None or 0 <= self.n + d < self.count else None


def pipeline(eng, step, count, ahead, behind):
    first, last = behind + behind % 2, (count - 1 - ahead) // 2 * 2
    for n in range(-ahead, first):
        step(Step(count, n))
    with eng.Fori(first // 2, last // 2) as i:
        for n in range(2):
            step(Step(count, n, i))
    for n in range(last, count + behind):
        step(Step(count, n))


def node_steps(eng, step):
    pipeline(eng, step, NT, 4, 5)


def edge_steps(eng, step):
    pipeline(eng, step, G, 1, 1)


def pair_steps(eng, step, ahead=0):
    pipeline(eng, step, PAIRS, ahead, 0)


class Steps:

    def __init__(self, eng, sem, turn, each):
        self.eng, self.sem, self.each, self.n = eng, sem, each, 0
        self.base = turn.t * each if turn is not None else 0

    def done(self, ins):
        self.n += 1
        assert self.each is None or self.n <= self.each
        ins.then_inc(self.sem, 1)
        return self.n

    def wait(self):
        self.eng.wait_ge(self.sem, self.base + self.n)

    def step(self, ins):
        self.done(ins)
        self.wait()

    def close(self):
        assert self.n == self.each, self.n


def gnn_kernel(nc, x, src, dst, edge_attr, edge_type, edge_weight, edge_weight1, l0_w, l0_comp, l0_b,
               l1_w, l1_b, w1, b1, w2, b2, wa, ba, w3, b3, w4, b4, v1, c1, v2, c2, out):
    ctx = ExitStack()
    with ctx:
        def sb(name, shape, dt=F32):
            return ctx.enter_context(nc.sbuf_tensor(name, shape, dt))

        def ps(name, shape):
            return ctx.enter_context(nc.psum_tensor(name, shape, F32))

        def sem(name):
            return ctx.enter_context(nc.semaphore(name))

        def sem2(name):
            return [sem(name + "_0"), sem(name + "_1")]

        def table(name, shape):
            return nc.dram_tensor(name, shape, F32, kind="Internal").ap()

        agg0 = table("agg0", [NR, D])
        agg1 = table("agg1", [NR, D])
        attr = table("attr", [NR, AW])
        den = table("den", [P * DQ, 1])
        x3 = table("x3", [NR, D])
        xsrc = table("xsrc", [G, P, J * D])
        hsrc = table("hsrc", [G, P, J * D])

        ident = sb("ident", [P, P])
        lower = sb("lower", [P, P])
        ones = sb("ones", [P, 1])
        part = sb("part", [P, 1])
        part_i = sb("part_i", [P, 1], I32)
        dummy = sb("dummy_row", [P, J, 2])
        dummy_i = sb("dummy_row_i", [P, J, 2], I32)
        zeros = sb("zeros", [P, 16 * D])
        row0 = sb("row0", [P, 16, D])
        row1 = sb("row1", [P, 16, D])
        wcat = sb("wcat", [P, NB, D])
        comp = sb("comp", [R, NB])
        l1w = sb("l1w", [P, D])
        l1wT = sb("l1wT", [P, D])
        w1x = sb("w1x", [P, H])
        w1a = sb("w1a", [A, H])
        w2n = sb("w2n", [P, 2, H])
        w2T = sb("w2T", [P, 2, H])
        w3x = sb("w3x", [P, H])
        w3h = sb("w3h", [P, 2, H])
        w23 = sb("w23", [P, 2, H])
        w4s = sb("w4s", [P, 2, D])
        wac = sb("wac", [P, 2])
        wab = sb("wab", [P, 2, P])
        w2a = sb("w2a", [P, 2])
        ones_b = sb("ones_b", [P, P])
        zpart = sb("zpart", [P, T])
        zsum = sb("zsum", [P, T])
        xh = sb("xh", [P, 2, T], F32R)
        xl = sb("xl", [P, 2, T], F32R)
        w1h, w1l = sb("w1h", [P, H], F32R), sb("w1l", [P, H], F32R)
        w3xh, w3xl = sb("w3xh", [P, H], F32R), sb("w3xl", [P, H], F32R)
        wch, wcl = sb("wch", [P, NB, D], F32R), sb("wcl", [P, NB, D], F32R)
        b1c = sb("b1c", [P, 2])
        b2c = sb("b2c", [P, 2])
        b2b = sb("b2b", [P, 2, P])
        b3c = sb("b3c", [P, 2])
        c23 = sb("c23", [P, 2])
        bab = sb("bab", [P, 1])
        zb = sb("zb", [P, 1])
        b4b = sb("b4b", [P, J, D])
        v1s = sb("v1s", [P, D])
        c1c = sb("c1c", [P, 1])
        v2s = sb("v2s", [P, 1])
        c2c = sb("c2c", [P, 1])

        src_x = sb("src_x", [P, C], I32)
        dst_x = sb("dst_x", [P, C], I32)
        src_s = sb("src_s", [P, C], I32)
        dst_s = sb("dst_s", [P, C], I32)
        et_i = sb("et_i", [P, C], I32)
        nrm = sb("nrm", [P, C])
        ew_s = sb("ew_s", [P, C])
        meta = sb("meta", [P, C, FIELDS])
        uniq = sb("uniq", [P, C, 2], I32)
        att_all = sb("att_all", [P, C])
        low_bits = sb("low_bits", [P, C], I32)
        high_bits = sb("high_bits", [P, C], I32)
        den_row = sb("den_row", [P, C], I32)
        numbers_i = sb("numbers_i", [P, DQ], I32)
        numbers = sb("numbers", [P, DQ])

        fa = sb("fa", [P, 2, J, D])
        fb = sb("fb", [P, 2, J, D])
        fc = sb("fc", [P, 2, J, D])
        fd = sb("fd", [P, 2, J, D])
        fe = sb("fe", [P, 2, J, D])
        ff = sb("ff", [P, 2, J, D])
        x2s = sb("x2s", [P, 2, J, D])
        big0 = sb("big0", [P, 2, J, T])
        big1 = sb("big1", [P, J, T])
        sl = sb("sl", [P, 2, J, P])
        at = sb("at", [P, 2, J, AW])
        ag = sb("ag", [P, 2, J, AW])
        m = sb("m", [P, 2, J, FIELDS])
        gi = sb("gi", [P, 2, J], I32)
        gi2 = sb("gi2", [P, 2, J], I32)
        ui = sb("ui", [P, 2, J, 2], I32)
        ot = sb("ot", [R, T])
        cf = sb("cf", [P, 2, J, NB])
        prod = sb("prod", [P, 2, NB, D])
        dd = sb("dd", [P, J, 2])
        lowerb = sb("lowerb", [P, P], BF16)
        onesb = sb("onesb", [P, 1], BF16)
        absd = sb("absd", [P, J, T])
        nf = sb("nf", [P, J, 2])
        st = sb("st", [P, 2 * J, 6])
        mv = sb("mv", [P, 2 * J, 2])
        h_sum = sb("h_sum", [P, 2 * J])
        h_dif = sb("h_dif", [P, 2 * J])
        h_sq = sb("h_sq", [P, 2 * J])
        pair_rows = sb("pair_rows", [P, 2, 2 * J], I32)
        pair_uniq = sb("pair_uniq", [P, 2, 2 * J], I32)
        den_e = sb("den_e", [P, 2, 2 * J])
        att_n = sb("att_n", [P, 2, 2 * J])
        nv = sb("nv", [P, 2 * J])
        ny = sb("ny", [P, 2 * J])
        na = sb("na", [P, 2 * J])
        nb = sb("nb", [P, 2 * J])
        rc = sb("rc", [P, J])
        sm = sb("sm", [P, 2, J])
        rc2 = sb("rc2", [P, 2, J])
        va = sb("va", [P, 2, J, D])
        vb = sb("vb", [P, 2, J, D])
        t3 = sb("t3", [P, 2, J, D])
        stq = sb("stq", [P, 2, 3, J, 6])
        nmean = sb("nmean", [P, 2, 3, J])
        nry = sb("nry", [P, 2, 4, J])
        nbias = sb("nbias", [P, 2, 2, J])
        pa, pb, pc, pd = (sb(n, [P, 3, J]) for n in ("pa", "pb", "pc", "pd"))
        pv, py2 = (sb(n, [P, 4, J]) for n in ("pv", "py2"))
        pnm = sb("pnm", [P, J])
        kc = sb("kc", [P, 5])
        x2T = sb("x2T", [P, 2, T])
        agT = sb("agT", [A, 2, T])
        rr = big0
        att_b = sb("att_b", [P, 2, T])
        h3_pre = big1
        h3 = prod[:, :, :, :].rearrange("p s (k b) f -> p s k (b f)", k=2)

        yA = ps("yA", [P, 2 * T])
        yB = ps("yB", [P, 2 * T])
        bk = [ps(f"bk{n}", [P, T]) for n in range(4)]
        yAB = [yA, yB]

        def eq0(v, s, k):
            return big0[:, v, k, :].bitcast(BF16)[:, s * T:(s + 1) * T]

        def low0(v, s, j):
            return sl[:, v, j, :].bitcast(BF16)[:, s * P:(s + 1) * P]

        def hot_q(j):
            return big0[:, j // 2, 2 * (j % 2):2 * (j % 2) + 2, :].rearrange("p k f -> p (k f)")[:, 0:DQ]

        def slot_bank(y, s):
            return y[:, s * T:(s + 1) * T]

        def cols(bank, j):
            return bank[:, j * P:(j + 1) * P]

        s_zero = sem("zeros_set")
        s_const = sem("constants_set")
        s_pad = sem("padding_set")
        s_w = sem("weights_loaded")
        s_e = sem("edges_loaded")
        s_dup = sem("weight_copies_made")
        s_meta = sem("meta_made")
        s_at = sem("attr_slots_set")
        s_wt = sem("weights_transposed")
        s_wte = sem("weights_transposed_kept")
        s_wp = sem("weight_products")
        s_wpk = sem("weight_products_kept")
        s_row = sem("bias_rows_loaded")
        s_fill0 = sem("agg0_filled")
        s_fill1 = sem("agg1_filled")
        s_filla = sem("attr_filled")
        s_filld = sem("den_filled")
        s_gate = sem("pool_gate_passed")
        s_pset = sem("pool_set_up")

        block = ctx.enter_context(nc.Block())

        def edge_rows(a, g):
            return a.rearrange("(p c) f -> p c f", p=EP)[:, bass.ds(g * J, J), :]

        def node_rows(a, start, rows=T):
            return a[bass.ds(start, rows), :].rearrange("(p j) f -> p (j f)", p=P)

        def flat(tile, s):
            return tile[:, s, :, :].rearrange("p j f -> p (j f)")

        FILL_TURNS = NR // (16 * P)
        FILL_REST = (NR - FILL_TURNS * 16 * P) // 32

        def fill_turn(eng, tab, tile, w, t, done):
            view = tab[0:FILL_TURNS * 16 * P, :].rearrange("(t p j) f -> t p (j f)", p=P, j=16)
            eng.dma_start(view[bass.ds(t, 1), :, :].rearrange("o p f -> (o p) f"), tile[:, 0:16 * w]).then_inc(done, 16)

        def fill_rest(eng, tab, tile, w, done):
            eng.dma_start(tab[FILL_TURNS * 16 * P:NR, :].rearrange("(p j) f -> p (j f)", p=32),
                          tile[0:32, 0:FILL_REST * w]).then_inc(done, 16)

        flat_den = absd[:, 0:2, :].rearrange("p k f -> p (k f)")[:, 0:DQ]
        row0_flat = row0[:, :, :].rearrange("p j f -> p (j f)")
        row1_flat = row1[:, :, :].rearrange("p j f -> p (j f)")

        def gate(pool):
            pool.sem_inc(s_gate, 1)

        pairs, counted = {}, {}

        def phase(name, turns, own, shared):
            found = {}
            for key, role in [(k, name + "_" + k) for k in own.split()] + list(shared.items()):
                if role not in pairs:
                    pairs[role], counted[role] = sem2(role), (0, 0)
                in_slot = ((turns + 1) // 2, turns // 2)
                found[key] = Signal(pairs[role], counted[role], in_slot)
                counted[role] = tuple(c + n for c, n in zip(counted[role], in_slot))
            return found

        def same(keys):
            return {k: k for k in keys.split()}

        q0 = phase("e0", G, "",
                   {"low": "hot", "earlier": "small_ps", "rows": "rows",
                    **same("meta dst_bc dst_eq src_bc src_eq gidx"), "x_in": "gathered", "x_out": "rows_saved"})
        q1 = phase("e1", G, "y_read y_read_scalar",
                   {"y": "columns_multiplied", "msg": "columns_made", "types_bc": "other_ps", "type_hot": "hot", "coef_ps": "small_ps", "coef": "rows",
                    **same("meta dst_bc dst_eq sum sum_kept uidx added"),
                    "x_in": "rows_loaded", "xT_ps": "turned_ps", "xT": "turned", "xT_low": "turned_low"})
        q2 = phase("e2", G, "y z_ps z attr_kept",
                   {"attr_added": "more_added", "attr_sum": "other_ps", "v": "residual_0", "attr_in": "attr_loaded",
                    **same("meta dst_bc dst_eq src_bc src_eq sum sum_kept gidx gidx2 uidx added"),
                    "agg_in": "gathered", "x_in": "rows_loaded", "yT_ps": "turned_ps", "yT": "turned"})
        qn = phase("n", NT, "in agg1_in v1 attr_mean agT_ps agT h3_ps h3_pre h3 y_ps x2b t3 x3 x4"
                   " x3_out x4_out stats scales",
                   {"x2T_low": "turned_low", "zsum": "rows", "zpart": "turned_more", "scaled": "hot", "x2T_ps": "turned_ps", "x2T": "turned", "h1_ps": "hidden_ps", "h1": "hidden", "z_ps": "logit_ps",
                    "attn": "attention", "v0": "residual_0", "x2": "normed", "attr_in": "attr_loaded"})
        q3 = phase("e3", G, "att_relu att_saved",
                   {"hd_in": "more_added", "dif": "residual_0", "hot_p": "hot", "hid_ps": "hidden_ps", "hid": "hidden", "att_ps": "logit_ps", "att": "attention",
                    **same("meta gidx gidx2"), "hot": "columns_made", "used": "columns_multiplied",
                    "hs_in": "gathered", "h_out": "rows_saved", "dT_ps": "turned_ps", "dT": "turned"})
        q4 = phase("e4", G, "msg",
                   {**same("meta dst_bc dst_eq sum sum_kept uidx added"), "h_in": "rows_loaded"})
        q4_pair = phase("e4", PAIRS, "weight", {"gidx": "gidx", "den_in": "pair_gathered"})
        q5 = phase("e5", G, "", {"out": "added"})
        q5_pair = phase("e5", PAIRS, "", {"y": "normed", **same("gidx gidx2"), "x_in": "pair_gathered"})
        c1s, c2s, c3s, c4s, c5s = (sem(f"vector_steps_e{n}") for n in (1, 2, 3, 4, 5))
        cna, pool_n = sem("vector_steps_n"), sem("pool_steps_n")
        s_kc = sem("constant_columns_set")
        s_bf = sem("bf16_constants_made")
        s_den_ps = sem("den_summed")
        s_den = sem("den_kept")
        s_abs = sem2("distances_made")
        s_stq = sem("stats_slots_set")
        s_split = sem("weights_split")
        x3_pad = sem("x3_dummies_set")

        WEIGHTS = 20

        @block.sync
        def _(sp):
            def bcast_rows(vec, n):
                return vec.rearrange("(o f) -> o f", o=1).to_broadcast([n, vec.shape[0]])

            sp.wait_ge(s_pad, 6)
            for tile, a in ((src_x, src), (src_s, src), (dst_x, dst), (dst_s, dst), (et_i, edge_type),
                            (ew_s, edge_weight)):
                sp.dma_start(tile[0:EP, :], a.rearrange("(p c) -> p c", p=EP)).then_inc(s_e, 16)
            sp.dma_start(nrm[0:EP, :], edge_weight1.rearrange("(p c) o -> p (c o)", p=EP)).then_inc(s_e, 16)
            for k in range(16):
                sp.dma_start(row0[:, k, :], bcast_rows(l0_b, P)).then_inc(s_row, 16)
            n = 0
            for o, i in ((wcat[:, :, :], l0_w.rearrange("b i o -> i b o")), (comp[:, :], l0_comp),
                         (l1w[:, :], l1_w), (w1x[:, :], w1[0:D, :]), (w1a[:, :], w1[D:D + A, :]),
                         (w2n[:, :, :], w2.rearrange("(k p) n -> p k n", p=P)),
                         (w3x[:, :], w3[0:D, :]),
                         (w3h[:, :, :], w3[D:D + H, :].rearrange("(k p) n -> p k n", p=P)),
                         (w4s[:, :, :], w4.rearrange("(k p) n -> p k n", p=P)),
                         (wac[:, :], wa.rearrange("(k p) o -> p (k o)", p=P)),
                         (b1c[:, :], b1.rearrange("(k p) -> p k", p=P)),
                         (b2c[:, :], b2.rearrange("(k p) -> p k", p=P)),
                         (b3c[:, :], b3.rearrange("(k p) -> p k", p=P)),
                         (bab[:, :], bcast_rows(ba, P)), (v1s[:, :], v1),
                         (c1c[:, :], c1.rearrange("(p o) -> p o", o=1)), (v2s[:, :], v2),
                         (c2c[:, :], bcast_rows(c2, P)), (b4b[:, 0, :], bcast_rows(b4, P)),
                         (row1[:, 0, :], bcast_rows(l1_b, P))):
                sp.dma_start(o, i, allow_slow_non_contiguous=True).then_inc(s_w, 16)
                n += 1
            assert n == WEIGHTS

            sp.wait_ge(s_zero, 1)
            sp.dma_start(x3[N:NR, :].rearrange("(p j) f -> p (j f)", p=P), zeros[:, 0:J * D]).then_inc(x3_pad, 16)

            def group_rows(tab, tr):
                return tab[bass.ds(tr.t, 1), :, :].rearrange("o p f -> (o p) f")

            with sp.Fori(0, G // 2) as i:
                for s in range(2):
                    tr = Turn(i, s)
                    tr.now(sp, q0["x_in"], 64)
                    sp.dma_start(group_rows(xsrc, tr), flat(fa, s)).then_inc(q0["x_out"][s], 16)
            q0["x_out"].all(sp, 16)
            sp.wait_ge(s_dup, 1)

            def edges_1(tr, part):
                tr.again(sp, q1["xT_ps"])
                sp.dma_start(flat(fa, tr.s), group_rows(xsrc, tr)).then_inc(q1["x_in"][tr.s], 16)
                if part == "turn":
                    fill_turn(sp, attr, zeros, AW, tr.t, s_filla)
                    fill_turn(sp, agg1, row1_flat, D, tr.t, s_fill1)
                elif part == "rest":
                    fill_rest(sp, attr, zeros, AW, s_filla)
                    fill_rest(sp, agg1, row1_flat, D, s_fill1)

            assert FILL_TURNS == G - 1
            with sp.Fori(0, G // 2 - 1) as i:
                for s in range(2):
                    edges_1(Turn(i, s), "turn")
            edges_1(Turn(G // 2 - 1, 0), "turn")
            edges_1(Turn(G // 2 - 1, 1), "rest")
            sp.wait_ge(s_at, 2)
            with sp.Fori(0, G // 2) as i:
                for s in range(2):
                    tr = Turn(i, s)
                    tr.again(sp, q2["attr_sum"])
                    sp.dma_start(at[0:EP, s, :, 0:A], edge_rows(edge_attr, tr.t)).then_inc(q2["attr_in"][s], 16)
                    tr.again(sp, q2["v"])
                    sp.dma_start(flat(fa, s), group_rows(xsrc, tr)).then_inc(q2["x_in"][s], 16)

            q1["added"].all(sp, 64)
            q2["attr_added"].all(sp, 64)
            q2["added"].all(sp, 64)
            q2["sum_kept"].all(sp)
            q2["attr_sum"].all(sp)

            def node_io(st):
                tr = st.tile(4)
                if tr:
                    tr.again(sp, qn["v0"])
                    sp.dma_start(flat(fa, tr.s), node_rows(x, tr.start)).then_inc(qn["in"][tr.s], 16)
                    sp.dma_start(flat(fb, tr.s), node_rows(agg0, tr.start)).then_inc(qn["in"][tr.s], 16)
                tr = st.tile(3)
                if tr:
                    tr.again(sp, qn["v1"])
                    sp.dma_start(flat(fc, tr.s), node_rows(agg1, tr.start)).then_inc(qn["agg1_in"][tr.s], 16)
                tr = st.tile(2)
                if tr:
                    tr.again(sp, qn["attr_mean"])
                    sp.dma_start(flat(at, tr.s), node_rows(attr, tr.start)).then_inc(qn["attr_in"][tr.s], 16)
                tr = st.tile(-4)
                if tr:
                    if st.i is None and st.n - 4 == NT - 1:
                        tr.before(sp, qn["x3_out"], 16)
                        tr.before(sp, qn["x4_out"], 16)
                    tr.now(sp, qn["x3"])
                    sp.dma_start(node_rows(x3, tr.start), flat(fe, tr.s)).then_inc(qn["x3_out"][tr.s], 16)
                    tr.now(sp, qn["x4"])
                    sp.dma_start(node_rows(out, tr.start), flat(ff, tr.s)).then_inc(qn["x4_out"][tr.s], 16)

            node_steps(sp, node_io)

            with sp.Fori(0, G // 2) as i:
                for s in range(2):
                    tr = Turn(i, s)
                    tr.now(sp, q3["hs_in"], 64)
                    sp.dma_start(hsrc[bass.ds(tr.t, 1), :, :].rearrange("o p f -> (o p) f"), fa[:, s, :, :].rearrange("p j f -> p (j f)")).then_inc(q3["h_out"][s], 16)
            q3["h_out"].all(sp, 16)
            q3["dif"].all(sp)
            sp.wait_ge(s_den, 1)
            sp.dma_start(den.rearrange("(p q) o -> p (q o)", p=P), flat_den).then_inc(s_filld, 16)
            with sp.Fori(0, G // 2) as i:
                for s in range(2):
                    tr = Turn(i, s)
                    tr.again(sp, q4["msg"])
                    sp.dma_start(fa[:, s, :, :].rearrange("p j f -> p (j f)"), hsrc[bass.ds(tr.t, 1), :, :].rearrange("o p f -> (o p) f")).then_inc(q4["h_in"][s], 16)
            qn["x4_out"].all(sp, 16)
            q5["out"].all(sp, 64)

        @block.gpsimd
        def _(pool):
            nc.gpsimd.memset(ident[:], 0.0).then_inc(s_pset, 1)
            nc.gpsimd.memset(lower[:], 1.0).then_inc(s_pset, 1)
            nc.gpsimd.iota(src_s[:], pattern=[[0, C]], base=N, channel_multiplier=J).then_inc(s_pad, 1)
            nc.gpsimd.iota(dst_s[:], pattern=[[0, C]], base=N, channel_multiplier=J).then_inc(s_pad, 1)
            nc.gpsimd.iota(part_i[:], pattern=[[0, 1]], base=0, channel_multiplier=1).then_inc(s_const, 1)
            nc.gpsimd.iota(dummy_i[:], pattern=[[1, J], [0, 2]], base=N, channel_multiplier=J).then_inc(s_const, 1)
            nc.gpsimd.iota(numbers_i[:], pattern=[[1, DQ]], base=0, channel_multiplier=0).then_inc(s_const, 1)
            pool.wait_ge(s_pset, 2)
            nc.gpsimd.affine_select(out=ident[:], in_=ident[:], compare_op=ALU.not_equal, fill=1.0, base=0,
                                    pattern=[[-1, P]], channel_multiplier=1).then_inc(s_const, 1)
            nc.gpsimd.affine_select(out=lower[:], in_=lower[:], compare_op=ALU.is_gt, fill=0.0, base=0,
                                    pattern=[[1, P]], channel_multiplier=-1).then_inc(s_const, 1)
            pool.wait_ge(s_e, 16 * 7)

            def index(tr, q, key, slot, source):
                nc.gpsimd.tensor_copy(slot, source).then_inc(q[key][tr.s], 1)
                tr.now(pool, q[key])
                gate(pool)

            def gather(tab, idx, tiles, done):
                for j in range(J):
                    nc.gpsimd.indirect_dma_start(tiles[j], None, tab, bass.IndirectOffsetOnAxis(idx[:, j:j + 1], 0)).then_inc(done, 16)

            def add(tab, idx, tiles, done):
                for j in range(J):
                    nc.gpsimd.indirect_dma_start(tab, bass.IndirectOffsetOnAxis(idx[j], 0), tiles[j], None, compute_op=ALU.add).then_inc(done, 16)

            def rows4(tile, s):
                return [tile[:, s, j, :] for j in range(J)]

            with pool.Fori(0, G // 2) as i:
                for s in range(2):
                    tr = Turn(i, s)
                    tr.again(pool, q0["x_out"], 16)
                    tr.again(pool, q0["x_in"], 64)
                    gate(pool)
                    index(tr, q0, "gidx", gi[:, s, :], src_x[:, bass.ds(tr.t * J, J)])
                    gather(x, gi[:, s, :], rows4(fa, s), q0["x_in"][s])

            q0["rows"].all(pool)
            pool.wait_ge(s_fill0, 16 * (FILL_TURNS + 1))
            with pool.Fori(0, G // 2) as i:
                for s in range(2):
                    tr = Turn(i, s)
                    tr.before(pool, q1["added"], 64)
                    gate(pool)
                    index(tr, q1, "uidx", ui[:, s, :, 1:2], uniq[:, bass.ds(tr.t * J, J), 1:2])
                    tr.now(pool, q1["sum_kept"])
                    gate(pool)
                    add(agg0, [ui[:, s, j, 1:2] for j in range(J)], rows4(fd, s), q1["added"][s])

            q1["added"].all(pool, 64)
            pool.wait_ge(s_fill1, 16 * (FILL_TURNS + 1))
            pool.wait_ge(s_filla, 16 * (FILL_TURNS + 1))
            gate(pool)

            def layer1_pool(st):
                tr = st.tile(2)
                if tr:
                    tr.again(pool, q2["v"])
                    tr.again(pool, q2["agg_in"], 64)
                    gate(pool)
                    index(tr, q2, "gidx", gi[:, tr.s, :], src_x[:, bass.ds(tr.t * J, J)])
                    gather(agg0, gi[:, tr.s, :], rows4(fb, tr.s), q2["agg_in"][tr.s])
                tr = st.tile(1)
                if tr:
                    tr.before(pool, q2["attr_added"], 64)
                    gate(pool)
                    index(tr, q2, "gidx2", ui[:, tr.s, :, 0:1], uniq[:, bass.ds(tr.t * J, J), 0:1])
                    tr.now(pool, q2["attr_kept"])
                    gate(pool)
                    add(attr, [ui[:, tr.s, j, 0:1] for j in range(J)], rows4(ag, tr.s), q2["attr_added"][tr.s])
                tr = st.tile(0)
                if tr:
                    tr.before(pool, q2["added"], 64)
                    gate(pool)
                    index(tr, q2, "uidx", ui[:, tr.s, :, 1:2], uniq[:, bass.ds(tr.t * J, J), 1:2])
                    tr.now(pool, q2["sum_kept"])
                    gate(pool)
                    add(agg1, [ui[:, tr.s, j, 1:2] for j in range(J)], rows4(fd, tr.s), q2["added"][tr.s])

            pipeline(pool, layer1_pool, G, 2, 0)

            pool.wait_ge(s_dup, 1)
            for k, value in enumerate(CONSTANTS):
                nc.gpsimd.memset(kc[:, k:k + 1], value).then_inc(s_kc, 1)
            pool.wait_ge(s_kc, len(CONSTANTS))
            q2["added"].all(pool, 64)
            q2["attr_added"].all(pool, 64)

            def batch(st, idx):
                idx.now(pool, qn["stats"])
                if st.tile(-5):
                    st.tile(-5).now(pool, qn["x4"])
                g = nc.gpsimd
                steps = Steps(pool, pool_n, idx, POOL_STEPS)
                raw, mean, y, bias = stq[:, idx.s], nmean[:, idx.s], nry[:, idx.s], nbias[:, idx.s]
                steps.done(g.tensor_tensor(pa[:], raw[:, :, :, 1], raw[:, :, :, 4], ALU.add))
                steps.done(g.tensor_tensor(pb[:], raw[:, :, :, 1], raw[:, :, :, 4], ALU.subtract))
                steps.step(g.tensor_tensor(pc[:], raw[:, :, :, 2], raw[:, :, :, 5], ALU.add))
                steps.done(g.tensor_tensor(mean, pa[:], const(HALF, 3), ALU.mult))
                steps.done(g.tensor_tensor(pnm[:], pa[:, 2, :], const(MINUS_HALF), ALU.mult))
                steps.done(g.tensor_tensor(pb[:], pb[:], const(HALF, 3), ALU.mult))
                steps.step(g.tensor_tensor(pc[:], pc[:], const(PER_ROW, 3), ALU.mult))
                steps.step(g.tensor_tensor(pd[:], pb[:], pb[:], ALU.mult))
                steps.step(g.tensor_tensor(pc[:], pc[:], pd[:], ALU.add))
                steps.step(g.tensor_tensor(pv[:, 0:3, :], pc[:], const(NORM_EPS, 3), ALU.add))
                steps.step(g.tensor_tensor(pv[:, 3, :], pv[:, 2, :], const(NORM_EPS), ALU.mult))
                steps.step(g.tensor_tensor(pv[:, 3, :], pv[:, 3, :], pc[:, 2, :], ALU.add))
                gate(pool)
                steps.step(g.tensor_scalar(y.bitcast(I32), pv[:].bitcast(I32), -0.5, MAGIC, ALU.mult, ALU.add))
                steps.done(g.tensor_tensor(pv[:], pv[:], const(HALF, 4), ALU.mult))
                for k in range(3):
                    steps.step(g.tensor_tensor(py2[:], y, y, ALU.mult))
                    steps.step(g.tensor_tensor(py2[:], py2[:], pv[:], ALU.mult))
                    steps.step(g.tensor_tensor(py2[:], const(THREE_HALVES, 4), py2[:], ALU.subtract))
                    steps.step(g.tensor_tensor(y, y, py2[:], ALU.mult))
                steps.done(g.tensor_tensor(bias[:, 0, :], pnm[:], y[:, 2, :], ALU.mult))
                steps.close()
                g.tensor_tensor(bias[:, 1, :], pnm[:], y[:, 3, :], ALU.mult).then_inc(qn["scales"][idx.s], 1)

            POOL_STEPS = 27

            def const(k, rows=None):
                if rows is None:
                    return kc[:, k:k + 1].to_broadcast([P, J])
                return kc[:, k:k + 1].rearrange("p (o j) -> p o j", o=1).to_broadcast([P, rows, J])

            def node_pool(st):
                tr = st.tile(-1)
                if tr:
                    tr.now(pool, qn["x2"])
                    tr.again(pool, qn["t3"])
                    nc.gpsimd.tensor_tensor(fd[:, tr.s, :, :], x2s[:, tr.s, :, :], b4b[:, :, :], ALU.add).then_inc(qn["x2b"][tr.s], 1)
                if st.tile(3) or st.tile(2) or st.tile(-3):
                    batch(st, st.turn(3))

            node_steps(pool, node_pool)

            qn["x3_out"].all(pool, 16)
            qn["t3"].all(pool)
            pool.wait_ge(x3_pad, 16)

            def h_rows(tr):
                tr.again(pool, q3["dif"])
                tr.again(pool, q3["h_out"], 16)
                tr.again(pool, q3["hs_in"], 64)
                tr.again(pool, q3["hd_in"], 64)
                gate(pool)
                nc.gpsimd.tensor_copy(gi[:, tr.s, :], src_x[:, bass.ds(tr.t * J, J)]).then_inc(q3["gidx"][tr.s], 1)
                nc.gpsimd.tensor_copy(gi2[:, tr.s, :], dst_x[:, bass.ds(tr.t * J, J)]).then_inc(q3["gidx2"][tr.s], 1)
                tr.now(pool, q3["gidx"])
                tr.now(pool, q3["gidx2"])
                gate(pool)
                gather(x3, gi[:, tr.s, :], rows4(fa, tr.s), q3["hs_in"][tr.s])
                gather(x3, gi2[:, tr.s, :], rows4(fb, tr.s), q3["hd_in"][tr.s])

            with pool.Fori(0, G // 2) as i:
                for s in range(2):
                    h_rows(Turn(i, s))

            pool.wait_ge(s_filld, 16)
            q3["hs_in"].all(pool, 64)
            q3["hd_in"].all(pool, 64)
            gate(pool)

            def gather_half(tab, tr, a, tiles, done):
                for j in range(J):
                    nc.gpsimd.indirect_dma_start(tiles[j], None, tab, bass.IndirectOffsetOnAxis(
                        pair_rows[:, tr.s, a * J + j:a * J + j + 1], 0)).then_inc(done, 16)

            def layer3_pool(st):
                tr, nxt = st.tile(0), st.tile(1)
                if nxt:
                    nxt.again(pool, q4_pair["weight"])
                    nxt.again(pool, q4_pair["den_in"], 128)
                    gate(pool)
                    index(nxt, q4_pair, "gidx", pair_rows[:, nxt.s, :], den_row[:, bass.ds(nxt.t * 2 * J, 2 * J)])
                for a in range(2):
                    if nxt:
                        gather_half(den, nxt, a, [den_e[:, nxt.s, a * J + j:a * J + j + 1] for j in range(J)],
                                    q4_pair["den_in"][nxt.s])
                    if tr:
                        grp = tr.group(a)
                        grp.before(pool, q4["added"], 64)
                        gate(pool)
                        index(grp, q4, "uidx", ui[:, a, :, 1:2], uniq[:, bass.ds(grp.t * J, J), 1:2])
                        grp.now(pool, q4["sum_kept"])
                        gate(pool)
                        add(x3, [ui[:, a, j, 1:2] for j in range(J)], rows4(fd, a), q4["added"][a])

            pair_steps(pool, layer3_pool, 1)

            q4["added"].all(pool, 64)
            q4_pair["den_in"].all(pool, 128)
            q4["sum"].all(pool)
            qn["x4_out"].all(pool, 16)
            gate(pool)

            def norm_pool(st):
                tr, nxt = st.tile(0), st.tile(1)
                if nxt:
                    nxt.again(pool, q5_pair["y"])
                    nxt.again(pool, q5_pair["x_in"], 128)
                    for a in range(2):
                        nxt.group(a).long_ago(pool, q5["out"], 64)
                    gate(pool)
                    nc.gpsimd.tensor_copy(pair_rows[:, nxt.s, :], dst_x[:, bass.ds(nxt.t * 2 * J, 2 * J)]).then_inc(q5_pair["gidx"][nxt.s], 1)
                    nc.gpsimd.tensor_copy(pair_uniq[:, nxt.s, :], uniq[:, bass.ds(nxt.t * 2 * J, 2 * J), 1:2].rearrange("p j o -> p (j o)")).then_inc(q5_pair["gidx2"][nxt.s], 1)
                    nxt.now(pool, q5_pair["gidx"])
                    nxt.now(pool, q5_pair["gidx2"])
                    gate(pool)
                for a in range(2):
                    if nxt:
                        gather_half(x3, nxt, a, rows4((fa, fb)[a], nxt.s), q5_pair["x_in"][nxt.s])
                    if tr:
                        grp = tr.group(a)
                        tr.now(pool, q5_pair["y"])
                        grp.before(pool, q5["out"], 64)
                        gate(pool)
                        for j in range(J):
                            nc.gpsimd.indirect_dma_start(out, bass.IndirectOffsetOnAxis(pair_uniq[:, tr.s, a * J + j:a * J + j + 1], 0),
                                                         (fd, fc)[a][:, tr.s, j, :], None, bounds_check=N - 1, oob_is_err=False).then_inc(q5["out"][a], 16)

            pair_steps(pool, norm_pool, 1)

        @block.vector
        def _(dve):
            nc.vector.memset(zeros[:], 0.0).then_inc(s_zero, 1)
            nc.vector.memset(src_x[:], 0)
            nc.vector.memset(dst_x[:], 0)
            nc.vector.memset(et_i[:], 0).then_inc(s_pad, 1)
            nc.vector.memset(ew_s[:], 0.0).then_inc(s_pad, 1)
            nc.vector.memset(nrm[:], 0.0).then_inc(s_pad, 1)
            nc.vector.memset(ones[:], 1.0)
            nc.vector.memset(ones_b[:], 1.0).then_inc(s_pad, 1)
            nc.vector.memset(at[:], 0.0).then_inc(s_at, 1)
            dve.wait_ge(s_at, 1)
            nc.vector.memset(at[0:EP, :, :, A:AW], 1.0).then_inc(s_at, 1)
            dve.wait_ge(s_const, 5)
            nc.vector.tensor_copy(part[:], part_i[:])
            nc.vector.tensor_copy(dummy[:], dummy_i[:])
            nc.vector.tensor_copy(numbers[:], numbers_i[:])
            dve.wait_ge(s_e, 16 * 7)
            for k, tile in ((SRC, src_s), (DST, dst_s), (ETYPE, et_i), (NORM, nrm), (EW, ew_s)):
                nc.vector.tensor_copy(meta[:, :, k:k + 1], tile[:].rearrange("p (c o) -> p c o", o=1)).then_inc(s_meta, 1)
            nc.vector.tensor_scalar(low_bits[:], src_s[:], P - 1, None, ALU.bitwise_and).then_inc(s_meta, 1)
            nc.vector.tensor_scalar(high_bits[:], src_s[:], P.bit_length() - 1, None, ALU.logical_shift_right).then_inc(s_meta, 1)
            dve.wait_ge(s_meta, 7)
            for k, tile in ((SRC_P, low_bits), (SRC_Q, high_bits)):
                nc.vector.tensor_copy(meta[:, :, k:k + 1], tile[:].rearrange("p (c o) -> p c o", o=1)).then_inc(s_meta, 1)
            dve.wait_ge(s_meta, 9)
            nc.vector.scalar_tensor_tensor(den_row[:], meta[:, :, SRC_P], float(DQ), meta[:, :, SRC_Q], ALU.mult, ALU.add).then_inc(s_meta, 1)
            dve.wait_ge(s_meta, 10)

            def norm_scale(stp, width):
                a, b, v, y = (t[:, 0:width] for t in (na, nb, nv, ny))
                stp.step(nc.vector.tensor_scalar(y.bitcast(I32), v.bitcast(I32), -0.5, MAGIC, ALU.mult, ALU.add))
                for _ in range(3):
                    stp.step(nc.vector.scalar_tensor_tensor(a, y, -0.5, y, ALU.mult, ALU.mult))
                    stp.step(nc.vector.tensor_tensor(b, a, v, ALU.mult))
                    stp.step(nc.vector.scalar_tensor_tensor(y, b, 1.5, y, ALU.add, ALU.mult))

            NORM_STEPS = 10

            def stats(stp, rows):
                w = len(rows)
                for j, row in enumerate(rows):
                    stp.done(nc.vector.bn_stats(st[:, j, :], row))
                stp.wait()
                stp.done(nc.vector.tensor_tensor(h_sum[:, 0:w], st[:, 0:w, 1], st[:, 0:w, 4], ALU.add))
                stp.done(nc.vector.tensor_tensor(h_dif[:, 0:w], st[:, 0:w, 1], st[:, 0:w, 4], ALU.subtract))
                stp.done(nc.vector.tensor_tensor(h_sq[:, 0:w], st[:, 0:w, 2], st[:, 0:w, 5], ALU.add))
                stp.wait()
                stp.done(nc.vector.tensor_scalar(mv[:, 0:w, 0], h_sum[:, 0:w], 0.5, None, ALU.mult))
                stp.step(nc.vector.scalar_tensor_tensor(h_dif[:, 0:w], h_dif[:, 0:w], 0.25, h_dif[:, 0:w], ALU.mult, ALU.mult))
                stp.step(nc.vector.scalar_tensor_tensor(mv[:, 0:w, 1], h_sq[:, 0:w], 1.0 / D, h_dif[:, 0:w], ALU.mult, ALU.add))
                stp.step(nc.vector.tensor_scalar(nv[:, 0:w], mv[:, 0:w, 1], EPS, None, ALU.add))
                norm_scale(stp, w)

            def stats_steps(rows):
                return rows + 7 + NORM_STEPS

            def equal(tr, bank, field, out4, done):
                for k in range(J):
                    last = nc.vector.tensor_scalar(out4[:, k, :], bank, m[:, tr.s, k, field:field + 1], None, ALU.is_equal)
                last.then_inc(done, 1)

            def meta_slot(tr, q):
                nc.vector.tensor_scalar(m[:, tr.s, :, :], meta[:, bass.ds(tr.t * J, J), :], 0.0, None,
                                        ALU.add).then_inc(q["meta"][tr.s], 1)
                tr.now(dve, q["meta"])

            def edges_0(st):
                tr = st.tile(1)
                if tr:
                    tr.again(dve, q0["dst_eq"])
                    tr.again(dve, q0["src_eq"])
                    meta_slot(tr, q0)
                tr = st.tile(0)
                if tr:
                    tr.now(dve, q0["dst_bc"])
                    tr.again(dve, q0["earlier"])
                    for k in range(J):
                        last = nc.vector.tensor_scalar(eq0(1, tr.s, k), slot_bank(yA, tr.s), m[:, tr.s, k, DST:DST + 1], None, ALU.is_equal)
                    last.then_inc(q0["dst_eq"][tr.s], 1)
                tr = st.tile(-1)
                if tr:
                    stp = Steps(dve, c1s, tr, 2)
                    tr.now(dve, q0["earlier"])
                    tr.before(dve, q0["rows"])
                    stp.step(nc.vector.tensor_tensor(dd[:], dummy[:], meta[:, bass.ds(tr.t * J, J), 0:2], ALU.subtract))
                    stp.step(nc.vector.scalar_tensor_tensor(nf[:], bk[0][:, 0:2 * J].rearrange("p (j v) -> p j v", v=2),
                                                            1.0, dd[:], ALU.min, ALU.mult))
                    stp.close()
                    nc.vector.tensor_tensor(uniq[:, bass.ds(tr.t * J, J), :], nf[:], meta[:, bass.ds(tr.t * J, J), 0:2], ALU.add).then_inc(q0["rows"][tr.s], 1)
                tr = st.tile(0)
                if tr:
                    tr.now(dve, q0["dst_eq"])
                    tr.now(dve, q0["src_eq"])
                    for v in (1, 0):
                        for j in range(J):
                            last = nc.vector.tensor_tensor(low0(v, tr.s, j), eq0(v, tr.s, j)[:, j * P:(j + 1) * P], lowerb[:], ALU.mult)
                    last.then_inc(q0["low"][tr.s], 1)

            nc.vector.tensor_copy(lowerb[:], lower[:])
            nc.vector.tensor_copy(onesb[:], ones[:]).then_inc(s_bf, 1)
            dve.wait_ge(s_bf, 1)
            edge_steps(dve, edges_0)

            dve.wait_ge(s_w, 16 * WEIGHTS)
            parts = ((wcat, wch, wcl), (w1x, w1h, w1l), (w3x, w3xh, w3xl))
            for k, (whole, high, low) in enumerate(parts):
                nc.vector.tensor_copy(high[:], whole[:]).then_inc(s_split, 1)
            for k, (whole, high, low) in enumerate(parts):
                dve.wait_ge(s_split, len(parts))
                nc.vector.tensor_tensor(low[:], whole[:], high[:], ALU.subtract).then_inc(s_split, 1)
            for k in range(1, J):
                nc.vector.tensor_copy(b4b[:, k, :], b4b[:, 0, :])
            for k in range(1, 16):
                last = nc.vector.tensor_copy(row1[:, k, :], row1[:, 0, :])
            last.then_inc(s_dup, 1)

            def weighted(tr, j):
                y = yAB[j % 2]
                tr.part(dve, q1["y"], J, j + 1)
                if j < 2:
                    tr.before_part(dve, q1["msg"], J, J - 1 + j)
                else:
                    tr.part(dve, q1["msg"], J, j - 1)
                nc.vector.tensor_tensor(prod[:, j % 2, 0:4, :], y[:, 0:T].rearrange("p (b f) -> p b f", b=4),
                                        cf[:, tr.s, j, 0:4].rearrange("p (b o) -> p b o", o=1).to_broadcast([P, 4, D]),
                                        ALU.mult).then_inc(q1["y_read"][tr.s], 1)

            def message(tr, j):
                tr.part(dve, q1["y_read"], J, j + 1)
                tr.part(dve, q1["y_read_scalar"], J, j + 1)
                nc.vector.tensor_reduce(fc[:, tr.s, j, :], prod[:, j % 2, :, :].rearrange("p b f -> p f b"), AX.X, ALU.add).then_inc(q1["msg"][tr.s], 1)

            def edges_1(st):
                tr, nxt = st.tile(0), st.tile(1)
                if nxt:
                    nxt.again(dve, q1["dst_eq"])
                    nxt.again(dve, q1["coef"])
                    nxt.again(dve, q1["dst_bc"])
                    meta_slot(nxt, q1)
                if tr:
                    tr.again(dve, q1["sum"])
                    weighted(tr, 0)
                    weighted(tr, 1)
                    message(tr, 0)
                    message(tr, 1)
                if nxt:
                    nxt.now(dve, q1["types_bc"])
                    nxt.before(dve, q1["coef_ps"])
                    nc.vector.tensor_scalar(ot[:], bk[0][0:R, :], part[0:R, :], None, ALU.is_equal).then_inc(q1["type_hot"][nxt.s], 1)
                if tr:
                    weighted(tr, 2)
                if nxt:
                    nxt.now(dve, q1["xT"])
                    nxt.again(dve, q1["y"], J)
                    nc.vector.tensor_tensor(xl[:, nxt.s, :], bk[1][:], xh[:, nxt.s, :], ALU.subtract).then_inc(q1["xT_low"][nxt.s], 1)
                    nxt.now(dve, q1["coef_ps"])
                    nc.vector.tensor_tensor(cf[:, nxt.s, :, :], bk[0][:, 0:J * NB].rearrange("p (j b) -> p j b", b=NB),
                                            m[:, nxt.s, :, NORM:NORM + 1].to_broadcast([P, J, NB]), ALU.mult).then_inc(q1["coef"][nxt.s], 1)
                    nxt.now(dve, q1["coef"])
                if tr:
                    weighted(tr, 3)
                    message(tr, 2)
                    message(tr, 3)

            edge_steps(dve, edges_1)

            S2 = stats_steps(J) + 2

            def edges_2(st):
                tr, nxt = st.tile(0), st.tile(1)
                if tr:
                    tr.now(dve, q2["dst_bc"])
                    tr.again(dve, q2["sum"])
                    equal(tr, bk[1][:], DST, big0[:, tr.s, :, :], q2["dst_eq"][tr.s])
                if nxt:
                    nxt.again(dve, q2["dst_eq"])
                    nxt.again(dve, q2["src_eq"])
                    nxt.again(dve, q2["y"])
                    meta_slot(nxt, q2)
                if tr:
                    s = tr.s
                    stp = Steps(dve, c2s, tr, S2)
                    tr.now(dve, q2["x_in"], 16)
                    tr.now(dve, q2["agg_in"], 64)
                    tr.again(dve, q2["y"])
                    nc.vector.scalar_tensor_tensor(fe[:, s, :, :], fb[:, s, :, :], 0.0, fa[:, s, :, :], ALU.max, ALU.add).then_inc(q2["v"][s], 1)
                    tr.now(dve, q2["v"])
                    stats(stp, [fe[:, s, j, :] for j in range(J)])
                    stp.step(nc.vector.tensor_tensor(rc[:], ny[:, 0:J], m[:, s, :, EW], ALU.mult))
                    stp.step(nc.vector.tensor_tensor(na[:, 0:J], mv[:, 0:J, 0], rc[:], ALU.mult))
                    stp.close()
                    tr.again(dve, q2["yT_ps"])
                    for j in range(J):
                        last = nc.vector.tensor_scalar(fc[:, s, j, :], fe[:, s, j, :], rc[:, j:j + 1], na[:, j:j + 1], ALU.mult, ALU.subtract)
                    last.then_inc(q2["y"][s], 1)

            pipeline(dve, edges_2, G, 1, 0)

            def stat(v, place):
                for j in range(J):
                    last = nc.vector.bn_stats(place[:, j, :], v[:, j, :])
                return last

            def node_vector(st):
                idx = st.turn(3)
                made = None
                if st.tile(3) or st.tile(2) or st.tile(-3):
                    idx.again(dve, qn["scales"])
                tr = st.tile(-3)
                if tr:
                    tr.now(dve, qn["y_ps"])
                    tr.now(dve, qn["x2b"])
                    tr.again(dve, qn["x4"])
                    nc.vector.tensor_tensor(t3[:, tr.s, :, :], bk[3][:].rearrange("p (j f) -> p j f", j=J), fd[:, tr.s, :, :],
                                            ALU.add).then_inc(qn["t3"][tr.s], 1)
                    tr.now(dve, qn["t3"])
                    made = stat(t3[:, tr.s], stq[:, idx.s, 2])
                tr = st.tile(3)
                if tr:
                    tr.now(dve, qn["in"], 32)
                    tr.again(dve, qn["v1"])
                    nc.vector.scalar_tensor_tensor(va[:, tr.s, :, :], fb[:, tr.s, :, :], 0.0, fa[:, tr.s, :, :], ALU.max, ALU.add).then_inc(qn["v0"][tr.s], 1)
                    tr.now(dve, qn["v0"])
                    made = stat(va[:, tr.s], stq[:, idx.s, 0])
                tr = st.tile(-1)
                if tr:
                    tr.now(dve, qn["attn"])
                    tr.again(dve, qn["h3_ps"], 2)
                    for k in range(2):
                        last = nc.vector.tensor_tensor(rr[:, tr.s, 2 + k, :], rr[:, tr.s, k, :], att_b[:, tr.s, :], ALU.mult)
                    last.then_inc(qn["scaled"][tr.s], 1)
                before = st.turn(2)
                tr = st.tile(2)
                if tr:
                    tr.now(dve, qn["agg1_in"], 16)
                    before.now(dve, qn["scales"])
                    tr.again(dve, qn["x2"])
                    for j in range(J):
                        last = nc.vector.scalar_tensor_tensor(vb[:, tr.s, j, :], va[:, tr.s, j, :], nry[:, before.s, 0, j:j + 1],
                                                              fc[:, tr.s, j, :], ALU.mult, ALU.add)
                    last.then_inc(qn["v1"][tr.s], 1)
                    tr.now(dve, qn["v1"])
                    made = stat(vb[:, tr.s], stq[:, idx.s, 1])
                if made is not None:
                    made.then_inc(qn["stats"][idx.s], 1)
                tr = st.tile(1)
                if tr:
                    before.now(dve, qn["scales"])
                    tr.again(dve, qn["x2T_ps"])
                    tr.again(dve, qn["x2b"])
                    for j in range(J):
                        last = nc.vector.tensor_scalar(x2s[:, tr.s, j, :], vb[:, tr.s, j, :], nmean[:, before.s, 1, j:j + 1],
                                                       nry[:, before.s, 1, j:j + 1], ALU.subtract, ALU.mult)
                    last.then_inc(qn["x2"][tr.s], 1)
                    tr.now(dve, qn["attr_in"], 16)
                    stp = Steps(dve, cna, tr, 2)
                    stp.step(nc.vector.tensor_scalar(rc[:], at[:, tr.s, :, A], 1.0, None, ALU.max))
                    stp.step(nc.vector.reciprocal(rc[:], rc[:]))
                    tr.again(dve, qn["agT_ps"])
                    nc.vector.tensor_tensor(ag[:, tr.s, :, 0:A], at[:, tr.s, :, 0:A], rc[:].rearrange("p (j o) -> p j o", o=1).to_broadcast([P, J, A]),
                                            ALU.mult).then_inc(qn["attr_mean"][tr.s], 1)
                    tr.now(dve, qn["attr_mean"])
                tr = st.tile(0)
                if tr:
                    tr.now(dve, qn["h1"])
                    tr.now(dve, qn["zpart"])
                    tr.before(dve, qn["z_ps"])
                    nc.vector.scalar_tensor_tensor(zsum[:], rr[:, tr.s, 1, :], w2a[:, 1:2], zpart[:], ALU.mult, ALU.add).then_inc(qn["zsum"][tr.s], 1)
                tr = st.tile(-1)
                if tr:
                    tr.before(dve, qn["h3"])
                    for k in range(2):
                        tr.part(dve, qn["h3_ps"], 2, k + 1)
                        nc.vector.scalar_tensor_tensor(h3_pre[:, k, :], att_b[:, tr.s, :], c23[:, k:k + 1], yB[:, k * T:(k + 1) * T],
                                                       ALU.mult, ALU.add).then_inc(qn["h3_pre"][tr.s], 1)
                tr = st.tile(1)
                if tr:
                    tr.now(dve, qn["x2T"])
                    tr.again(dve, qn["h3_ps"], 2)
                    nc.vector.tensor_tensor(xl[:, tr.s, :], bk[0][:], xh[:, tr.s, :], ALU.subtract).then_inc(qn["x2T_low"][tr.s], 1)

            dve.wait_ge(s_wpk, 1)
            nc.vector.memset(stq[:], 1.0).then_inc(s_stq, 1)
            dve.wait_ge(s_stq, 1)
            node_steps(dve, node_vector)

            qn["y_ps"].all(dve)

            def attention(st):
                tr = st.tile(0)
                if tr:
                    tr.again(dve, q3["hot"], J)
                    tr.again(dve, q3["hot_p"])
                    meta_slot(tr, q3)
                    tr.now(dve, q3["hs_in"], 64)
                    tr.now(dve, q3["hd_in"], 64)
                    tr.again(dve, q3["dT_ps"])
                    nc.vector.tensor_tensor(fc[:, tr.s, :, :], fa[:, tr.s, :, :], fb[:, tr.s, :, :], ALU.subtract).then_inc(q3["dif"][tr.s], 1)
                tr = st.tile(-1)
                if tr:
                    for j in range(J):
                        tr.before_part(dve, q3["used"], J, j + 1)
                        nc.vector.tensor_scalar(hot_q(j), numbers[:], m[:, tr.s, j, SRC_Q:SRC_Q + 1], None, ALU.is_equal).then_inc(q3["hot"][tr.s], 1)
                    tr.now(dve, q3["att"])
                    tr.again(dve, q3["used"], J)
                    for j in range(J):
                        last = nc.vector.tensor_scalar(sl[:, tr.s, j, :], numbers[:, 0:P], m[:, tr.s, j, SRC_P:SRC_P + 1],
                                                       sm[:, tr.s, j:j + 1], ALU.is_equal, ALU.mult)
                    last.then_inc(q3["hot_p"][tr.s], 1)
                    nc.vector.tensor_scalar(att_all[:, bass.ds(tr.t * J, J)], sm[:, tr.s, :], 0.0, None, ALU.add).then_inc(q3["att_saved"][tr.s], 1)

            edge_steps(dve, attention)

            q3["att_saved"].all(dve)
            q3["hot"].all(dve, J)
            q3["used"].all(dve, J)

            def weight_messages(st):
                tr = st.tile(0)
                for a in range(2):
                    grp = tr.group(a)
                    grp.again(dve, q4["dst_eq"])
                    meta_slot(grp, q4)

                def ends(a):
                    grp = tr.group(a)
                    grp.now(dve, q4["dst_bc"])
                    grp.again(dve, q4["sum"])
                    equal(grp, bk[1][:], DST, big0[:, a, :, :], q4["dst_eq"][a])

                def messages(a):
                    grp = tr.group(a)
                    grp.now(dve, q4["h_in"], 16)
                    nc.vector.tensor_tensor(fc[:, a, :, :], fa[:, a, :, :],
                                            att_n[:, tr.s, a * J:(a + 1) * J].rearrange("p (j o) -> p j o", o=1).to_broadcast([P, J, D]),
                                            ALU.mult).then_inc(q4["msg"][a], 1)

                ends(0)
                tr.now(dve, q4_pair["den_in"], 128)
                stp = Steps(dve, c4s, tr, 1)
                for a in range(2):
                    tr.group(a).again(dve, q4["msg"])
                stp.step(nc.vector.reciprocal(att_n[:, tr.s, :], den_e[:, tr.s, :]))
                stp.close()
                nc.vector.tensor_tensor(att_n[:, tr.s, :], att_n[:, tr.s, :], att_all[:, bass.ds(tr.t * 2 * J, 2 * J)], ALU.mult).then_inc(q4_pair["weight"][tr.s], 1)
                tr.now(dve, q4_pair["weight"])
                messages(0)
                ends(1)
                messages(1)

            pair_steps(dve, weight_messages)

            q4["sum"].all(dve)
            q4["added"].all(dve, 64)

            def norm_rows(st):
                tr = st.tile(0)
                stp = Steps(dve, c5s, tr, stats_steps(2 * J))
                tr.now(dve, q5_pair["x_in"], 128)
                rows = [tile[:, tr.s, j, :] for tile in (fa, fb) for j in range(J)]
                tr.again(dve, q5_pair["y"])
                stats(stp, rows)
                stp.close()
                for a in range(2):
                    tr.group(a).long_ago(dve, q5["out"], 64)
                for j, row in enumerate(rows):
                    last = nc.vector.tensor_scalar((fd, fc)[j // J][:, tr.s, j % J, :], row, mv[:, j, 0:1], ny[:, j:j + 1], ALU.subtract, ALU.mult)
                last.then_inc(q5_pair["y"][tr.s], 1)

            pair_steps(dve, norm_rows)

        @block.scalar
        def _(act):
            act.wait_ge(s_w, 16 * WEIGHTS)
            nc.scalar.activation(wab[:, 0, :], zeros[:, 0:P], ACT.Identity, bias=wac[:, 0:1])
            nc.scalar.activation(wab[:, 1, :], zeros[:, 0:P], ACT.Identity, bias=wac[:, 1:2])
            nc.scalar.activation(b2b[:, 0, :], zeros[:, 0:P], ACT.Identity, bias=b2c[:, 0:1])
            nc.scalar.activation(b2b[:, 1, :], zeros[:, 0:P], ACT.Identity, bias=b2c[:, 1:2])
            act.wait_ge(s_wt, 1)
            nc.scalar.copy(w2T[:, 0, :], bk[0][:, 0:H])
            nc.scalar.copy(w2T[:, 1, :], bk[0][:, H:2 * H])
            nc.scalar.copy(l1wT[:], bk[1][:, 0:D]).then_inc(s_wte, 1)
            act.wait_ge(s_wp, 1)
            nc.scalar.copy(w23[:, 0, :], bk[2][:, 0:H])
            nc.scalar.copy(w23[:, 1, :], bk[2][:, H:2 * H])
            nc.scalar.copy(w2a[:, 0:1], bk[3][:, 0:1])
            nc.scalar.copy(w2a[:, 1:2], bk[3][:, P:P + 1])
            nc.scalar.copy(c23[:], bk[3][:, 2 * P:2 * P + 2])
            nc.scalar.activation(zb[:], bk[3][:, 2 * P + 2:2 * P + 3], ACT.Identity, bias=bab[:]).then_inc(s_wpk, 1)

            def distances(tr, bank, field, done):
                for k in range(J):
                    last = nc.scalar.activation(absd[:, k, :], bank, ACT.Abs, bias=m[:, tr.s, k, field:field + 1], scale=-1.0)
                last.then_inc(done[tr.s], 1)

            def where_equal(tr, out, done, count, equal_done):
                act.wait_ge(done[tr.s], tr.i + (count + 1))
                for k in range(J):
                    last = nc.scalar.activation(out(k), absd[:, k, :], ACT.Relu, bias=1.0, scale=-1.0)
                last.then_inc(equal_done[tr.s], 1)
                tr.now(act, equal_done)

            def edges_0(st):
                tr = st.tile(0)
                if tr:
                    tr.now(act, q0["src_bc"])
                    tr.again(act, q0["earlier"])
                    distances(tr, slot_bank(yB, tr.s), SRC, s_abs)
                    where_equal(tr, lambda k: eq0(0, tr.s, k), s_abs, 0, q0["src_eq"])
                    if st.i is None and tr.t == FILL_TURNS:
                        fill_rest(act, agg0, row0_flat, D, s_fill0)
                    else:
                        fill_turn(act, agg0, row0_flat, D, tr.t, s_fill0)

            act.wait_ge(s_row, 16 * 16)
            edge_steps(act, edges_0)

            def products(tr, j):
                tr.part(act, q1["y"], J, j + 1)
                if j < 2:
                    tr.before_part(act, q1["msg"], J, J - 1 + j)
                else:
                    tr.part(act, q1["msg"], J, j - 1)
                for b in range(4, NB):
                    last = nc.scalar.activation(prod[:, j % 2, b, :], yAB[j % 2][:, b * D:(b + 1) * D], ACT.Copy, scale=cf[:, tr.s, j, b:b + 1])
                last.then_inc(q1["y_read_scalar"][tr.s], 1)

            def edges_1(st):
                tr, nxt, prev = st.tile(0), st.tile(1), st.tile(-1)
                if tr:
                    tr.now(act, q1["coef"])
                    products(tr, 0)
                    products(tr, 1)
                    tr.now(act, q1["dst_bc"])
                    distances(tr, bk[3][:], DST, s_abs)
                if prev:
                    prev.now(act, q1["sum"])
                    prev.again(act, q1["added"], 64)
                    nc.scalar.copy(flat(fd, prev.s), bk[2][:]).then_inc(q1["sum_kept"][prev.s], 1)
                if nxt:
                    nxt.now(act, q1["xT_ps"])
                    nxt.again(act, q1["y"], J)
                    nc.scalar.copy(xh[:, nxt.s, :], bk[1][:]).then_inc(q1["xT"][nxt.s], 1)
                if tr:
                    tr.again(act, q1["sum"])
                    where_equal(tr, lambda k: big0[:, tr.s, k, :], s_abs, G // 2, q1["dst_eq"])
                    products(tr, 2)
                    products(tr, 3)

            edge_steps(act, edges_1)

            q1["added"].all(act, 64)

            def edges_2(st):
                tr, nxt, prev = st.tile(0), st.tile(1), st.tile(-1)
                if tr:
                    tr.now(act, q2["attr_sum"])
                    tr.again(act, q2["attr_added"], 64)
                    nc.scalar.copy(flat(ag, tr.s), yB[:, 0:J * AW]).then_inc(q2["attr_kept"][tr.s], 1)
                if nxt:
                    nxt.now(act, q2["src_bc"])
                    nxt.before(act, q2["attr_sum"])
                    distances(nxt, bk[2][:], SRC, s_abs)
                    where_equal(nxt, lambda k: big1[:, k, :], s_abs, G, q2["src_eq"])
                if prev:
                    prev.now(act, q2["sum"])
                    prev.again(act, q2["added"], 64)
                    nc.scalar.copy(flat(fd, prev.s), yA[:, 0:T]).then_inc(q2["sum_kept"][prev.s], 1)
                if tr:
                    tr.now(act, q2["yT_ps"])
                    tr.again(act, q2["z_ps"])
                    nc.scalar.copy(x2T[:, tr.s, :], bk[0][:]).then_inc(q2["yT"][tr.s], 1)
                    tr.now(act, q2["z_ps"])
                    tr.again(act, q2["sum"])
                    nc.scalar.copy(flat(ff, tr.s), bk[3][:]).then_inc(q2["z"][tr.s], 1)

            edge_steps(act, edges_2)

            q2["sum"].all(act)

            def node_scalar(st):
                before = st.turn(2)
                tr = st.tile(0)
                if tr:
                    tr.now(act, qn["h1_ps"])
                    tr.again(act, qn["scaled"])
                    for k in range(2):
                        last = nc.scalar.activation(rr[:, tr.s, k, :], yA[:, k * T:(k + 1) * T], ACT.Relu, bias=b1c[:, k:k + 1])
                    last.then_inc(qn["h1"][tr.s], 1)
                    tr.now(act, qn["h1"])
                    tr.before(act, qn["zsum"])
                    nc.scalar.activation(zpart[:], rr[:, tr.s, 0, :], ACT.Copy, scale=w2a[:, 0:1]).then_inc(qn["zpart"][tr.s], 1)
                tr = st.tile(-4)
                if tr:
                    before.now(act, qn["scales"])
                    for v, (tile, key) in enumerate(((fe, "x3"), (ff, "x4"))):
                        tr.again(act, qn[key + "_out"], 16)
                        for j in range(J):
                            last = nc.scalar.activation(tile[:, tr.s, j, :], t3[:, tr.s, j, :], ACT.Identity,
                                                        bias=nbias[:, before.s, v, j:j + 1], scale=nry[:, before.s, 2 + v, j:j + 1])
                        last.then_inc(qn[key][tr.s], 1)
                tr = st.tile(1)
                if tr:
                    tr.now(act, qn["x2T_ps"])
                    tr.again(act, qn["h3_ps"], 2)
                    nc.scalar.copy(xh[:, tr.s, :], bk[0][:]).then_inc(qn["x2T"][tr.s], 1)
                    tr.now(act, qn["agT_ps"])
                    tr.again(act, qn["h1_ps"])
                    nc.scalar.copy(agT[:, tr.s, :], bk[1][0:A, :]).then_inc(qn["agT"][tr.s], 1)
                tr = st.tile(0)
                if tr:
                    tr.now(act, qn["z_ps"])
                    tr.again(act, qn["h3_pre"], 2)
                    nc.scalar.activation(att_b[:, tr.s, :], bk[2][:], ACT.Sigmoid, bias=zb[:]).then_inc(qn["attn"][tr.s], 1)
                tr = st.tile(-1)
                if tr:
                    tr.again(act, qn["y_ps"])
                    for k in range(2):
                        tr.part(act, qn["h3_pre"], 2, k + 1)
                        last = nc.scalar.activation(h3[:, tr.s, k, :], h3_pre[:, k, :], ACT.Relu, bias=b3c[:, k:k + 1])
                    last.then_inc(qn["h3"][tr.s], 1)

            node_steps(act, node_scalar)

            with act.Fori(0, G // 2) as i:
                for s in range(2):
                    tr = Turn(i, s)
                    tr.now(act, q3["dT_ps"])
                    tr.again(act, q3["hid_ps"])
                    nc.scalar.copy(x2T[:, s, :], bk[0][:]).then_inc(q3["dT"][s], 1)
                    tr.now(act, q3["hid_ps"])
                    tr.again(act, q3["att_ps"])
                    nc.scalar.activation(att_b[:, s, :], bk[2][:], ACT.Relu, bias=c1c[:]).then_inc(q3["hid"][s], 1)
                    tr.now(act, q3["att_ps"])
                    tr.again(act, q3["att"])
                    nc.scalar.activation(rc2[:, s, :], bk[3][:, 0:J], ACT.Relu, bias=c2c[:]).then_inc(q3["att_relu"][s], 1)
                    tr.now(act, q3["att_relu"])
                    tr.again(act, q3["att_saved"])
                    nc.scalar.activation(sm[:, s, :], rc2[:, s, :], ACT.Sigmoid).then_inc(q3["att"][s], 1)
            act.wait_ge(s_den_ps, 1)
            nc.scalar.copy(flat_den, yA[:, 0:DQ]).then_inc(s_den, 1)
            with act.Fori(0, G // 2) as i:
                for s in range(2):
                    tr = Turn(i, s)
                    tr.now(act, q4["sum"])
                    tr.again(act, q4["added"], 64)
                    nc.scalar.copy(fd[:, s, :, :].rearrange("p j f -> p (j f)"), bk[2][:]).then_inc(q4["sum_kept"][s], 1)



        @block.tensor
        def _(pe):
            def mm(o, l, r, k, n):
                return nc.tensor.matmul(o, l, r, start=(k == 0), stop=(k == n - 1))

            pe.wait_ge(s_const, 5)
            pe.wait_ge(s_w, 16 * WEIGHTS)
            for k in range(2):
                for h in range(2):
                    nc.tensor.transpose(bk[0][:, h * H + k * P:h * H + (k + 1) * P], w2n[:, k, h * P:(h + 1) * P], ident[:])
            nc.tensor.transpose(bk[1][:, 0:D], l1w[:], ident[:]).then_inc(s_wt, 1)
            pe.wait_ge(s_wte, 1)
            for h_out in range(2):
                for k in range(2):
                    mm(bk[2][:, h_out * H:(h_out + 1) * H], w2T[:, k, h_out * P:(h_out + 1) * P], w3h[:, k, :], k, 2)
            for h_out in range(2):
                for k in range(2):
                    mm(bk[3][:, h_out * P:(h_out + 1) * P], w2T[:, k, h_out * P:(h_out + 1) * P], wab[:, k, :], k, 2)
            for h in range(2):
                for k in range(2):
                    mm(bk[3][:, 2 * P + h:2 * P + h + 1], w3h[:, k, h * P:(h + 1) * P], b2c[:, k:k + 1], k, 2)
            for k in range(2):
                last = mm(bk[3][:, 2 * P + 2:2 * P + 3], b2b[:, k, :], wac[:, k:k + 1], k, 2)
            last.then_inc(s_wp, 1)
            pe.wait_ge(s_wpk, 1)

            def spread(tr, bank, field, done):
                for j in range(J):
                    last = nc.tensor.transpose(cols(bank, j), m[:, tr.s, j, field:field + 1].to_broadcast([P, P]), ident[:])
                last.then_inc(done, 1)

            def turned(bank, tile, s, done, w=D):
                for j in range(J):
                    last = nc.tensor.transpose(bank[0:w, j * P:(j + 1) * P], tile[:, s, j, 0:w], ident[:])
                last.then_inc(done, 1)

            def totals(eq, rows, place, done):
                for j in range(J):
                    for k in range(J):
                        last = mm(place(j), eq[:, k, j * P:(j + 1) * P], rows(k), k, J)
                last.then_inc(done, 1)

            def edges_0(st):
                tr = st.tile(1)
                if tr:
                    tr.now(pe, q0["meta"])
                    tr.again(pe, q0["dst_eq"])
                    spread(tr, slot_bank(yA, tr.s), DST, q0["dst_bc"][tr.s])
                    tr.again(pe, q0["src_eq"])
                    spread(tr, slot_bank(yB, tr.s), SRC, q0["src_bc"][tr.s])
                tr = st.tile(-1)
                if tr:
                    tr.now(pe, q0["low"])
                    tr.before(pe, q0["rows"])
                    for j in range(J):
                        for v in range(2):
                            place = 2 * j + v
                            for k in range(j):
                                mm(bk[0][:, place:place + 1], eq0(v, tr.s, k)[:, j * P:(j + 1) * P], onesb[:], k, j + 1)
                            last = mm(bk[0][:, place:place + 1], low0(v, tr.s, j), onesb[:], j, j + 1)
                    last.then_inc(q0["earlier"][tr.s], 1)

            pe.wait_ge(s_bf, 1)
            edge_steps(pe, edges_0)

            pe.wait_ge(s_split, 6)
            q0["rows"].all(pe)
            q0["src_eq"].all(pe)

            def product(tr, j):
                for key in ("y_read", "y_read_scalar"):
                    if j < 2:
                        tr.before_part(pe, q1[key], J, J - 1 + j)
                    else:
                        tr.part(pe, q1[key], J, j - 1)
                chunk = slice(j * P, (j + 1) * P)
                for h in range(2):
                    for k, (x_part, w_part) in enumerate(((xh, wch), (xh, wcl), (xl, wch))):
                        last = mm(yAB[j % 2][:, h * T:(h + 1) * T], x_part[:, tr.s, chunk],
                                  w_part[:, h * 4:(h + 1) * 4, :].rearrange("p b f -> p (b f)"), k, 3)
                last.then_inc(q1["y"][tr.s], 1)

            def edges_1(st):
                tr, nxt, prev = st.tile(0), st.tile(1), st.tile(-1)
                if tr:
                    tr.now(pe, q1["xT"])
                    tr.now(pe, q1["xT_low"])
                    product(tr, 0)
                    product(tr, 1)
                if prev:
                    prev.now(pe, q1["msg"], J)
                    prev.now(pe, q1["dst_eq"])
                    prev.before(pe, q1["sum_kept"])
                    totals(big0[:, prev.s, :, :], lambda k: fc[:, prev.s, k, :], lambda j: cols(bk[2], j), q1["sum"][prev.s])
                if nxt:
                    nxt.now(pe, q1["x_in"], 16)
                    nxt.before(pe, q1["xT"])
                    nxt.before(pe, q1["xT_low"])
                    turned(bk[1], fa, nxt.s, q1["xT_ps"][nxt.s])
                    nxt.now(pe, q1["meta"])
                    nxt.before(pe, q1["coef"])
                    spread(nxt, bk[0], ETYPE, q1["types_bc"][nxt.s])
                if tr:
                    product(tr, 2)
                if nxt:
                    nxt.now(pe, q1["type_hot"])
                    for j in range(J):
                        last = nc.tensor.matmul(bk[0][:, j * NB:(j + 1) * NB], ot[:, j * P:(j + 1) * P], comp[:], start=True, stop=True)
                    last.then_inc(q1["coef_ps"][nxt.s], 1)
                    nxt.before(pe, q1["dst_eq"])
                    spread(nxt, bk[3], DST, q1["dst_bc"][nxt.s])
                if tr:
                    product(tr, 3)

            edge_steps(pe, edges_1)

            q1["sum_kept"].all(pe)
            q1["y_read"].all(pe, J)
            q1["y_read_scalar"].all(pe, J)
            q1["dst_eq"].all(pe)

            def edges_2(st):
                tr, nxt, prev = st.tile(0), st.tile(1), st.tile(-1)
                if tr:
                    tr.now(pe, q2["src_eq"])
                    tr.now(pe, q2["attr_in"], 16)
                    tr.before(pe, q2["attr_kept"])
                    totals(big1[:, :, :], lambda k: at[:, tr.s, k, :], lambda j: yB[:, j * AW:(j + 1) * AW], q2["attr_sum"][tr.s])
                if nxt:
                    nxt.now(pe, q2["meta"])
                    nxt.before(pe, q2["src_eq"])
                    spread(nxt, bk[2], SRC, q2["src_bc"][nxt.s])
                    nxt.before(pe, q2["dst_eq"])
                    spread(nxt, bk[1], DST, q2["dst_bc"][nxt.s])
                if prev:
                    prev.now(pe, q2["dst_eq"])
                    prev.now(pe, q2["z"])
                    prev.before(pe, q2["sum_kept"])
                    totals(big0[:, prev.s, :, :], lambda k: ff[:, prev.s, k, :], lambda j: cols(yA, j), q2["sum"][prev.s])
                if tr:
                    tr.now(pe, q2["y"])
                    tr.before(pe, q2["yT"])
                    turned(bk[0], fc, tr.s, q2["yT_ps"][tr.s])
                    tr.now(pe, q2["yT"])
                    tr.before(pe, q2["z"])
                    for j in range(J):
                        last = nc.tensor.matmul(cols(bk[3], j), x2T[:, tr.s, j * P:(j + 1) * P], l1wT[:], start=True, stop=True)
                    last.then_inc(q2["z_ps"][tr.s], 1)

            edge_steps(pe, edges_2)

            q2["dst_eq"].all(pe)
            q2["sum_kept"].all(pe)
            q2["attr_kept"].all(pe)

            def node_tensor(st):
                tr = st.tile(0)
                if tr:
                    tr.now(pe, qn["x2T"])
                    tr.now(pe, qn["agT"])
                    tr.before(pe, qn["h1"])
                    for k in range(2):
                        o, half = yA[:, k * T:(k + 1) * T], slice(k * P, (k + 1) * P)
                        mm(o, w1a[:, half], agT[:, tr.s, :], 0, 4)
                        mm(o, w1h[:, half], xh[:, tr.s, :], 1, 4)
                        mm(o, w1l[:, half], xh[:, tr.s, :], 2, 4)
                        if k == 0:
                            tr.now(pe, qn["x2T_low"])
                        last = mm(o, w1h[:, half], xl[:, tr.s, :], 3, 4)
                    last.then_inc(qn["h1_ps"][tr.s], 1)
                tr = st.tile(-2)
                if tr:
                    tr.now(pe, qn["h3"])
                    tr.before(pe, qn["t3"])
                    for j in range(J):
                        for k in range(2):
                            last = mm(cols(bk[3], j), h3[:, tr.s, k, j * P:(j + 1) * P], w4s[:, k, :], k, 2)
                    last.then_inc(qn["y_ps"][tr.s], 1)
                tr = st.tile(-1)
                if tr:
                    tr.before(pe, qn["h3_pre"], 2)
                    tr.now(pe, qn["scaled"])
                    for k in range(2):
                        o, half = yB[:, k * T:(k + 1) * T], slice(k * P, (k + 1) * P)
                        mm(o, w3xh[:, half], xh[:, tr.s, :], 0, 5)
                        mm(o, w3xl[:, half], xh[:, tr.s, :], 1, 5)
                        mm(o, w3xh[:, half], xl[:, tr.s, :], 2, 5)
                        for h in range(2):
                            last = mm(o, w23[:, h, half], rr[:, tr.s, 2 + h, :], 3 + h, 5)
                        last.then_inc(qn["h3_ps"][tr.s], 1)
                tr = st.tile(1)
                if tr:
                    tr.now(pe, qn["x2"])
                    tr.before(pe, qn["x2T"])
                    tr.before(pe, qn["x2T_low"])
                    turned(bk[0], x2s, tr.s, qn["x2T_ps"][tr.s])
                    tr.now(pe, qn["attr_mean"])
                    tr.before(pe, qn["agT"])
                    turned(bk[1], ag, tr.s, qn["agT_ps"][tr.s], A)
                tr = st.tile(0)
                if tr:
                    tr.now(pe, qn["zsum"])
                    tr.before(pe, qn["attn"])
                    mm(bk[2][:], ones_b[:], zsum[:], 0, 1).then_inc(qn["z_ps"][tr.s], 1)

            node_steps(pe, node_tensor)

            qn["t3"].all(pe)
            qn["h1"].all(pe)

            def den_sums(l, r, start, stop):
                for a, b in ((0, T), (T, DQ)):
                    last = nc.tensor.matmul(yA[:, a:b], l, r[:, a:b], start=start, stop=stop)
                return last

            den_sums(zeros[:, 0:P], zeros[:, 0:DQ], True, False)

            def attention(st):
                tr, prev = st.tile(0), st.tile(-1)
                if tr:
                    tr.now(pe, q3["dif"])
                    tr.before(pe, q3["dT"])
                    turned(bk[0], fc, tr.s, q3["dT_ps"][tr.s])
                    tr.now(pe, q3["dT"])
                    tr.before(pe, q3["hid"])
                    nc.tensor.matmul(bk[2][:], v1s[:], x2T[:, tr.s, :], start=True, stop=True).then_inc(q3["hid_ps"][tr.s], 1)
                if prev:
                    prev.now(pe, q3["hot_p"])
                    for j in range(J):
                        prev.part(pe, q3["hot"], J, j + 1)
                        den_sums(sl[:, prev.s, j, :], hot_q(j), False, False).then_inc(q3["used"][prev.s], 1)
                if tr:
                    tr.now(pe, q3["hid"])
                    tr.before(pe, q3["att_relu"])
                    for j in range(J):
                        last = nc.tensor.matmul(bk[3][:, j:j + 1], att_b[:, tr.s, j * P:(j + 1) * P], v2s[:], start=True, stop=True)
                    last.then_inc(q3["att_ps"][tr.s], 1)

            edge_steps(pe, attention)
            den_sums(zeros[:, 0:P], zeros[:, 0:DQ], False, True).then_inc(s_den_ps, 1)

            q3["hid"].all(pe)

            def edges_4(st):
                nxt, tr = st.tile(1), st.tile(0)
                if nxt:
                    nxt.now(pe, q4["meta"])
                    nxt.before(pe, q4["dst_eq"])
                    spread(nxt, bk[1], DST, q4["dst_bc"][nxt.s])
                if tr:
                    tr.now(pe, q4["dst_eq"])
                    tr.now(pe, q4["msg"])
                    tr.before(pe, q4["sum_kept"])
                    totals(big0[:, tr.s, :, :], lambda k: fc[:, tr.s, k, :], lambda j: cols(bk[2], j), q4["sum"][tr.s])

            edge_steps(pe, edges_4)


_INS = ['x', 'src', 'dst', 'edge_attr_96', 'edge_type_32', 'edge_weight', 'edge_weight1', 'L0_gnn_weight',
        'L0_gnn_w_comp', 'L0_gnn_bias_param', 'L1_gnn_W', 'L1_gnn_b', 'L2_gnn_W1', 'L2_gnn_b1', 'L2_gnn_W2',
        'L2_gnn_b2', 'L2_gnn_Wa', 'L2_gnn_ba', 'L2_gnn_W3', 'L2_gnn_b3', 'L2_gnn_W4', 'L2_gnn_b4', 'L3_gnn_W1',
        'L3_gnn_b1', 'L3_gnn_W2', 'L3_gnn_b2']
_OUTS = [((N, D), 'float32')]


def kernel(**inputs):
    import numpy as _np
    import concourse.bacc as _bacc
    from concourse import mybir as _mybir
    from concourse.bass_utils import run_bass_kernel_spmd as _run

    nc = _bacc.Bacc("TRN2", target_bir_lowering=False, num_devices=1)
    arrays, args = {}, []
    for name in _INS:
        a = _np.ascontiguousarray(inputs[name])
        arrays[f"in_{name}_dram"] = a
        args.append(nc.dram_tensor(f"in_{name}_dram", a.shape, _mybir.dt.from_np(a.dtype), kind="ExternalInput").ap())
    for i, (shape, dtype) in enumerate(_OUTS):
        dt = _mybir.dt.from_np(_np.dtype(dtype))
        args.append(nc.dram_tensor(f"out_{i}_dram", shape, dt, kind="ExternalOutput").ap())
    gnn_kernel(nc, *args)
    r = _run(nc, [arrays], core_ids=[0])
    return r.results[0]["out_0_dram"]
```
